# Optimizing a Trainium2 kernel written in Bass

```python
import numpy as np
import jax
import jax.numpy as jnp

def _softmax(x, axis=-1):
    return jax.nn.softmax(x, axis=axis)

def _gelu(x):
    return jax.nn.gelu(x, approximate=True)

def _silu(x):
    return jax.nn.silu(x)

def _sigmoid(x):
    return jax.nn.sigmoid(x)

def _layernorm(x, axis=-1, eps=1e-05):
    m = jnp.mean(x, axis=axis, keepdims=True)
    v = jnp.var(x, axis=axis, keepdims=True)
    return (x - m) / jnp.sqrt(v + eps)

def _scatter_add(tgt, idx, src, axis=0):
    return tgt.at[idx].add(src)

def _segment_sum(src, seg, n):
    return jax.ops.segment_sum(src, seg, n)
kernel_name = 'mk_seq_postln_d1_jaxref_r8_4daf74'

def setup_inputs(seed: int=0):
    np.random.seed(seed)
    _w = jnp.asarray

    def _L0_attn_setup():
        import jax, jax.numpy as jnp
        import numpy as np
        H, DK, DV = (8, 64, 128)
        DECAY, THR, SBETA = (0.9, 0.5, 10.0)
        EPS = 1e-06

        def _rms(h, w):
            return h * jax.lax.rsqrt(jnp.mean(h * h, axis=-1, keepdims=True) + EPS) * w

        def _forward(x, w_norm_in, conv_w, conv_b, wq, wk, wv, w_out, w_spike, w_au, b_au, w_ad, b_ad, alpha_spike, w_beta, b_beta, beta_spike, w_hn, w_u1, b_u1, w_u2, b_u2, w_ffn, w_ff1, w_ff3, w_ff2):
            B, T, D = x.shape
            h = _rms(x, w_norm_in)
            CK = conv_w.shape[-1]
            hp = jnp.pad(h, ((0, 0), (CK - 1, 0), (0, 0)))
            conv = conv_b + sum((hp[:, j:j + T, :] * conv_w[:, j] for j in range(CK)))
            h = jax.nn.silu(conv)
            q = (h @ wq).reshape(B, T, H, DK)
            k = (h @ wk).reshape(B, T, H, DK)
            v = (h @ wv).reshape(B, T, H, DV)
            q = q / (jnp.linalg.norm(q, axis=-1, keepdims=True) + EPS)
            k = k / (jnp.linalg.norm(k, axis=-1, keepdims=True) + EPS)
            sd = (h @ w_spike).reshape(B, T, H, DK)
            ab = (jax.nn.silu(h @ w_au + b_au) @ w_ad + b_ad).reshape(B, T, H, DK)
            bb = h @ w_beta + b_beta

            def step(carry, inp):
                s, mem = carry
                qt, kt, vt, sdt, abt, bbt = inp
                mem = DECAY * mem + sdt
                sur = jax.nn.sigmoid(SBETA * (mem - THR))
                hard = (mem > THR).astype(x.dtype)
                spike = sur + jax.lax.stop_gradient(hard - sur)
                mem = mem - spike * THR
                alpha = jax.nn.sigmoid(abt + alpha_spike * spike)
                beta = jax.nn.sigmoid(bbt[..., None] + jnp.sum(spike * beta_spike, axis=-1, keepdims=True))
                active = jax.lax.stop_gradient((jnp.sum(hard, axis=-1, keepdims=True) > 0).astype(x.dtype))
                alpha = jnp.where(active > 0, alpha, jnp.ones_like(alpha))
                beta = beta * active
                s = s * alpha[..., None]
                u = jnp.einsum('bhd,bhdv->bhv', kt, s)
                s = s - beta[..., None] * jnp.einsum('bhd,bhv->bhdv', kt, u)
                s = s + beta[..., None] * jnp.einsum('bhd,bhv->bhdv', kt, vt)
                out = jnp.einsum('bhdv,bhd->bhv', s, qt)
                return ((s, mem), out)
            s0 = jnp.zeros((B, H, DK, DV), x.dtype)
            m0 = jnp.zeros((B, H, DK), x.dtype)
            tmaj = lambda a: jnp.moveaxis(a, 1, 0)
            (s, mem), outs = jax.lax.scan(step, (s0, m0), (tmaj(q), tmaj(k), tmaj(v), tmaj(sd), tmaj(ab), tmaj(bb)))
            y = jnp.moveaxis(outs, 0, 1)
            y = y * jax.lax.rsqrt(jnp.mean(y * y, axis=-1, keepdims=True) + EPS) * w_hn
            y = y.reshape(B, T, H * DV)
            gate = jax.nn.sigmoid(jax.nn.silu(x @ w_u1 + b_u1) @ w_u2 + b_u2)
            y = x + y @ w_out * gate
            h2 = _rms(y, w_ffn)
            y = y + jax.nn.silu(h2 @ w_ff1) * (h2 @ w_ff3) @ w_ff2
            return (y, s, mem)

        def _reference_tuple_inner(x, w_norm_in, conv_w, conv_b, wq, wk, wv, w_out, w_spike, w_au, b_au, w_ad, b_ad, alpha_spike, w_beta, b_beta, beta_spike, w_hn, w_u1, b_u1, w_u2, b_u2, w_ffn, w_ff1, w_ff3, w_ff2):
            return _forward(x, w_norm_in, conv_w, conv_b, wq, wk, wv, w_out, w_spike, w_au, b_au, w_ad, b_ad, alpha_spike, w_beta, b_beta, beta_spike, w_hn, w_u1, b_u1, w_u2, b_u2, w_ffn, w_ff1, w_ff3, w_ff2)
        key = jax.random.key(seed)
        B, T, D = (8, 256, 128)
        R, F, CK = (64, 512, 4)
        ks = jax.random.split(key, 16)
        n = lambda k, shp, s=0.02: jax.random.normal(k, shp, jnp.float32) * s
        return {'x': jax.random.normal(ks[0], (B, T, D), jnp.float32), 'w_norm_in': jnp.ones((D,), jnp.float32), 'conv_w': n(ks[1], (D, CK), 0.2), 'conv_b': jnp.zeros((D,), jnp.float32), 'wq': n(ks[2], (D, H * DK)), 'wk': n(ks[3], (D, H * DK)), 'wv': n(ks[4], (D, H * DV)), 'w_out': n(ks[5], (H * DV, D)), 'w_spike': n(ks[6], (D, H * DK), 0.1), 'w_au': n(ks[7], (D, R)), 'b_au': jnp.zeros((R,), jnp.float32), 'w_ad': n(ks[8], (R, H * DK)), 'b_ad': jnp.zeros((H * DK,), jnp.float32), 'alpha_spike': jnp.zeros((1, H, DK), jnp.float32), 'w_beta': n(ks[9], (D, H)), 'b_beta': jnp.zeros((H,), jnp.float32), 'beta_spike': jnp.zeros((1, H, DK), jnp.float32), 'w_hn': jnp.ones((H, DV), jnp.float32), 'w_u1': n(ks[10], (D, R)), 'b_u1': jnp.zeros((R,), jnp.float32), 'w_u2': n(ks[11], (R, D)), 'b_u2': jnp.zeros((D,), jnp.float32), 'w_ffn': jnp.ones((D,), jnp.float32), 'w_ff1': n(ks[12], (D, F)), 'w_ff3': n(ks[13], (D, F)), 'w_ff2': n(ks[14], (F, D))}
    _L0_attn_in = _L0_attn_setup()

    def _L0_ffn_setup():
        import jax, jax.numpy as jnp
        import numpy as np
        E, D, F = (8, 128, 512)
        LN_EPS = 1e-05
        key = jax.random.key(seed)
        k = jax.random.split(key, 8)
        x = jax.random.normal(k[0], (4, 256, D), jnp.float32)
        centroids = jax.random.normal(k[1], (E, D), jnp.float32) * 0.1
        ln_g = jnp.ones((E, D), jnp.float32)
        ln_b = jnp.zeros((E, D), jnp.float32)
        w1 = jax.random.normal(k[2], (E, F, D), jnp.float32) * (1.0 / np.sqrt(D))
        b1 = jnp.zeros((E, F), jnp.float32)
        w2 = jax.random.normal(k[3], (E, D, F), jnp.float32) * (1.0 / np.sqrt(F))
        b2 = jnp.zeros((E, D), jnp.float32)
        return {'input_features': x, 'centroids': centroids, 'ln_g': ln_g, 'ln_b': ln_b, 'w1': w1, 'b1': b1, 'w2': w2, 'b2': b2}
    _L0_ffn_in = _L0_ffn_setup()
    _d = {'L0_attn_x': _L0_attn_in['x'], 'L0_attn_w_norm_in': _L0_attn_in['w_norm_in'], 'L0_attn_conv_w': _L0_attn_in['conv_w'], 'L0_attn_conv_b': _L0_attn_in['conv_b'], 'L0_attn_wq': _L0_attn_in['wq'], 'L0_attn_wk': _L0_attn_in['wk'], 'L0_attn_wv': _L0_attn_in['wv'], 'L0_attn_w_out': _L0_attn_in['w_out'], 'L0_attn_w_spike': _L0_attn_in['w_spike'], 'L0_attn_w_au': _L0_attn_in['w_au'], 'L0_attn_b_au': _L0_attn_in['b_au'], 'L0_attn_w_ad': _L0_attn_in['w_ad'], 'L0_attn_b_ad': _L0_attn_in['b_ad'], 'L0_attn_alpha_spike': _L0_attn_in['alpha_spike'], 'L0_attn_w_beta': _L0_attn_in['w_beta'], 'L0_attn_b_beta': _L0_attn_in['b_beta'], 'L0_attn_beta_spike': _L0_attn_in['beta_spike'], 'L0_attn_w_hn': _L0_attn_in['w_hn'], 'L0_attn_w_u1': _L0_attn_in['w_u1'], 'L0_attn_b_u1': _L0_attn_in['b_u1'], 'L0_attn_w_u2': _L0_attn_in['w_u2'], 'L0_attn_b_u2': _L0_attn_in['b_u2'], 'L0_attn_w_ffn': _L0_attn_in['w_ffn'], 'L0_attn_w_ff1': _L0_attn_in['w_ff1'], 'L0_attn_w_ff3': _L0_attn_in['w_ff3'], 'L0_attn_w_ff2': _L0_attn_in['w_ff2'], 'L0_ffn_centroids': _L0_ffn_in['centroids'], 'L0_ffn_ln_g': _L0_ffn_in['ln_g'], 'L0_ffn_ln_b': _L0_ffn_in['ln_b'], 'L0_ffn_w1': _L0_ffn_in['w1'], 'L0_ffn_b1': _L0_ffn_in['b1'], 'L0_ffn_w2': _L0_ffn_in['w2'], 'L0_ffn_b2': _L0_ffn_in['b2']}
    _x0 = _d['L0_attn_x']
    _d['L0_attn_x'] = jax.random.normal(jax.random.fold_in(jax.random.key(seed), 1), (16, 256, 128), dtype=_x0.dtype)
    del _x0
    return _d

def reference(L0_attn_x, L0_attn_w_norm_in, L0_attn_conv_w, L0_attn_conv_b, L0_attn_wq, L0_attn_wk, L0_attn_wv, L0_attn_w_out, L0_attn_w_spike, L0_attn_w_au, L0_attn_b_au, L0_attn_w_ad, L0_attn_b_ad, L0_attn_alpha_spike, L0_attn_w_beta, L0_attn_b_beta, L0_attn_beta_spike, L0_attn_w_hn, L0_attn_w_u1, L0_attn_b_u1, L0_attn_w_u2, L0_attn_b_u2, L0_attn_w_ffn, L0_attn_w_ff1, L0_attn_w_ff3, L0_attn_w_ff2, L0_ffn_centroids, L0_ffn_ln_g, L0_ffn_ln_b, L0_ffn_w1, L0_ffn_b1, L0_ffn_w2, L0_ffn_b2):

    def _L0_attn_ref(x, w_norm_in, conv_w, conv_b, wq, wk, wv, w_out, w_spike, w_au, b_au, w_ad, b_ad, alpha_spike, w_beta, b_beta, beta_spike, w_hn, w_u1, b_u1, w_u2, b_u2, w_ffn, w_ff1, w_ff3, w_ff2):
        import jax, jax.numpy as jnp
        import numpy as np
        H, DK, DV = (8, 64, 128)
        DECAY, THR, SBETA = (0.9, 0.5, 10.0)
        EPS = 1e-06

        def _rms(h, w):
            return h * jax.lax.rsqrt(jnp.mean(h * h, axis=-1, keepdims=True) + EPS) * w

        def _forward(x, w_norm_in, conv_w, conv_b, wq, wk, wv, w_out, w_spike, w_au, b_au, w_ad, b_ad, alpha_spike, w_beta, b_beta, beta_spike, w_hn, w_u1, b_u1, w_u2, b_u2, w_ffn, w_ff1, w_ff3, w_ff2):
            B, T, D = x.shape
            h = _rms(x, w_norm_in)
            CK = conv_w.shape[-1]
            hp = jnp.pad(h, ((0, 0), (CK - 1, 0), (0, 0)))
            conv = conv_b + sum((hp[:, j:j + T, :] * conv_w[:, j] for j in range(CK)))
            h = jax.nn.silu(conv)
            q = (h @ wq).reshape(B, T, H, DK)
            k = (h @ wk).reshape(B, T, H, DK)
            v = (h @ wv).reshape(B, T, H, DV)
            q = q / (jnp.linalg.norm(q, axis=-1, keepdims=True) + EPS)
            k = k / (jnp.linalg.norm(k, axis=-1, keepdims=True) + EPS)
            sd = (h @ w_spike).reshape(B, T, H, DK)
            ab = (jax.nn.silu(h @ w_au + b_au) @ w_ad + b_ad).reshape(B, T, H, DK)
            bb = h @ w_beta + b_beta

            def step(carry, inp):
                s, mem = carry
                qt, kt, vt, sdt, abt, bbt = inp
                mem = DECAY * mem + sdt
                sur = jax.nn.sigmoid(SBETA * (mem - THR))
                hard = (mem > THR).astype(x.dtype)
                spike = sur + jax.lax.stop_gradient(hard - sur)
                mem = mem - spike * THR
                alpha = jax.nn.sigmoid(abt + alpha_spike * spike)
                beta = jax.nn.sigmoid(bbt[..., None] + jnp.sum(spike * beta_spike, axis=-1, keepdims=True))
                active = jax.lax.stop_gradient((jnp.sum(hard, axis=-1, keepdims=True) > 0).astype(x.dtype))
                alpha = jnp.where(active > 0, alpha, jnp.ones_like(alpha))
                beta = beta * active
                s = s * alpha[..., None]
                u = jnp.einsum('bhd,bhdv->bhv', kt, s)
                s = s - beta[..., None] * jnp.einsum('bhd,bhv->bhdv', kt, u)
                s = s + beta[..., None] * jnp.einsum('bhd,bhv->bhdv', kt, vt)
                out = jnp.einsum('bhdv,bhd->bhv', s, qt)
                return ((s, mem), out)
            s0 = jnp.zeros((B, H, DK, DV), x.dtype)
            m0 = jnp.zeros((B, H, DK), x.dtype)
            tmaj = lambda a: jnp.moveaxis(a, 1, 0)
            (s, mem), outs = jax.lax.scan(step, (s0, m0), (tmaj(q), tmaj(k), tmaj(v), tmaj(sd), tmaj(ab), tmaj(bb)))
            y = jnp.moveaxis(outs, 0, 1)
            y = y * jax.lax.rsqrt(jnp.mean(y * y, axis=-1, keepdims=True) + EPS) * w_hn
            y = y.reshape(B, T, H * DV)
            gate = jax.nn.sigmoid(jax.nn.silu(x @ w_u1 + b_u1) @ w_u2 + b_u2)
            y = x + y @ w_out * gate
            h2 = _rms(y, w_ffn)
            y = y + jax.nn.silu(h2 @ w_ff1) * (h2 @ w_ff3) @ w_ff2
            return (y, s, mem)

        def _reference_tuple_inner(x, w_norm_in, conv_w, conv_b, wq, wk, wv, w_out, w_spike, w_au, b_au, w_ad, b_ad, alpha_spike, w_beta, b_beta, beta_spike, w_hn, w_u1, b_u1, w_u2, b_u2, w_ffn, w_ff1, w_ff3, w_ff2):
            return _forward(x, w_norm_in, conv_w, conv_b, wq, wk, wv, w_out, w_spike, w_au, b_au, w_ad, b_ad, alpha_spike, w_beta, b_beta, beta_spike, w_hn, w_u1, b_u1, w_u2, b_u2, w_ffn, w_ff1, w_ff3, w_ff2)
        return _reference_tuple_inner(x, w_norm_in, conv_w, conv_b, wq, wk, wv, w_out, w_spike, w_au, b_au, w_ad, b_ad, alpha_spike, w_beta, b_beta, beta_spike, w_hn, w_u1, b_u1, w_u2, b_u2, w_ffn, w_ff1, w_ff3, w_ff2)[0]

    def _L0_ffn_ref(input_features, centroids, ln_g, ln_b, w1, b1, w2, b2):
        import jax, jax.numpy as jnp
        import numpy as np
        E, D, F = (8, 128, 512)
        LN_EPS = 1e-05
        x = input_features.reshape(-1, D)
        aff = jax.lax.stop_gradient(x) @ centroids.T
        assign = jnp.argmax(aff, axis=1)
        onehot = jax.nn.one_hot(assign, E, dtype=x.dtype)
        mu = jnp.mean(x, axis=-1, keepdims=True)
        var = jnp.mean((x - mu) ** 2, axis=-1, keepdims=True)
        xhat = (x - mu) * jax.lax.rsqrt(var + LN_EPS)
        xn = xhat[None, :, :] * ln_g[:, None, :] + ln_b[:, None, :]
        h = jax.nn.relu(jnp.einsum('etd,efd->etf', xn, w1) + b1[:, None, :])
        y = x[None, :, :] + jnp.einsum('etf,edf->etd', h, w2) + b2[:, None, :]
        alpha = jax.nn.sigmoid(x @ centroids.T)
        a = alpha.T[:, :, None]
        gated = a * y + (1.0 - a) * x[None, :, :]
        out = jnp.einsum('te,etd->td', onehot, gated)
        return out.reshape(input_features.shape)
    x = L0_attn_x
    x = _layernorm(x + _L0_attn_ref(x, L0_attn_w_norm_in, L0_attn_conv_w, L0_attn_conv_b, L0_attn_wq, L0_attn_wk, L0_attn_wv, L0_attn_w_out, L0_attn_w_spike, L0_attn_w_au, L0_attn_b_au, L0_attn_w_ad, L0_attn_b_ad, L0_attn_alpha_spike, L0_attn_w_beta, L0_attn_b_beta, L0_attn_beta_spike, L0_attn_w_hn, L0_attn_w_u1, L0_attn_b_u1, L0_attn_w_u2, L0_attn_b_u2, L0_attn_w_ffn, L0_attn_w_ff1, L0_attn_w_ff3, L0_attn_w_ff2), axis=-1)
    x = _layernorm(x + _L0_ffn_ref(x, L0_ffn_centroids, L0_ffn_ln_g, L0_ffn_ln_b, L0_ffn_w1, L0_ffn_b1, L0_ffn_w2, L0_ffn_b2), axis=-1)
    return x

_drawn_inputs = setup_inputs


def setup_inputs(seed=0):
    import zlib

    import numpy as np

    out = dict(_drawn_inputs(seed))
    spreads = {'L0_attn_w_norm_in': (1.0, 0.2),
     'L0_attn_conv_b': (0.0, 0.1),
     'L0_attn_b_au': (0.0, 0.8),
     'L0_attn_b_ad': (0.0, 0.1),
     'L0_attn_alpha_spike': (0.0, 0.712),
     'L0_attn_b_beta': (0.0, 0.709),
     'L0_attn_beta_spike': (0.0, 0.291),
     'L0_attn_w_hn': (1.0, 0.2),
     'L0_attn_b_u1': (0.0, 0.8),
     'L0_attn_b_u2': (0.0, 0.277),
     'L0_attn_w_ffn': (1.0, 0.6),
     'L0_ffn_ln_g': (1.0, 0.2),
     'L0_ffn_ln_b': (0.0, 0.278),
     'L0_ffn_b1': (0.0, 0.286),
     'L0_ffn_b2': (0.0, 0.1)}
    factors = {'L0_attn_w_au': 8.0,
     'L0_attn_w_ad': 8.0,
     'L0_attn_w_beta': 3.345,
     'L0_attn_w_u1': 4.707,
     'L0_attn_w_u2': 6.284}
    for name, (base, spread) in spreads.items():
        noise = np.random.default_rng([zlib.crc32(name.encode()), seed]).standard_normal(out[name].shape)
        drawn = base * np.exp(spread * noise) if base else spread * noise
        out[name] = jnp.asarray(drawn.astype(out[name].dtype))
    for name, factor in factors.items():
        out[name] = (out[name] * factor).astype(out[name].dtype)
    return out
```

```python
from contextlib import ExitStack

import concourse.bass as bass
from concourse import mybir

F32 = mybir.dt.float32
BF16 = mybir.dt.bfloat16
ALU = mybir.AluOpType
ACT = mybir.ActivationFunctionType
AX = mybir.AxisListType

P = 128
NB, NT, D = 16, 256, 128
H, DK, DV = 8, 64, 128
HP = H // 2
CH = 32
NC = NT // CH
TOK = NB * CH
NG = TOK // P
GB = P // CH
UN = HP * NG * 2
R = 64
FF = 512
FT = FF // P
E = 8
LEAF, BLK = 8, 16
THR2 = 1.0
DECAY = 0.9
EPS = 1e-6
LN_EPS = 1e-5
TINY = 1e-18
LMAX = 20.0
TILES = 2 * NG


class Signal:

    def __init__(self, sem, per, start=0):
        self.sem, self.per, self.start = sem, per, start

    def at(self, c, n, back=0):
        return c * self.per + (n + self.start - back * self.per)


class Bank:

    def __init__(self, tensor, full, drained, fills):
        self.t, self.fills = tensor, list(fills)
        self.full = Signal(full, len(self.fills))
        self.drained = Signal(drained, len(self.fills), 1)

    def filled(self, c, fill, back=0):
        return self.full.at(c, self.fills.index(fill) + 1, back)

    def emptied(self, c, fill, back=0):
        return self.drained.at(c, self.fills.index(fill) + 1, back)

    def freed(self, c, fill):
        return self.drained.at(c, self.fills.index(fill))

    def n(self, fill):
        return self.fills.index(fill)


class Count:

    def __init__(self):
        self.n = 0

    def next(self):
        self.n += 1
        return 1


def later(c):
    return not isinstance(c, int)


def build(nc, a, out):
    top = ExitStack()
    with top:
        sem = lambda name: top.enter_context(nc.semaphore(name))
        ctx = ExitStack()
        sb = lambda name, shape, dt=F32: ctx.enter_context(nc.sbuf_tensor(name, shape, dt))
        attn_d = nc.dram_tensor("attn_d", (NC, P, TOK), F32, kind="Internal").ap()
        with ctx:
            attention(nc, a, attn_d, ctx, sb, sem)
        ctx = ExitStack()
        sb = lambda name, shape, dt=F32: ctx.enter_context(nc.sbuf_tensor(name, shape, dt))
        with ctx:
            feed_forward(nc, a, attn_d, out, ctx, sb, sem)


def attention(nc, a, attn_d, ctx, sb, sem):
    a_d = nc.dram_tensor("a_d", (GB, CH, UN, CH), F32, kind="Internal").ap()
    b_d = nc.dram_tensor("b_d", (GB, CH, NG, H, CH), F32, kind="Internal").ap()
    u_d = nc.dram_tensor("u_d", (GB, NG, H, CH, CH), F32, kind="Internal").ap()

    wq, wk, wsd = sb("wq", [P, H * DK]), sb("wk", [P, H * DK]), sb("wsd", [P, H * DK])
    wad = sb("wad", [R + 1, H * DK])
    wv = sb("wv", [P, H * DV])
    wout = sb("wout", [P, H, D])
    w_hn = sb("w_hn", [P, H])
    wau = sb("wau", [P, R])
    wbeta = sb("wbeta", [P, H])
    bbeta = sb("bbeta", [P, HP, NG, 2])
    wnorm, convw, convb = sb("wnorm", [P, 1]), sb("convw", [P, 4]), sb("convb", [P, 1])
    bau = sb("bau", [R, 1])
    aspike, bspike = sb("aspike", [P, HP]), sb("bspike", [P, HP])
    bsrest = sb("bsrest", [P, HP])
    bsel = sb("bsel", [P, HP, 8], BF16)
    ident = sb("ident", [P, P])
    eye = sb("eye", [P, CH])
    leafmask = sb("leafmask", [P, 2, CH])
    rowmask = sb("rowmask", [P, 3])
    headind = sb("headind", [P, 2, HP, 16])
    meanw = sb("meanw", [P, P])
    sumblk = sb("sumblk", [P, P], BF16)
    sumblk_f = sb("sumblk_f", [P, P])
    step0 = sb("step0", [P, NB, CH])
    eps_t, tiny_t = sb("eps_t", [P, 1]), sb("tiny_t", [P, 1])

    xt, xsq = sb("xt", [P, TOK]), sb("xsq", [P, TOK])
    rstd = xsq
    hn = sb("hn", [P, NB, CH + 3])
    cacc, tz, h = sb("cacc", [P, NB, CH]), sb("tz", [P, TOK]), sb("h", [P, TOK])
    zau, au = sb("zau", [R, TOK]), sb("au", [R + 1, TOK])
    tau = sb("tau", [R, TOK])
    mem = sb("mem", [P, HP, NB, CH])
    carry, residue = sb("carry", [P, HP * NB]), sb("residue", [P, HP * NB])
    sp = sb("sp", [P, HP, NB * CH], BF16)
    kq, kqsq = sb("kq", [P, 2, TOK]), sb("kqsq", [P, 2, TOK])
    ss_row = sb("ss_row", [16, TOK])
    dend, dleaf, dpair, dblk = (sb(x, [P, TOK]) for x in ("dend", "dleaf", "dpair", "dblk"))
    eleaf, estart = sb("eleaf", [P, TOK]), sb("estart", [P, TOK])
    gam = sb("gam", [P, HP, NB])
    kq_leaf, kq_pair, kq_blk = (sb(x, [P, 2, TOK]) for x in ("kq_leaf", "kq_pair", "kq_blk"))
    km, kend = sb("km", [P, TOK]), sb("kend", [P, TOK])
    kq_start = sb("kq_start", [P, HP, 2, TOK])
    kend_t = sb("kend_t", [P, NG, HP, P])
    ab = sb("ab", [P, HP, 2, 8, CH])
    ca = sb("ca", [P, NG, H, CH])
    na, tu, tmp = sb("na", [P, CH, CH]), sb("tu", [P, CH, CH]), sb("tmp", [P, CH * CH // 4])
    stat = sb("stat", [P, UN * 4 + UN])
    logit, beta = sb("logit", [P, UN]), sb("beta", [P, UN])
    act_n, nrm, inv = sb("act_n", [P, UN]), sb("nrm", [P, 2, UN]), sb("inv", [P, 2, UN])
    sqn = sb("sqn", [P, 2, UN])
    cvec, q2 = sb("cvec", [P, UN]), sb("q2", [P, UN])
    state = sb("state", [P, HP, NB, DV])
    ub, bb = sb("ub", [P, 2, 8, P]), sb("bb", [P, 2, 8, P])
    nv, r, w = sb("nv", [P, 4, DV]), sb("r", [P, 4, DV]), sb("w", [P, 4, DV])
    ysb, ysq = sb("ysb", [P, 2, 8, DV]), sb("ysq", [P, 4, DV])
    yss, yr = sb("yss", [P, H]), sb("yr", [P, H])
    yt = sb("yt", [P, 8, P])
    attn = sb("attn", [P, TOK])

    front = ["ms", "sd0", "sd1", "sd2", "sd3", "au"]
    for p in range(HP):
        front += [f"ab{p}", f"cnt{p}"]
    front += ["beta"]
    for p in range(HP):
        front += [f"k{p}", f"q{p}", f"leaf{p}", f"cross{p}", f"kend{p}"]
    front += ["sst"] + [f"v{i}" for i in range(TILES)]
    psum = [ctx.enter_context(nc.psum_tensor(f"ps{i}", [P, 512], F32)) for i in range(8)]

    def bank(i, name, fills):
        return Bank(psum[i], sem(f"{name}_full"), sem(f"{name}_drained"), fills)

    ring = [bank(0, "front0", front[0::2]), bank(1, "front1", front[1::2])]
    bp = bank(2, "pred", ["p0"] + [x for i in range(TILES + 1) for x in
                                   ([f"p{i + 1}"] if i + 1 < TILES else []) +
                                   ([f"o{i // 2 - 1}"] if i % 2 == 0 and i else [])])
    bw = bank(3, "write", [f"w{i}" for i in range(TILES)])
    by = bank(4, "read", [f"y{i}" for i in range(TILES)])
    bm = bank(5, "turn", ["ss"] + [f"t{i}" for i in range(TILES)])
    bd = [bank(6 + j, f"delta{j}", [f"d{i}" for i in range(TILES)]) for j in range(2)]
    bank_of = {f: b for b in ring + [bp, bw, by, bm] for f in b.fills}

    sig = lambda name, per: Signal(sem(name), per)
    passed_pe, passed_pool, passed_sp = sem("passed_pe"), sem("passed_pool"), sem("passed_sp")
    s_const, s_zero = sem("const_loaded"), sem("constants_made")
    x_loaded = sig("x_loaded", 16)
    xsq_ready, rstd_ready = sig("xsq_ready", 1), sig("rstd_ready", 1)
    halo_ready, hn_ready, conv_step = sig("halo_ready", 1), sig("hn_ready", 1), sig("conv_step", 4)
    tz_ready, h_ready = sig("tz_ready", 1), sig("h_ready", 1)
    tau_ready, au_ready = sig("tau_ready", 1), sig("au_ready", 1)
    rec_step = sem("rec_step")
    sp_ready = sig("sp_ready", 1)
    xa_ready, e1_ready = sig("xa_ready", HP), sig("e1_ready", HP)
    l_ready, g_ready = sig("l_ready", 1), sig("g_ready", 1)
    d_ready, e_ready = sig("d_ready", HP), sig("e_ready", HP)
    kq_ready, kqsq_used = sig("kq_ready", 2 * HP), sig("kqsq_used", 2 * HP - 1)
    prod_ready, kstart_ready = sig("prod_ready", HP), sig("kstart_ready", HP)
    cross_step = sig("cross_step", 2 * HP)
    bsel_cleared, bsel_step = sem("bsel_cleared"), sem("bsel_step")
    row_step = sem("row_step")
    small = sig("small_step", 15)
    ab_ready, ca_step = sig("ab_ready", 1), sig("ca_step", 2)
    a_stored, b_stored, na_loaded = sig("a_stored", 16), sig("b_stored", 16 * NG), sig("na_loaded", 64)
    tu_cleared, tri_step, tri_done = sig("tu_cleared", 1), sem("tri_step"), sig("tri_done", 1)
    u_stored = sig("u_stored", 16)
    ub_loaded = [sig(f"ub_loaded{j}", 128) for j in range(2)]
    bb_loaded = [sig(f"bb_loaded{j}", 128) for j in range(2)]
    yss_ready, ylog, yrs_ready = sig("yss_ready", NG), sig("ylog", NG), sig("yrs_ready", NG)
    ysum_step, yn_ready = sig("ysum_step", TILES), sig("yn_ready", NG)
    yr_ready = sig("yr_ready", NG)
    attn_stored = sig("attn_stored", 16)

    loads = [
        (wq[:, :], a["wq"]), (wk[:, :], a["wk"]), (wsd[:, :], a["w_spike"]), (wad[0:R, :], a["w_ad"]),
        (wad[R:R + 1, :], a["b_ad"].unsqueeze(0)), (wv[:, :], a["wv"]), (wout[:, :, :], a["w_out"]),
        (w_hn[:, :], a["w_hn"]), (wau[:, :], a["w_au"]), (wbeta[:, :], a["w_beta"]),
        (wnorm[:, :], a["w_norm_in"].unsqueeze(1)), (convw[:, :], a["conv_w"]), (convb[:, :], a["conv_b"].unsqueeze(1)),
        (bau[:, :], a["b_au"].unsqueeze(1)), (aspike[:, :], a["alpha_spike"]), (bspike[:, :], a["beta_spike"]),
        (ident[:, :], a["ident"]), (eye[:, :], a["eye"]), (leafmask[:, :, :], a["leafmask"]),
        (rowmask[:, :], a["rowmask"]), (headind[:, :, :, :], a["headind"]), (sumblk_f[:, :], a["sumblk"]),
    ]
    for g in range(NG):
        loads.append((bbeta[:, :, g, :], a["b_beta"].rearrange("(p h) -> p h", h=2).unsqueeze(0).broadcast_to([P, HP, 2])))
    n_const = 16 * len(loads)
    n_made = 17

    def quad(t, g, q):
        return t.rearrange("p (a g h) -> p a g h", g=NG, h=2)[:, 2 * q:2 * q + 2, g, :]

    block = ctx.enter_context(nc.Block())

    def chunks(eng, body):
        body(0)
        with eng.Fori(1, NC) as c:
            body(c)

    @block.sync
    def _(sp_e):
        for dst, src in loads:
            sp_e.dma_start(dst, src).then_inc(s_const, 16)

        def settle(c):
            if later(c):
                sp_e.sem_inc(passed_sp, 1)

        def body(c):
            sp_e.wait_ge(ab_ready.sem, ab_ready.at(c, 1))
            settle(c)
            for j in range(2):
                if later(c):
                    sp_e.wait_ge(bb_loaded[j].sem, bb_loaded[j].at(c, 128, 1))
            for g in range(NG):
                sp_e.dma_start(b_d[:, :, g, :, :].rearrange("b j (a h) i -> (b j) a (h i)", h=2),
                               ab[:, :, 1, 2 * g:2 * g + 2, :].rearrange("p a h i -> p a (h i)")
                               ).then_inc(b_stored.sem, 16)
            sp_e.wait_ge(ca_step.sem, ca_step.at(c, 2))
            settle(c)
            if later(c):
                sp_e.wait_ge(na_loaded.sem, na_loaded.at(c, 64, 1))
            sp_e.dma_start(a_d.rearrange("b i u j -> (b i) (u j)"),
                           ca[:, :, :, :].rearrange("p g u j -> p (g u j)")).then_inc(a_stored.sem, 16)
            sp_e.wait_ge(a_stored.sem, a_stored.at(c, 16))
            settle(c)
            if later(c):
                sp_e.wait_ge(tri_done.sem, tri_done.at(c, 1, 1))
            for b4 in range(GB):
                sp_e.dma_start(na[CH * b4:CH * b4 + CH, :, :],
                               a_d[b4].rearrange("i u j -> u i j")).then_inc(na_loaded.sem, 16)
            sp_e.wait_ge(tri_done.sem, tri_done.at(c, 1))
            for j in range(2):
                if later(c):
                    sp_e.wait_ge(ub_loaded[j].sem, ub_loaded[j].at(c, 128, 1))
            sp_e.dma_start(u_d.rearrange("b g h c i -> (b g h) (c i)"),
                           tu[:, :, :].rearrange("p c i -> p (c i)")).then_inc(u_stored.sem, 16)
            sp_e.wait_ge(u_stored.sem, u_stored.at(c, 16))
            settle(c)
            sp_e.wait_ge(b_stored.sem, b_stored.at(c, 16 * NG))
            for g in range(NG):
                back, last = (1, TILES - 1 - 2 * (1 - g)) if g < 2 else (0, 2 * (g - 2) + 1)
                if not back or later(c):
                    sp_e.wait_ge(by.full.sem, by.full.at(c, last + 1, back))
                for buf, dram, loaded in ((ub, u_d, ub_loaded), (bb, b_d, bb_loaded)):
                    for b4 in range(GB):
                        rows, cols = slice(CH * b4, CH * b4 + CH), slice(CH * b4, CH * b4 + CH)
                        src = dram[b4, g].rearrange("h c i -> c h i") if dram is u_d else dram[b4, :, g]
                        sp_e.dma_start(buf[rows, g % 2, :, cols], src).then_inc(loaded[g % 2].sem, 16)
            sp_e.wait_ge(bank_of[f"o{NG - 1}"].drained.sem, bank_of[f"o{NG - 1}"].emptied(c, f"o{NG - 1}"))
            sp_e.dma_start(attn_d[c], attn[:, :]).then_inc(attn_stored.sem, 16)

        chunks(sp_e, body)
        sp_e.wait_ge(attn_stored.sem, 16 * NC)

    @block.gpsimd
    def _(pool):
        for b in ring + [bp, bw, by, bm] + bd:
            pool.sem_inc(b.drained.sem, 1)
        pool.memset(hn[:, :, :], 0.0).then_inc(s_zero, 1)
        pool.memset(state[:, :, :, :], 0.0).then_inc(s_zero, 1)
        pool.memset(carry[:, :], 0.0).then_inc(s_zero, 1)
        pool.memset(ub[:, :, :, :], 0.0).then_inc(s_zero, 1)
        pool.memset(bb[:, :, :, :], 0.0).then_inc(s_zero, 1)
        pool.memset(meanw[:, :], 1.0 / D).then_inc(s_zero, 1)
        pool.memset(eps_t[:, :], EPS).then_inc(s_zero, 1)
        pool.memset(tiny_t[:, :], TINY).then_inc(s_zero, 1)
        pool.memset(step0[:, :, 1:CH], 1.0).then_inc(s_zero, 1)
        pool.memset(step0[:, :, 0:1], 0.0).then_inc(s_zero, 1)

        def settle(c):
            if later(c):
                pool.sem_inc(passed_pool, 1)

        def body(c):
            if later(c):
                pool.wait_ge(xsq_ready.sem, xsq_ready.at(c, 1, 1))
            if later(c):
                pool.wait_ge(hn_ready.sem, hn_ready.at(c, 1, 1))
            settle(c)
            pool.dma_start(xt[:, :], a["xT"][c]).then_inc(x_loaded.sem, 16)
            for p in range(HP):
                if p == 0:
                    pool.wait_ge(g_ready.sem, g_ready.at(c, 1))
                    if later(c):
                        pool.wait_ge(kstart_ready.sem, kstart_ready.at(c, HP, 1))
                else:
                    pool.wait_ge(kstart_ready.sem, kstart_ready.at(c, p))
                settle(c)
                g3 = mem[:, p, :, :].rearrange("p b t -> p (b t)")
                for dst, span, anchor in ((dleaf, LEAF, LEAF // 2 - 1), (dpair, BLK, LEAF - 1),
                                          (dblk, CH, BLK - 1), (dend, CH, CH - 1)):
                    v = g3.rearrange("p (n t) -> p n t", t=span)
                    i = pool.tensor_tensor(dst[:, :].rearrange("p (n t) -> p n t", t=span), v,
                                           v[:, :, anchor:anchor + 1].broadcast_to([P, TOK // span, span]),
                                           ALU.subtract)
                i.then_inc(d_ready.sem, 1)
            if later(c):
                pool.wait_ge(u_stored.sem, u_stored.at(c, 16, 1))
            settle(c)
            pool.memset(tu[:, :, :], 0.0).then_inc(tu_cleared.sem, 1)

        pool.wait_ge(s_zero, n_made)
        chunks(pool, body)

    @block.scalar
    def _(act):
        act.wait_ge(s_const, n_const)
        act.activation(sumblk[:, :], sumblk_f[:, :], ACT.Copy).then_inc(s_zero, 1)
        act.wait_ge(s_zero, n_made)

        def body(c):
            act.wait_ge(x_loaded.sem, x_loaded.at(c, 16))
            act.activation(xsq[:, :], xt[:, :], ACT.Square).then_inc(xsq_ready.sem, 1)
            act.wait_ge(bank_of["ms"].full.sem, bank_of["ms"].filled(c, "ms"))
            act.activation(rstd[:, :], ring[0].t[:, :], ACT.Ln, bias=eps_t[:, 0:1]).then_inc(ring[0].drained.sem, 1)
            act.wait_ge(bank_of["ms"].drained.sem, bank_of["ms"].emptied(c, "ms"))
            act.activation(rstd[:, :], rstd[:, :], ACT.Exp, scale=-0.5).then_inc(rstd_ready.sem, 1)
            act.wait_ge(conv_step.sem, conv_step.at(c, 4))
            act.activation(tz[:, :], cacc[:, :, :].rearrange("p b t -> p (b t)"), ACT.Tanh).then_inc(tz_ready.sem, 1)
            if later(c):
                act.wait_ge(d_ready.sem, d_ready.at(c, HP, 1))
            for p in range(HP):
                act.wait_ge(bank_of[f"sd{p}"].full.sem, bank_of[f"sd{p}"].filled(c, f"sd{p}"))
                b = bank_of[f"sd{p}"]
                act.activation(mem[:, p, :, :].rearrange("p b t -> p (b t)"), b.t[:, :], ACT.Copy,
                               scale=2.0).then_inc(b.drained.sem, 1)
            act.wait_ge(bank_of["au"].drained.sem, bank_of["au"].emptied(c, "au"))
            act.activation(tau[:, :], zau[:, :], ACT.Tanh).then_inc(tau_ready.sem, 1)
            for p in range(HP):
                x = mem[:, p, :, :].rearrange("p b t -> p (b t)")
                act.wait_ge(xa_ready.sem, xa_ready.at(c, p + 1))
                act.activation(x, x, ACT.Exp, scale=-1.0).then_inc(e1_ready.sem, 1)
            act.wait_ge(bank_of[f"cnt{HP - 1}"].drained.sem, bank_of[f"cnt{HP - 1}"].emptied(c, f"cnt{HP - 1}"))
            x = mem[:, :, :, :].rearrange("p a b t -> p (a b t)")
            act.activation(x, x, ACT.Ln, bias=1.0).then_inc(l_ready.sem, 1)
            act.wait_ge(small.sem, small.at(c, 3))
            act.activation(beta[:, :], logit[:, :], ACT.Exp, scale=-1.0).then_inc(small.sem, 1)
            for p in range(HP):
                for j, name in ((0, "k"), (1, "q")):
                    b = bank_of[f"{name}{p}"]
                    act.wait_ge(b.full.sem, b.filled(c, f"{name}{p}"))
                    if j == 0:
                        if p or later(c):
                            act.wait_ge(kstart_ready.sem, kstart_ready.at(c, p))
                    act.activation(kq[:, j, :], b.t[:, :], ACT.Copy).then_inc(kq_ready.sem, 1)
                    if p:
                        act.wait_ge(kqsq_used.sem, kqsq_used.at(c, 2 * p + j - 1))
                    act.activation(kqsq[:, j, :], b.t[:, :], ACT.Square).then_inc(b.drained.sem, 1)
                act.wait_ge(d_ready.sem, d_ready.at(c, p + 1))
                g3 = mem[:, p, :, :].rearrange("p b t -> p (b t)")
                act.activation(eleaf[:, :], dleaf[:, :], ACT.Exp, scale=-1.0)
                act.activation(dleaf[:, :], dleaf[:, :], ACT.Exp)
                for t, span in ((dpair, BLK), (dblk, CH)):
                    v = t[:, :].rearrange("p (n t) -> p n t", t=span)
                    act.activation(v[:, :, 0:span // 2], v[:, :, 0:span // 2], ACT.Exp)
                    act.activation(v[:, :, span // 2:span], v[:, :, span // 2:span], ACT.Exp, scale=-1.0)
                act.activation(dend[:, :], dend[:, :], ACT.Exp)
                act.activation(gam[:, p, :], mem[:, p, :, CH - 1], ACT.Exp, scale=-1.0)
                act.activation(estart[:, :], g3, ACT.Exp, scale=-1.0).then_inc(e_ready.sem, 1)
                b = bank_of[f"kend{p}"]
                act.wait_ge(b.full.sem, b.filled(c, f"kend{p}"))
                if p == 0:
                    for j in range(2):
                        if later(c):
                            act.wait_ge(bd[j].full.sem, bd[j].full.at(c, TILES, 1))
                act.activation(kend_t[:, :, p, :], b.t[:, :].rearrange("p (g k) -> p g k", g=NG),
                               ACT.Copy).then_inc(b.drained.sem, 1)
            act.wait_ge(bank_of["ss"].full.sem, bank_of["ss"].filled(c, "ss"))
            act.activation(ss_row[:, :], bm.t[0:16, :], ACT.Copy).then_inc(bm.drained.sem, 1)
            act.wait_ge(bank_of["sst"].drained.sem, bank_of["sst"].emptied(c, "sst"))
            act.activation(sqn[:, :, :], nrm[:, :, :], ACT.Ln, bias=tiny_t[:, 0:1]).then_inc(small.sem, 1)
            act.wait_ge(small.sem, small.at(c, 9))
            act.activation(sqn[:, :, :], sqn[:, :, :], ACT.Exp, scale=0.5).then_inc(small.sem, 1)
            for i in range(TILES + 1):
                if i < TILES:
                    act.wait_ge(bank_of[f"w{i}"].full.sem, bank_of[f"w{i}"].filled(c, f"w{i}"))
                    if i:
                        act.wait_ge(bd[1].full.sem, bd[1].full.at(c, i))
                    act.activation(w[:, :, :].rearrange("p h v -> p (h v)"), bw.t[:, :],
                                   ACT.Copy).then_inc(bw.drained.sem, 1)
                if i % 2 == 0 and i:
                    g = i // 2 - 1
                    act.wait_ge(yss_ready.sem, yss_ready.at(c, g + 1))
                    act.activation(yr[:, :], yss[:, :], ACT.Ln, bias=eps_t[:, 0:1]).then_inc(ylog.sem, 1)
                    act.wait_ge(ylog.sem, ylog.at(c, g + 1))
                    act.activation(yr[:, :], yr[:, :], ACT.Exp, scale=-0.5).then_inc(yrs_ready.sem, 1)
                if i < TILES:
                    g, q = i // 2, i % 2
                    act.wait_ge(bank_of[f"y{i}"].full.sem, bank_of[f"y{i}"].filled(c, f"y{i}"))
                    if i:
                        act.wait_ge(ysum_step.sem, ysum_step.at(c, i))
                    ytile = by.t[:, :].rearrange("p (h v) -> p h v", v=DV)
                    act.activation(ysb[:, g % 2, 4 * q:4 * q + 4, :], ytile, ACT.Copy)
                    act.activation(ysq[:, :, :], ytile, ACT.Square).then_inc(by.drained.sem, 1)
                if i % 2 == 0 and i:
                    g = i // 2 - 1
                    for q in range(2):
                        act.wait_ge(bank_of[f"t{2 * g + q}"].full.sem, bank_of[f"t{2 * g + q}"].filled(c, f"t{2 * g + q}"))
                        act.activation(yt[:, 4 * q:4 * q + 4, :].rearrange("p h t -> p (h t)"), bm.t[:, :],
                                       ACT.Copy).then_inc(bm.drained.sem, 1)
                    act.wait_ge(bank_of[f"o{g}"].full.sem, bank_of[f"o{g}"].filled(c, f"o{g}"))
                    if g == 0:
                        if later(c):
                            act.wait_ge(attn_stored.sem, attn_stored.at(c, 16, 1))
                    act.activation(attn[:, P * g:P * g + P], bp.t[:, 0:P], ACT.Copy).then_inc(bp.drained.sem, 1)

        chunks(act, body)

    @block.tensor
    def _(pe):
        pe.wait_ge(s_const, n_const)
        pe.wait_ge(s_zero, n_made)

        def settle(c):
            if later(c):
                pe.sem_inc(passed_pe, 1)


        def predict(c, i, runs):
            g, q = i // 2, i % 2
            pe.wait_ge(bank_of[f"p{i}"].drained.sem, bank_of[f"p{i}"].freed(c, f"p{i}"))
            if i == 0:
                pe.wait_ge(kstart_ready.sem, kstart_ready.at(c, HP))
            for j in range(2):
                if later(c):
                    pe.wait_ge(bd[j].drained.sem, bd[j].drained.at(c, i + 1, 1))
            settle(c)
            for hq in (0, 2, 1, 3):
                hp, h2 = 2 * q + hq // 2, hq % 2
                rows = slice(DK * h2, DK * h2 + DK)
                if hq == 1:
                    m.then_inc(row_step, runs.next())
                    pe.wait_ge(row_step, runs.n)
                for b4 in range(GB):
                    b = GB * g + b4
                    m = pe.matmul(bp.t[CH * b4:CH * b4 + CH, DV * hq:DV * hq + DV],
                                  kq_start[rows, hp, 0, CH * b:CH * b + CH], state[rows, hp, b, :],
                                  start=True, stop=True)
            m.then_inc(bp.full.sem, 1)

        def values(c, i):
            g, q = i // 2, i % 2
            b = bank_of[f"v{i}"]
            pe.wait_ge(b.drained.sem, b.freed(c, f"v{i}"))
            settle(c)
            pe.matmul(b.t[:, :], h[:, P * g:P * g + P], wv[:, 512 * q:512 * q + 512],
                      start=True, stop=True).then_inc(b.full.sem, 1)

        def body(c):
            runs = Count()
            pe.wait_ge(bank_of["ms"].drained.sem, bank_of["ms"].freed(c, "ms"))
            pe.wait_ge(xsq_ready.sem, xsq_ready.at(c, 1))
            settle(c)
            pe.matmul(ring[0].t[:, :], meanw[:, :], xsq[:, :], start=True, stop=True).then_inc(ring[0].full.sem, 1)
            pe.wait_ge(h_ready.sem, h_ready.at(c, 1))
            for p in range(HP):
                b = bank_of[f"sd{p}"]
                pe.wait_ge(b.drained.sem, b.freed(c, f"sd{p}"))
                settle(c)
                pe.matmul(b.t[:, :], wsd[:, P * p:P * p + P], h[:, :], start=True, stop=True).then_inc(b.full.sem, 1)
            b = bank_of["au"]
            pe.wait_ge(b.drained.sem, b.freed(c, "au"))
            settle(c)
            pe.matmul(b.t[0:R, :], wau[:, :], h[:, :], start=True, stop=True).then_inc(b.full.sem, 1)
            for p in range(HP):
                b = bank_of[f"ab{p}"]
                if p == 0:
                    pe.wait_ge(au_ready.sem, au_ready.at(c, 1))
                pe.wait_ge(bank_of[f"ab{p}"].drained.sem, bank_of[f"ab{p}"].freed(c, f"ab{p}"))
                settle(c)
                pe.matmul(b.t[:, :], wad[:, P * p:P * p + P], au[:, :], start=True, stop=True).then_inc(b.full.sem, 1)
                b = bank_of[f"cnt{p}"]
                if p == 0:
                    pe.wait_ge(sp_ready.sem, sp_ready.at(c, 1))
                pe.wait_ge(bank_of[f"cnt{p}"].drained.sem, bank_of[f"cnt{p}"].freed(c, f"cnt{p}"))
                settle(c)
                pe.matmul(b.t[:, :], sumblk[:, :], sp[:, p, :], start=True, stop=True).then_inc(b.full.sem, 1)
            b = bank_of["beta"]
            pe.wait_ge(b.drained.sem, b.freed(c, "beta"))
            settle(c)
            units = b.t[:, 0:4 * UN].rearrange("p (a g n) -> p a g n", a=HP, g=NG)
            lin = b.t[:, 4 * UN:5 * UN].rearrange("p (a g h) -> p a g h", a=HP, g=NG)
            for g in range(NG):
                for p in range(HP):
                    pe.matmul(units[:, p, g, :], sp[:, p, P * g:P * g + P], bsel[:, p, :], start=True, stop=True)
            for g in range(NG):
                m = pe.matmul(lin[:, :, g, :], h[:, P * g:P * g + P], wbeta[:, :].rearrange("p (a h) -> p a h", h=2),
                              start=True, stop=True)
            m.then_inc(b.full.sem, 1)
            for p in range(HP):
                for name, wt in (("k", wk), ("q", wq)):
                    b = bank_of[f"{name}{p}"]
                    pe.wait_ge(b.drained.sem, b.freed(c, f"{name}{p}"))
                    settle(c)
                    pe.matmul(b.t[:, :], wt[:, P * p:P * p + P], h[:, :], start=True, stop=True).then_inc(b.full.sem, 1)
                for j, name in enumerate("kq"):
                    first, last = p == 0 and j == 0, p == HP - 1 and j == 1
                    pe.wait_ge(bank_of[f"{name}{p}"].drained.sem, bank_of[f"{name}{p}"].emptied(c, f"{name}{p}"))
                    if first:
                        pe.wait_ge(bank_of["ss"].drained.sem, bank_of["ss"].freed(c, "ss"))
                    settle(c)
                    pe.matmul(bm.t[0:16, :], headind[:, j, p, :], kqsq[:, j, :], start=first,
                              stop=last).then_inc(bm.full.sem if last else kqsq_used.sem, 1)
                b = bank_of[f"leaf{p}"]
                pe.wait_ge(prod_ready.sem, prod_ready.at(c, p + 1))
                pe.wait_ge(bank_of[f"leaf{p}"].drained.sem, bank_of[f"leaf{p}"].freed(c, f"leaf{p}"))
                settle(c)
                leaf = b
                o = b.t[:, :].rearrange("p (m u i) -> p m u i", m=2, u=8)
                cross = bank_of[f"cross{p}"]
                o1 = cross.t[:, 0:256].rearrange("p (m u n i) -> p m u n i", m=2, u=8, n=2)
                o2 = cross.t[:, 256:512].rearrange("p (m u i) -> p m u i", m=2, u=8)
                for h2 in range(2):
                    rows = slice(DK * h2, DK * h2 + DK)
                    if h2:
                        pe.wait_ge(row_step, runs.n - 1)
                    for g in range(NG):
                        for b4 in range(GB):
                            t = CH * (GB * g + b4)
                            m = pe.matmul(o[CH * b4:CH * b4 + CH, :, 2 * g + h2, :], km[rows, t:t + CH],
                                          kq_leaf[rows, :, t:t + CH], start=True, stop=True)
                    if h2:
                        m.then_inc(leaf.full.sem, 1)
                        pe.wait_ge(row_step, runs.n)
                    else:
                        m.then_inc(row_step, runs.next())
                        pe.wait_ge(bank_of[f"cross{p}"].drained.sem, bank_of[f"cross{p}"].freed(c, f"cross{p}"))
                        settle(c)
                    for g in range(NG):
                        for b4 in range(GB):
                            t, u = CH * (GB * g + b4), 2 * g + h2
                            part = slice(CH * b4, CH * b4 + CH)
                            second = kq_pair[rows, :, t:t + CH].rearrange("p m (n i) -> p m n i", i=BLK)[:, :, :, LEAF:BLK]
                            pe.matmul(o1[part, :, u, :, :], kq_pair[rows, 0, t:t + CH], second, start=True, stop=True)
                            m = pe.matmul(o2[part, :, u, :], kq_blk[rows, 0, t:t + CH], kq_blk[rows, :, t + BLK:t + CH],
                                          start=True, stop=True)
                    if h2:
                        m.then_inc(cross.full.sem, 1)
                    else:
                        m.then_inc(row_step, runs.next())
                b = bank_of[f"kend{p}"]
                pe.wait_ge(b.drained.sem, b.freed(c, f"kend{p}"))
                settle(c)
                for g in range(NG):
                    m = pe.transpose(b.t[:, P * g:P * g + P], kend[:, P * g:P * g + P], ident[:, :])
                m.then_inc(b.full.sem, 1)
            b = bank_of["sst"]
            pe.wait_ge(bank_of["ss"].drained.sem, bank_of["ss"].emptied(c, "ss"))
            pe.wait_ge(bank_of["sst"].drained.sem, bank_of["sst"].freed(c, "sst"))
            settle(c)
            for g in range(NG):
                m = pe.transpose(b.t[:, 16 * g:16 * g + 16], ss_row[:, P * g:P * g + P], ident[0:16, 0:16])
            m.then_inc(b.full.sem, 1)

            values(c, 0)
            predict(c, 0, runs)
            for i in range(TILES + 1):
                g, q = i // 2, i % 2
                if i < TILES:
                    if i + 1 < TILES:
                        values(c, i + 1)
                    pe.wait_ge(bank_of[f"p{i}"].drained.sem, bank_of[f"p{i}"].emptied(c, f"p{i}"))
                    if q == 0:
                        pe.wait_ge(ub_loaded[g % 2].sem, ub_loaded[g % 2].at(c, 64 * (g // 2) + 64))
                    pe.wait_ge(bank_of[f"w{i}"].drained.sem, bank_of[f"w{i}"].freed(c, f"w{i}"))
                    settle(c)
                    for hq in range(4):
                        m = pe.matmul(bw.t[:, DV * hq:DV * hq + DV], ub[:, g % 2, 4 * q + hq, :], r[:, hq, :],
                                      start=True, stop=True)
                    m.then_inc(bw.full.sem, 1)
                    if i + 1 < TILES:
                        predict(c, i + 1, runs)
                    pe.wait_ge(bank_of[f"w{i}"].drained.sem, bank_of[f"w{i}"].emptied(c, f"w{i}"))
                    if q == 0:
                        pe.wait_ge(bb_loaded[g % 2].sem, bb_loaded[g % 2].at(c, 64 * (g // 2) + 64))
                    pe.wait_ge(bank_of[f"y{i}"].drained.sem, bank_of[f"y{i}"].freed(c, f"y{i}"))
                    settle(c)
                    for hq in range(4):
                        cols = slice(DV * hq, DV * hq + DV)
                        m = pe.matmul(by.t[:, cols], bb[:, g % 2, 4 * q + hq, :], w[:, hq, :], start=(hq == 0), stop=False)
                    m.then_inc(row_step, runs.next())
                    pe.wait_ge(row_step, runs.n)
                    for hq in (0, 2, 1, 3):
                        hp, rows = 2 * q + hq // 2, slice(DK * (hq % 2), DK * (hq % 2) + DK)
                        cols = slice(DV * hq, DV * hq + DV)
                        if hq == 1:
                            m.then_inc(row_step, runs.next())
                            pe.wait_ge(row_step, runs.n)
                        for b4 in range(GB):
                            b = GB * g + b4
                            m = pe.matmul(by.t[CH * b4:CH * b4 + CH, cols], kq_start[rows, hp, 1, CH * b:CH * b + CH],
                                          state[rows, hp, b, :], start=False, stop=(hq == 3))
                    m.then_inc(by.full.sem, 1)
                    for j in range(2):
                        pe.wait_ge(bd[j].drained.sem, bd[j].drained.at(c, i))
                    settle(c)
                    for b4 in range(GB):
                        part = slice(CH * b4, CH * b4 + CH)
                        if b4 >= 2:
                            pe.wait_ge(row_step, runs.n - (3 - b4))
                        for j in range(2):
                            for h2 in range(2):
                                o = DV * (2 * (b4 // 2) + j)
                                m = pe.matmul(bd[b4 % 2].t[DK * h2:DK * h2 + DK, o:o + DV],
                                              kend_t[part, g, 2 * q + j, DK * h2:DK * h2 + DK],
                                              w[part, 2 * j + h2, :], start=True, stop=True)
                        if b4 < 2:
                            m.then_inc(row_step, runs.next())
                        else:
                            m.then_inc(bd[b4 % 2].full.sem, 1)
                if i % 2 == 0 and i:
                    g = i // 2 - 1
                    pe.wait_ge(yn_ready.sem, yn_ready.at(c, g + 1))
                    for q in range(2):
                        pe.wait_ge(bank_of[f"t{2 * g + q}"].drained.sem, bank_of[f"t{2 * g + q}"].freed(c, f"t{2 * g + q}"))
                        settle(c)
                        for hq in range(4):
                            m = pe.transpose(bm.t[:, P * hq:P * hq + P], ysb[:, g % 2, 4 * q + hq, :], ident[:, :])
                        m.then_inc(bm.full.sem, 1)
                    pe.wait_ge(bank_of[f"t{2 * g + 1}"].drained.sem, bank_of[f"t{2 * g + 1}"].emptied(c, f"t{2 * g + 1}"))
                    pe.wait_ge(bank_of[f"o{g}"].drained.sem, bank_of[f"o{g}"].freed(c, f"o{g}"))
                    settle(c)
                    for hh in range(H):
                        m = pe.matmul(bp.t[:, 0:P], wout[:, hh, :], yt[:, hh, :], start=(hh == 0), stop=(hh == H - 1))
                    m.then_inc(bp.full.sem, 1)

            pe.wait_ge(row_step, runs.n)
            pe.sem_clear(row_step)
        chunks(pe, body)

    @block.vector
    def _(dve):
        dve.wait_ge(s_const, n_const)
        dve.memset(au[R:R + 1, :], 1.0).then_inc(s_zero, 1)
        dve.memset(bsel[:, :, :], 0.0).then_inc(bsel_cleared, 1)
        dve.tensor_scalar(convw[:, :], convw[:, :], 0.5, None, ALU.mult).then_inc(s_zero, 1)
        dve.tensor_scalar(convb[:, :], convb[:, :], 0.5, None, ALU.mult).then_inc(s_zero, 1)
        dve.tensor_scalar(bau[:, :], bau[:, :], 0.5, None, ALU.mult).then_inc(s_zero, 1)
        for hh in range(H):
            i = dve.tensor_scalar(wout[:, hh, :], wout[:, hh, :], w_hn[:, hh:hh + 1], None, ALU.mult)
        i.then_inc(s_zero, 1)
        dve.wait_ge(bsel_cleared, 1)
        halves = ((slice(0, DK), 0), (slice(DK, P), 4))
        for n in range(3):
            if n:
                dve.wait_ge(bsel_step, 4 * n)
            for rows, col in halves:
                dve.tensor_copy(bsel[rows, :, col + n], bspike[rows, :]).then_inc(bsel_step, 1)
            dve.wait_ge(bsel_step, 4 * n + 2)
            for rows, col in halves:
                dve.tensor_tensor(bspike[rows, :], bspike[rows, :], bsel[rows, :, col + n],
                                  ALU.subtract).then_inc(bsel_step, 1)
        dve.wait_ge(bsel_step, 12)
        dve.memset(bsel[0:DK, :, 3], 1.0)
        dve.memset(bsel[DK:P, :, 7], 1.0).then_inc(s_zero, 1)
        dve.wait_ge(s_zero, n_made)

        def values(c, i):
            g, q = i // 2, i % 2
            b = bank_of[f"v{i}"]
            dve.wait_ge(b.full.sem, b.filled(c, f"v{i}"))
            if i:
                dve.wait_ge(bp.drained.sem, bp.emptied(c, f"p{i - 1}"))
            elif later(c):
                dve.wait_ge(bp.drained.sem, bp.emptied(c, f"p{TILES - 1}", 1))
            dve.tensor_tensor(nv[:, :, :].rearrange("p (a h) v -> p a h v", h=2),
                              b.t[:, :].rearrange("p (a h v) -> p a h v", h=2, v=DV),
                              quad(nrm[:, 0, :], g, q).unsqueeze(3).broadcast_to([P, 2, 2, DV]),
                              ALU.mult).then_inc(b.drained.sem, 1)

        def body(c):
            if later(c):
                dve.wait_ge(conv_step.sem, conv_step.at(c, 4, 1))
            if later(c):
                dve.tensor_copy(hn[:, :, 0:3], hn[:, :, CH:CH + 3]).then_inc(halo_ready.sem, 1)
            if later(c):
                dve.wait_ge(halo_ready.sem, halo_ready.at(c, 0))
            dve.wait_ge(rstd_ready.sem, rstd_ready.at(c, 1))
            tok3 = lambda t: t[:, :].rearrange("p (b t) -> p b t", t=CH)
            dve.scalar_tensor_tensor(out=hn[:, :, 3:CH + 3], in0=tok3(xt), scalar=wnorm[:, 0:1], in1=tok3(rstd),
                                     op0=ALU.mult, op1=ALU.mult).then_inc(hn_ready.sem, 1)
            dve.wait_ge(hn_ready.sem, hn_ready.at(c, 1))
            dve.tensor_scalar(cacc[:, :, :], hn[:, :, 0:CH], convw[:, 0:1], convb[:, 0:1], ALU.mult,
                              ALU.add).then_inc(conv_step.sem, 1)
            for k in range(1, 4):
                dve.wait_ge(conv_step.sem, conv_step.at(c, k))
                dve.scalar_tensor_tensor(out=cacc[:, :, :], in0=hn[:, :, k:k + CH], scalar=convw[:, k:k + 1],
                                         in1=cacc[:, :, :], op0=ALU.mult, op1=ALU.add).then_inc(conv_step.sem, 1)
            dve.wait_ge(tz_ready.sem, tz_ready.at(c, 1))
            dve.scalar_tensor_tensor(out=h[:, :], in0=tz[:, :], scalar=1.0,
                                     in1=cacc[:, :, :].rearrange("p b t -> p (b t)"),
                                     op0=ALU.add, op1=ALU.mult).then_inc(h_ready.sem, 1)
            b = bank_of["au"]
            dve.wait_ge(b.full.sem, b.filled(c, "au"))
            dve.tensor_scalar(zau[:, :], b.t[0:R, :], 0.5, bau[:, 0:1], ALU.mult, ALU.add).then_inc(b.drained.sem, 1)
            dve.wait_ge(tau_ready.sem, tau_ready.at(c, 1))
            dve.scalar_tensor_tensor(out=au[0:R, :], in0=tau[:, :], scalar=1.0, in1=zau[:, :],
                                     op0=ALU.add, op1=ALU.mult).then_inc(au_ready.sem, 1)
            for p in range(HP):
                dve.wait_ge(bank_of[f"sd{p}"].drained.sem, bank_of[f"sd{p}"].emptied(c, f"sd{p}"))
            for t in range(CH):
                now = mem[:, :, :, t].rearrange("p a b -> p (a b)")
                last = carry[:, :] if t == 0 else mem[:, :, :, t - 1].rearrange("p a b -> p (a b)")
                if t:
                    dve.wait_ge(rec_step, 2 * t)
                dve.scalar_tensor_tensor(out=residue[:, :], in0=last, scalar=THR2, in1=last,
                                         op0=ALU.is_gt, op1=ALU.subtract).then_inc(rec_step, 1)
                dve.wait_ge(rec_step, 2 * t + 1)
                dve.scalar_tensor_tensor(out=now, in0=residue[:, :], scalar=-DECAY, in1=now,
                                         op0=ALU.mult, op1=ALU.add).then_inc(rec_step, 1)
            dve.wait_ge(rec_step, 2 * CH)
            dve.sem_clear(rec_step)
            dve.tensor_copy(carry[:, :], mem[:, :, :, CH - 1].rearrange("p a b -> p (a b)"))
            dve.tensor_scalar(sp[:, :, :].rearrange("p a n -> p (a n)"),
                              mem[:, :, :, :].rearrange("p a b t -> p (a b t)"), THR2, None,
                              ALU.is_gt).then_inc(sp_ready.sem, 1)
            dve.wait_ge(sp_ready.sem, sp_ready.at(c, 1))

            def alpha_input(p):
                x = mem[:, p, :, :].rearrange("p b t -> p (b t)")
                b = bank_of[f"ab{p}"]
                dve.wait_ge(b.full.sem, b.filled(c, f"ab{p}"))
                dve.scalar_tensor_tensor(out=x, in0=sp[:, p, :], scalar=aspike[:, p:p + 1], in1=b.t[:, :],
                                         op0=ALU.mult, op1=ALU.add).then_inc(b.drained.sem, 1)
                dve.wait_ge(bank_of[f"ab{p}"].drained.sem, bank_of[f"ab{p}"].emptied(c, f"ab{p}"))
                dve.tensor_scalar(x, x, -LMAX, None, ALU.max).then_inc(xa_ready.sem, 1)

            alpha_input(0)
            for p in range(HP):
                if p + 1 < HP:
                    alpha_input(p + 1)
                x = mem[:, p, :, :].rearrange("p b t -> p (b t)")
                b = bank_of[f"cnt{p}"]
                dve.wait_ge(b.full.sem, b.filled(c, f"cnt{p}"))
                dve.wait_ge(e1_ready.sem, e1_ready.at(c, p + 1))
                dve.scalar_tensor_tensor(out=x, in0=b.t[:, :], scalar=0.0, in1=x, op0=ALU.is_gt,
                                         op1=ALU.mult).then_inc(b.drained.sem, 1)
            b = bank_of["beta"]
            dve.wait_ge(b.full.sem, b.filled(c, "beta"))
            dve.tensor_copy(stat[:, :], b.t[:, 0:5 * UN]).then_inc(b.drained.sem, 1)
            dve.wait_ge(bank_of["beta"].drained.sem, bank_of["beta"].emptied(c, "beta"))
            s4 = stat[:, 0:4 * UN].rearrange("p (u n) -> p u n", n=4)
            dve.tensor_reduce(logit[:, :], s4[:, :, 0:3], AX.X, ALU.add).then_inc(small.sem, 1)
            dve.wait_ge(small.sem, small.at(c, 1))
            dve.tensor_tensor(logit[:, :], logit[:, :], stat[:, 4 * UN:5 * UN], ALU.add).then_inc(small.sem, 1)
            dve.wait_ge(small.sem, small.at(c, 2))
            dve.tensor_tensor(logit[:, :], logit[:, :], bbeta[:, :, :, :].rearrange("p a g h -> p (a g h)"),
                              ALU.add).then_inc(small.sem, 1)
            dve.wait_ge(small.sem, small.at(c, 4))
            dve.tensor_scalar(beta[:, :], beta[:, :], 1.0, None, ALU.add).then_inc(small.sem, 1)
            dve.wait_ge(small.sem, small.at(c, 5))
            dve.reciprocal(beta[:, :], beta[:, :]).then_inc(small.sem, 1)
            dve.tensor_scalar(act_n[:, :], s4[:, :, 3], 1.0, None, ALU.min).then_inc(small.sem, 1)
            dve.wait_ge(small.sem, small.at(c, 7))
            dve.tensor_tensor(beta[:, :], beta[:, :], act_n[:, :], ALU.mult).then_inc(small.sem, 1)
            dve.wait_ge(l_ready.sem, l_ready.at(c, 1))
            for p in range(HP):
                x = mem[:, p, :, :].rearrange("p b t -> p (b t)")
                i = dve.tensor_tensor_scan(x, step0[:, :, :].rearrange("p b t -> p (b t)"), x, 0.0, ALU.mult, ALU.add)
            i.then_inc(g_ready.sem, 1)
            for p in range(HP):
                both = lambda t: t[:, :].unsqueeze(1).broadcast_to([P, 2, TOK])
                if p:
                    b = bank_of[f"kend{p - 1}"]
                    dve.wait_ge(b.full.sem, b.filled(c, f"kend{p - 1}"))
                elif later(c):
                    b = bank_of[f"kend{HP - 1}"]
                    dve.wait_ge(b.full.sem, b.filled(c, f"kend{HP - 1}", 1))
                dve.wait_ge(kq_ready.sem, kq_ready.at(c, 2 * p + 2))
                dve.wait_ge(e_ready.sem, e_ready.at(c, p + 1))
                dve.tensor_tensor(kq_leaf[:, :, :], kq[:, :, :], both(eleaf), ALU.mult)
                dve.tensor_tensor(km[:, :], kq[:, 0, :], dleaf[:, :], ALU.mult)
                dve.tensor_tensor(kq_pair[:, :, :], kq[:, :, :], both(dpair), ALU.mult)
                dve.tensor_tensor(kq_blk[:, :, :], kq[:, :, :], both(dblk), ALU.mult)
                dve.tensor_tensor(kend[:, :], kq[:, 0, :], dend[:, :], ALU.mult).then_inc(prod_ready.sem, 1)
                if p == 0:
                    if later(c):
                        dve.wait_ge(by.full.sem, by.full.at(c, TILES, 1))
                dve.tensor_tensor(kq_start[:, p, :, :], kq[:, :, :], both(estart), ALU.mult).then_inc(kstart_ready.sem, 1)
                b = bank_of[f"leaf{p}"]
                dve.wait_ge(b.full.sem, b.filled(c, f"leaf{p}"))
                if p == 0:
                    if later(c):
                        dve.wait_ge(b_stored.sem, b_stored.at(c, 16 * NG, 1))
                dve.tensor_tensor(ab[:, p, :, :, :], b.t[:, :].rearrange("p (m u i) -> p m u i", m=2, u=8),
                                  leafmask[:, :, :].unsqueeze(2).broadcast_to([P, 2, 8, CH]),
                                  ALU.mult).then_inc(b.drained.sem, 1)
                dve.wait_ge(bank_of[f"leaf{p}"].drained.sem, bank_of[f"leaf{p}"].emptied(c, f"leaf{p}"))
                b = bank_of[f"cross{p}"]
                dve.wait_ge(b.full.sem, b.filled(c, f"cross{p}"))
                abp = ab[:, p, :, :, :].rearrange("p m u i -> p (m u) i")
                for n in range(2):
                    o = abp[:, :, BLK * n + LEAF:BLK * n + BLK]
                    dve.scalar_tensor_tensor(
                        out=o, in0=b.t[:, 0:256].rearrange("p (x n i) -> p x n i", n=2, i=LEAF)[:, :, n, :],
                        scalar=rowmask[:, n:n + 1], in1=o, op0=ALU.mult, op1=ALU.add).then_inc(cross_step.sem, 1)
                dve.wait_ge(cross_step.sem, cross_step.at(c, 2 * p + 2))
                dve.scalar_tensor_tensor(
                    out=abp[:, :, BLK:CH], in0=b.t[:, 256:512].rearrange("p (x i) -> p x i", i=BLK),
                    scalar=rowmask[:, 2:3], in1=abp[:, :, BLK:CH], op0=ALU.mult, op1=ALU.add).then_inc(b.drained.sem, 1)
            dve.wait_ge(bank_of[f"cross{HP - 1}"].drained.sem, bank_of[f"cross{HP - 1}"].emptied(c, f"cross{HP - 1}"))
            a4 = ab[:, :, 0, :, :]
            dve.tensor_tensor(a4, a4, eye[:, :].unsqueeze(1).unsqueeze(1).broadcast_to([P, HP, 8, CH]),
                              ALU.add).then_inc(ab_ready.sem, 1)
            b = bank_of["sst"]
            dve.wait_ge(b.full.sem, b.filled(c, "sst"))
            for j in range(2):
                i = dve.tensor_copy(
                    nrm[:, j, :].rearrange("p (a g h) -> p a g h", a=HP, g=NG),
                    b.t[:, 0:64].rearrange("p (g m a h) -> p m a g h", g=NG, m=2, a=HP)[:, j, :, :, :])
            i.then_inc(b.drained.sem, 1)
            dve.wait_ge(small.sem, small.at(c, 10))
            dve.tensor_scalar(nrm[:, :, :], sqn[:, :, :], EPS, None, ALU.add).then_inc(small.sem, 1)
            dve.wait_ge(small.sem, small.at(c, 11))
            dve.reciprocal(inv[:, :, :], nrm[:, :, :]).then_inc(small.sem, 1)
            dve.wait_ge(small.sem, small.at(c, 12))
            dve.tensor_tensor(sqn[:, :, :], inv[:, :, :], inv[:, :, :], ALU.mult).then_inc(small.sem, 1)
            dve.wait_ge(small.sem, small.at(c, 13))
            dve.tensor_tensor(cvec[:, :], beta[:, :], sqn[:, 0, :], ALU.mult).then_inc(small.sem, 1)
            dve.tensor_scalar(q2[:, :], sqn[:, 1, :], 1.0 / DV, None, ALU.mult).then_inc(small.sem, 1)
            dve.wait_ge(ab_ready.sem, ab_ready.at(c, 1))
            if later(c):
                dve.wait_ge(a_stored.sem, a_stored.at(c, 16, 1))
            turned = kq_leaf[:, :, :].rearrange("p m n -> p (m n)")
            for p in range(HP):
                i = dve.transpose(turned[:, 256 * p:256 * p + 256], ab[:, p, 0, :, :].rearrange("p u i -> p (u i)"))
            i.then_inc(ca_step.sem, 1)
            dve.wait_ge(ca_step.sem, ca_step.at(c, 1))
            dve.wait_ge(small.sem, small.at(c, 15))
            for p in range(HP):
                i = dve.tensor_tensor(ca[:, :, 2 * p:2 * p + 2, :],
                                      turned[:, 256 * p:256 * p + 256].rearrange("p (g h j) -> p g h j", g=NG, h=2),
                                      cvec[:, 8 * p:8 * p + 8].rearrange("p (g h) -> p g h", h=2).unsqueeze(3)
                                      .broadcast_to([P, NG, 2, CH]), ALU.mult)
            i.then_inc(ca_step.sem, 1)
            dve.wait_ge(na_loaded.sem, na_loaded.at(c, 64))
            dve.wait_ge(tu_cleared.sem, tu_cleared.at(c, 1))
            diag = lambda t: t[:, :, :].rearrange("p i j -> p (i j)")[:, 0:CH * CH:CH + 1]
            dve.tensor_copy(diag(tu), diag(na)).then_inc(tri_step, 1)
            for j in range(CH - 1):
                n, m = j + 1, CH - 1 - j
                prod = tmp[:, 0:n * m].rearrange("p (c i) -> p c i", i=m)
                dve.wait_ge(tri_step, 2 * j + 1)
                dve.tensor_tensor(prod, tu[:, 0:n, j:j + 1].broadcast_to([P, n, m]),
                                  na[:, j + 1:CH, j].unsqueeze(1).broadcast_to([P, n, m]),
                                  ALU.mult).then_inc(tri_step, 1)
                dve.wait_ge(tri_step, 2 * j + 2)
                i = dve.tensor_tensor(tu[:, 0:n, j + 1:CH], tu[:, 0:n, j + 1:CH], prod, ALU.subtract)
                i.then_inc(tri_step if j < CH - 2 else tri_done.sem, 1)
            dve.wait_ge(tri_step, 2 * CH - 2)
            dve.sem_clear(tri_step)

            values(c, 0)
            for i in range(TILES + 1):
                g, q = i // 2, i % 2
                if i < TILES:
                    if i or later(c):
                        dve.wait_ge(bw.full.sem, bw.full.at(c, i))
                    dve.wait_ge(bank_of[f"v{i}"].drained.sem, bank_of[f"v{i}"].emptied(c, f"v{i}"))
                    dve.wait_ge(bank_of[f"p{i}"].full.sem, bank_of[f"p{i}"].filled(c, f"p{i}"))
                    dve.tensor_tensor(r[:, :, :], nv[:, :, :], bp.t[:, :].rearrange("p (h v) -> p h v", v=DV),
                                      ALU.subtract).then_inc(bp.drained.sem, 1)
                    if i + 1 < TILES:
                        values(c, i + 1)
                if i:
                    n = i - 1
                    for j in range(2):
                        dve.wait_ge(bd[j].full.sem, bd[j].full.at(c, n + 1))
                        for x in range(4):
                            hp, b = 2 * (n % 2) + x % 2, GB * (n // 2) + j + 2 * (x // 2)
                            k = dve.scalar_tensor_tensor(
                                out=state[:, hp, b, :], in0=state[:, hp, b, :], scalar=gam[:, hp, b:b + 1],
                                in1=bd[j].t[:, DV * x:DV * x + DV], op0=ALU.mult, op1=ALU.add)
                        k.then_inc(bd[j].drained.sem, 1)
                    dve.wait_ge(bank_of[f"y{n}"].drained.sem, bank_of[f"y{n}"].emptied(c, f"y{n}"))
                    dve.tensor_reduce(yss[:, 4 * (n % 2):4 * (n % 2) + 4], ysq[:, :, :], AX.X,
                                      ALU.add).then_inc(ysum_step.sem, 1)
                if i and q == 0:
                    g -= 1
                    unit = lambda t: t.rearrange("p (a g h) -> p a g h", g=NG, h=2)[:, :, g, :]
                    by2 = lambda t: t[:, :].rearrange("p (a h) -> p a h", h=2)
                    dve.wait_ge(ysum_step.sem, ysum_step.at(c, 2 * g + 2))
                    dve.tensor_tensor(by2(yss), by2(yss), unit(q2[:, :]), ALU.mult).then_inc(yss_ready.sem, 1)
                    dve.wait_ge(yrs_ready.sem, yrs_ready.at(c, g + 1))
                    dve.tensor_tensor(by2(yr), by2(yr), unit(inv[:, 1, :]), ALU.mult).then_inc(yr_ready.sem, 1)
                    dve.wait_ge(yr_ready.sem, yr_ready.at(c, g + 1))
                    dve.tensor_tensor(ysb[:, g % 2, :, :], ysb[:, g % 2, :, :],
                                      yr[:, :].unsqueeze(2).broadcast_to([P, H, DV]), ALU.mult).then_inc(yn_ready.sem, 1)

        chunks(dve, body)


def feed_forward(nc, a, attn_d, out, ctx, sb, sem):
    wu1, bu1, wu2, bu2 = sb("wu1", [P, R]), sb("bu1", [R, 1]), sb("wu2", [R, D]), sb("bu2", [P, 1])
    wffn = sb("wffn", [P, 1])
    wf1, wf3, wf2 = sb("wf1", [P, FF]), sb("wf3", [P, FF]), sb("wf2", [P, FT, D])
    w1, w2 = sb("w1", [P, E, FF]), sb("w2", [P, E, FT, D])
    b1, b2 = sb("b1", [P, E, FT]), sb("b2", [E, D])
    lng, lnb = sb("lng", [P, E]), sb("lnb", [P, E])
    cent = sb("cent", [P, E])
    iota = sb("iota", [P, NG, E])
    ident = sb("ident2", [P, P])
    meanw = sb("meanw2", [P, P])
    eps_t, ln_eps_t = sb("eps2", [P, 1]), sb("ln_eps", [P, 1])

    x0, at = sb("x0", [P, TOK]), sb("at", [P, TOK])
    zu, tu, u1 = sb("zu", [R, TOK]), sb("tu1", [R, TOK]), sb("u1", [R, TOK])
    gate, sq, y1, h2, rs = (sb(n, [P, TOK]) for n in ("gate", "sq", "y1", "h2", "rs"))
    th, hid = sb("th", [P, 2, TOK]), sb("hid", [P, FT, TOK])
    x1, xl, xh, xf = (sb(n, [P, TOK]) for n in ("x1", "xl", "xh", "xf"))
    hm = sb("hm", [P, 2, FT, TOK])
    acc = sb("acc", [P, NG, D])
    aff, ea, oh, sel = (sb(n, [P, NG, E]) for n in ("aff", "ea", "oh", "sel"))
    top = sb("top", [P, NG])
    sel_t = sb("sel_t", [E, TOK])

    dense = ["u1", "u2", "ms"] + [f"{n}{t}" for t in range(FT) for n in ("f", "g")] + [
        "ff", "m1", "v1", "aff", "m2", "v2", "selt"]
    tail = ["back", "m3", "v3"]
    fills = dense + tail
    psum = [ctx.enter_context(nc.psum_tensor(f"pf{i}", [P, 512], F32)) for i in range(8)]

    def bank(i, name, fills):
        return Bank(psum[i], sem(f"{name}_full"), sem(f"{name}_drained"), fills)

    ring = [bank(i, f"dense{i}", fills[i::3]) for i in range(3)]
    bh = [bank(3 + i, f"hidden{i}", [f"h{e}_{t}" for e in range(E) for t in range(FT) if (FT * e + t) % 3 == i])
          for i in range(3)]
    bo = [bank(6 + i, f"expert{i}", [f"e{e}" for e in range(E) if e % 2 == i]) for i in range(2)]
    bank_of = {f: b for b in ring + bh + bo for f in b.fills}

    sig = lambda name, per: Signal(sem(name), per)
    passed_pe2 = sem("ffn_passed_pe")
    s_const, s_made, s_b1 = sem("ffn_const_loaded"), sem("ffn_made"), sem("b1_folded")
    in_loaded = sig("in_loaded", 32)
    tu_ready, u1_ready = sig("tanh_u_ready", 1), sig("u1_ready", 1)
    gate_ready, gated, y1_ready = sig("gate_ready", 1), sig("gated", 1), sig("y1_ready", 1)
    sq_ready, rs_ready = sig("sq_ready", 4), sig("rs_ready", 4)
    h2_ready, th_ready, hid_ready = sig("h2_ready", 1), sig("th_ready", FT), sig("hid_ready", 2 * FT)
    x1_ready, xc_ready = sig("x1_ready", 2), sig("xc_ready", 3)
    normed = sig("normed", 2)
    route = sig("route_step", 10)
    acc_step = sig("acc_step", E)
    xf_ready, stored = sig("xf_ready", 1), sig("out_stored", 16)

    col = lambda x: x.unsqueeze(1)
    loads = [(wu1[:, :], a["w_u1"]), (bu1[:, :], col(a["b_u1"])), (wu2[:, :], a["w_u2"]), (bu2[:, :], col(a["b_u2"])),
             (wffn[:, :], col(a["w_ffn"])), (wf1[:, :], a["w_ff1"]), (wf3[:, :], a["w_ff3"]),
             (wf2[:, :, :], a["w_ff2"]), (w1[:, :, :], a["w1"]), (w2[:, :, :, :], a["w2"]), (b1[:, :, :], a["b1"]),
             (b2[:, :], a["b2"]), (lng[:, :], a["ln_g"]), (lnb[:, :], a["ln_b"]), (cent[:, :], a["centroids"]),
             (iota[:, :, :], a["iota"]), (ident[:, :], a["ident"])]
    n_const = 16 * len(loads)
    n_made = 6

    block = ctx.enter_context(nc.Block())

    def chunks(eng, body):
        body(0)
        with eng.Fori(1, NC) as c:
            body(c)

    @block.sync
    def _(sp):
        for dst, src in loads:
            sp.dma_start(dst, src).then_inc(s_const, 16)

        def body(c):
            if later(c):
                sp.wait_ge(x1_ready.sem, x1_ready.at(c, 2, 1))
            sp.dma_start(x0[:, :], a["xT"][c]).then_inc(in_loaded.sem, 16)
            sp.dma_start(at[:, :], attn_d[c]).then_inc(in_loaded.sem, 16)
            sp.wait_ge(xf_ready.sem, xf_ready.at(c, 1))
            sp.dma_start(out[c], xf[:, :]).then_inc(stored.sem, 16)

        chunks(sp, body)
        sp.wait_ge(stored.sem, 16 * NC)

    @block.gpsimd
    def _(pool):
        for b in ring + bh + bo:
            pool.sem_inc(b.drained.sem, 1)
        pool.memset(meanw[:, :], 1.0 / D).then_inc(s_made, 1)
        pool.memset(eps_t[:, :], EPS).then_inc(s_made, 1)
        pool.memset(ln_eps_t[:, :], LN_EPS).then_inc(s_made, 1)

    @block.scalar
    def _(act):
        act.wait_ge(s_const, n_const)
        act.wait_ge(s_made, n_made)

        def square(c, n, src):
            act.activation(sq[:, :], src[:, :], ACT.Square).then_inc(sq_ready.sem, 1)

        def rsqrt(c, n, fill, eps):
            b = bank_of[fill]
            act.wait_ge(b.full.sem, b.filled(c, fill))
            act.activation(rs[:, :], b.t[:, :], ACT.Ln, bias=eps[:, 0:1]).then_inc(b.drained.sem, 1)
            act.wait_ge(bank_of[fill].drained.sem, bank_of[fill].emptied(c, fill))
            act.activation(rs[:, :], rs[:, :], ACT.Exp, scale=-0.5).then_inc(rs_ready.sem, 1)

        def body(c):
            act.wait_ge(bank_of["u1"].drained.sem, bank_of["u1"].emptied(c, "u1"))
            act.activation(tu[:, :], zu[:, :], ACT.Tanh).then_inc(tu_ready.sem, 1)
            b = bank_of["u2"]
            act.wait_ge(b.full.sem, b.filled(c, "u2"))
            act.activation(gate[:, :], b.t[:, :], ACT.Tanh, bias=bu2[:, 0:1], scale=0.5).then_inc(b.drained.sem, 1)
            act.wait_ge(y1_ready.sem, y1_ready.at(c, 1))
            square(c, 0, y1)
            rsqrt(c, 0, "ms", eps_t)
            for t in range(FT):
                if t >= 2:
                    act.wait_ge(hid_ready.sem, hid_ready.at(c, 2 * (t - 2) + 1))
                act.wait_ge(bank_of[f"f{t}"].full.sem, bank_of[f"f{t}"].filled(c, f"f{t}"))
                b = bank_of[f"f{t}"]
                act.activation(th[:, t % 2, :], b.t[:, :], ACT.Tanh, scale=0.5).then_inc(th_ready.sem, 1)
            act.wait_ge(xc_ready.sem, xc_ready.at(c, 1))
            square(c, 1, x1)
            rsqrt(c, 1, "v1", ln_eps_t)
            act.wait_ge(xc_ready.sem, xc_ready.at(c, 2))
            square(c, 2, xh)
            act.wait_ge(route.sem, route.at(c, 1))
            act.activation(ea[:, :, :], aff[:, :, :], ACT.Exp, scale=-1.0).then_inc(route.sem, 1)
            rsqrt(c, 2, "v2", ln_eps_t)
            b = bank_of["selt"]
            act.wait_ge(b.full.sem, b.filled(c, "selt"))
            act.activation(sel_t[:, :], b.t[0:E, :], ACT.Copy).then_inc(b.drained.sem, 1)
            for e in range(E):
                for t in range(0, FT, 2):
                    fill = f"h{e}_{t}"
                    b = bank_of[fill]
                    act.wait_ge(b.full.sem, b.filled(c, fill))
                    if e >= 2:
                        act.wait_ge(bo[e % 2].full.sem, bo[e % 2].full.at(c, bo[e % 2].n(f"e{e - 2}") + 1))
                    else:
                        if later(c):
                            act.wait_ge(bo[e % 2].full.sem, bo[e % 2].full.at(c, E // 2, 1))
                    act.activation(hm[:, e % 2, t, :], b.t[:, :], ACT.Relu,
                                   bias=b1[:, e, t:t + 1]).then_inc(b.drained.sem, 1)
            act.wait_ge(xc_ready.sem, xc_ready.at(c, 3))
            square(c, 3, xf)
            rsqrt(c, 3, "v3", ln_eps_t)

        chunks(act, body)

    @block.tensor
    def _(pe):
        pe.wait_ge(s_const, n_const)
        pe.wait_ge(s_made, 3)
        m = None
        for e in range(E):
            for t in range(FT):
                m = pe.matmul(ring[0].t[:, FT * e + t:FT * e + t + 1], w1[:, e, P * t:P * t + P], lnb[:, e:e + 1],
                              start=True, stop=True)
        m.then_inc(s_b1, 1)
        pe.wait_ge(s_made, n_made)

        def settle(c):
            if later(c):
                pe.sem_inc(passed_pe2, 1)

        def mean(c, fill, src, ready, n):
            b = bank_of[fill]
            pe.wait_ge(ready.sem, ready.at(c, n))
            pe.wait_ge(bank_of[fill].drained.sem, bank_of[fill].freed(c, fill))
            settle(c)
            pe.matmul(b.t[:, :], meanw[:, :], src[:, :], start=True, stop=True).then_inc(b.full.sem, 1)

        def body(c):
            pe.wait_ge(in_loaded.sem, in_loaded.at(c, 32))
            pe.wait_ge(bank_of["u1"].drained.sem, bank_of["u1"].freed(c, "u1"))
            settle(c)
            pe.matmul(bank_of["u1"].t[0:R, :], wu1[:, :], x0[:, :], start=True,
                      stop=True).then_inc(bank_of["u1"].full.sem, 1)
            pe.wait_ge(u1_ready.sem, u1_ready.at(c, 1))
            pe.wait_ge(bank_of["u2"].drained.sem, bank_of["u2"].freed(c, "u2"))
            settle(c)
            pe.matmul(bank_of["u2"].t[:, :], wu2[:, :], u1[:, :], start=True,
                      stop=True).then_inc(bank_of["u2"].full.sem, 1)
            mean(c, "ms", sq, sq_ready, 1)
            pe.wait_ge(h2_ready.sem, h2_ready.at(c, 1))
            for t in range(FT):
                for name, wt in (("f", wf1), ("g", wf3)):
                    b = bank_of[f"{name}{t}"]
                    pe.wait_ge(b.drained.sem, b.freed(c, f"{name}{t}"))
                    settle(c)
                    pe.matmul(b.t[:, :], wt[:, P * t:P * t + P], h2[:, :], start=True, stop=True).then_inc(b.full.sem, 1)
            b = bank_of["ff"]
            pe.wait_ge(b.drained.sem, b.freed(c, "ff"))
            for t in range(FT):
                pe.wait_ge(hid_ready.sem, hid_ready.at(c, 2 * t + 2))
                settle(c)
                m = pe.matmul(b.t[:, :], wf2[:, t, :], hid[:, t, :], start=(t == 0), stop=(t == FT - 1))
            m.then_inc(b.full.sem, 1)
            mean(c, "m1", x1, x1_ready, 2)
            mean(c, "v1", sq, sq_ready, 2)
            b = bank_of["aff"]
            pe.wait_ge(normed.sem, normed.at(c, 1))
            pe.wait_ge(bank_of["aff"].drained.sem, bank_of["aff"].freed(c, "aff"))
            settle(c)
            for g in range(NG):
                m = pe.matmul(b.t[:, E * g:E * g + E], xl[:, P * g:P * g + P], cent[:, :], start=True, stop=True)
            m.then_inc(b.full.sem, 1)
            mean(c, "m2", xl, normed, 1)
            mean(c, "v2", sq, sq_ready, 3)
            b = bank_of["selt"]
            pe.wait_ge(route.sem, route.at(c, 10))
            pe.wait_ge(bank_of["selt"].drained.sem, bank_of["selt"].freed(c, "selt"))
            settle(c)
            for g in range(NG):
                m = pe.transpose(b.t[0:E, P * g:P * g + P], sel[:, g, :], ident[:, :])
            m.then_inc(b.full.sem, 1)

            def up(e, t):
                b = bank_of[f"h{e}_{t}"]
                pe.wait_ge(b.drained.sem, b.freed(c, f"h{e}_{t}"))
                settle(c)
                pe.matmul(b.t[:, :], w1[:, e, P * t:P * t + P], xh[:, :], start=True, stop=True).then_inc(b.full.sem, 1)

            pe.wait_ge(normed.sem, normed.at(c, 2))
            for t in range(FT):
                up(0, t)
            for e in range(E):
                if e + 1 < E:
                    for t in range(FT):
                        up(e + 1, t)
                b = bank_of[f"e{e}"]
                for t in range(FT):
                    pe.wait_ge(bank_of[f"h{e}_{t}"].drained.sem, bank_of[f"h{e}_{t}"].emptied(c, f"h{e}_{t}"))
                pe.wait_ge(bank_of[f"e{e}"].drained.sem, bank_of[f"e{e}"].freed(c, f"e{e}"))
                settle(c)
                for g in range(NG):
                    for t in range(FT):
                        m = pe.matmul(b.t[:, D * g:D * g + D], hm[:, e % 2, t, P * g:P * g + P], w2[:, e, t, :],
                                      start=(t == 0), stop=(t == FT - 1))
                m.then_inc(b.full.sem, 1)
            b = bank_of["back"]
            pe.wait_ge(bank_of["selt"].drained.sem, bank_of["selt"].emptied(c, "selt"))
            pe.wait_ge(bank_of["back"].drained.sem, bank_of["back"].freed(c, "back"))
            pe.wait_ge(acc_step.sem, acc_step.at(c, E))
            settle(c)
            pe.matmul(b.t[:, :], b2[:, :], sel_t[:, :], start=True, stop=False)
            for g in range(NG):
                m = pe.matmul(b.t[:, P * g:P * g + P], acc[:, g, :], ident[:, :], start=False, stop=(g == NG - 1))
            m.then_inc(b.full.sem, 1)
            b = bank_of["m3"]
            pe.wait_ge(bank_of["back"].drained.sem, bank_of["back"].emptied(c, "back"))
            pe.wait_ge(bank_of["m3"].drained.sem, bank_of["m3"].freed(c, "m3"))
            settle(c)
            pe.matmul(b.t[:, :], meanw[:, :], xf[:, :], start=True, stop=True).then_inc(b.full.sem, 1)
            mean(c, "v3", sq, sq_ready, 4)

        chunks(pe, body)

    @block.vector
    def _(dve):
        dve.wait_ge(s_const, n_const)
        dve.wait_ge(s_made, 3)
        dve.tensor_scalar(bu1[:, :], bu1[:, :], 0.5, None, ALU.mult)
        dve.tensor_scalar(bu2[:, :], bu2[:, :], 0.5, None, ALU.mult).then_inc(s_made, 1)
        dve.wait_ge(s_b1, 1)
        dve.tensor_tensor(b1[:, :, :].rearrange("p e t -> p (e t)"), b1[:, :, :].rearrange("p e t -> p (e t)"),
                          ring[0].t[:, 0:E * FT], ALU.add).then_inc(s_made, 1)
        for e in range(E):
            i = dve.tensor_scalar(w1[:, e, :], w1[:, e, :], lng[:, e:e + 1], None, ALU.mult)
        i.then_inc(s_made, 1)
        dve.wait_ge(s_made, n_made)

        def center(c, n, fill, src, dst):
            b = bank_of[fill]
            dve.wait_ge(b.full.sem, b.filled(c, fill))
            dve.tensor_tensor(dst[:, :], src[:, :], b.t[:, :], ALU.subtract).then_inc(b.drained.sem, 1)
            dve.wait_ge(bank_of[fill].drained.sem, bank_of[fill].emptied(c, fill))
            dve.sem_inc(xc_ready.sem, 1)

        def body(c):
            b = bank_of["u1"]
            dve.wait_ge(b.full.sem, b.filled(c, "u1"))
            dve.tensor_scalar(zu[:, :], b.t[0:R, :], 0.5, bu1[:, 0:1], ALU.mult, ALU.add).then_inc(b.drained.sem, 1)
            dve.wait_ge(tu_ready.sem, tu_ready.at(c, 1))
            dve.scalar_tensor_tensor(out=u1[:, :], in0=tu[:, :], scalar=1.0, in1=zu[:, :], op0=ALU.add,
                                     op1=ALU.mult).then_inc(u1_ready.sem, 1)
            dve.wait_ge(in_loaded.sem, in_loaded.at(c, 32))
            dve.wait_ge(bank_of["u2"].drained.sem, bank_of["u2"].emptied(c, "u2"))
            dve.scalar_tensor_tensor(out=gate[:, :], in0=gate[:, :], scalar=1.0, in1=at[:, :], op0=ALU.add,
                                     op1=ALU.mult).then_inc(gated.sem, 1)
            dve.wait_ge(gated.sem, gated.at(c, 1))
            dve.scalar_tensor_tensor(out=y1[:, :], in0=gate[:, :], scalar=0.5, in1=x0[:, :], op0=ALU.mult,
                                     op1=ALU.add).then_inc(y1_ready.sem, 1)
            dve.wait_ge(rs_ready.sem, rs_ready.at(c, 1))
            dve.scalar_tensor_tensor(out=h2[:, :], in0=y1[:, :], scalar=wffn[:, 0:1], in1=rs[:, :], op0=ALU.mult,
                                     op1=ALU.mult).then_inc(h2_ready.sem, 1)
            for t in range(FT):
                b = bank_of[f"f{t}"]
                dve.wait_ge(th_ready.sem, th_ready.at(c, t + 1))
                dve.scalar_tensor_tensor(out=hid[:, t, :], in0=th[:, t % 2, :], scalar=1.0, in1=b.t[:, :],
                                         op0=ALU.add, op1=ALU.mult).then_inc(b.drained.sem, 1)
                dve.wait_ge(bank_of[f"f{t}"].drained.sem, bank_of[f"f{t}"].emptied(c, f"f{t}"))
                dve.sem_inc(hid_ready.sem, 1)
                b = bank_of[f"g{t}"]
                dve.wait_ge(b.full.sem, b.filled(c, f"g{t}"))
                dve.tensor_tensor(hid[:, t, :], hid[:, t, :], b.t[:, :], ALU.mult).then_inc(b.drained.sem, 1)
                dve.wait_ge(bank_of[f"g{t}"].drained.sem, bank_of[f"g{t}"].emptied(c, f"g{t}"))
                dve.sem_inc(hid_ready.sem, 1)
            b = bank_of["ff"]
            dve.wait_ge(b.full.sem, b.filled(c, "ff"))
            dve.scalar_tensor_tensor(out=x1[:, :], in0=b.t[:, :], scalar=0.5, in1=y1[:, :], op0=ALU.mult,
                                     op1=ALU.add).then_inc(b.drained.sem, 1)
            dve.wait_ge(bank_of["ff"].drained.sem, bank_of["ff"].emptied(c, "ff"))
            dve.sem_inc(x1_ready.sem, 1)
            dve.tensor_tensor(x1[:, :], x1[:, :], x0[:, :], ALU.add).then_inc(x1_ready.sem, 1)
            dve.wait_ge(x1_ready.sem, x1_ready.at(c, 2))
            center(c, 1, "m1", x1, x1)
            dve.wait_ge(rs_ready.sem, rs_ready.at(c, 2))
            dve.tensor_tensor(xl[:, :], x1[:, :], rs[:, :], ALU.mult).then_inc(normed.sem, 1)
            b = bank_of["aff"]
            dve.wait_ge(b.full.sem, b.filled(c, "aff"))
            dve.tensor_copy(aff[:, :, :].rearrange("p g e -> p (g e)"), b.t[:, 0:NG * E]).then_inc(b.drained.sem, 1)
            dve.wait_ge(bank_of["aff"].drained.sem, bank_of["aff"].emptied(c, "aff"))
            dve.sem_inc(route.sem, 1)
            dve.wait_ge(normed.sem, normed.at(c, 1))
            center(c, 2, "m2", xl, xh)
            wide = lambda t: t[:, :].unsqueeze(2).broadcast_to([P, NG, E])
            dve.wait_ge(route.sem, route.at(c, 2))
            dve.tensor_reduce(top[:, :], aff[:, :, :], AX.X, ALU.max).then_inc(route.sem, 1)
            dve.wait_ge(route.sem, route.at(c, 3))
            dve.tensor_tensor(oh[:, :, :], aff[:, :, :], wide(top), ALU.is_lt).then_inc(route.sem, 1)
            dve.wait_ge(route.sem, route.at(c, 4))
            dve.scalar_tensor_tensor(out=oh[:, :, :], in0=oh[:, :, :], scalar=float(2 * E), in1=iota[:, :, :],
                                     op0=ALU.mult, op1=ALU.add).then_inc(route.sem, 1)
            dve.wait_ge(route.sem, route.at(c, 5))
            dve.tensor_reduce(top[:, :], oh[:, :, :], AX.X, ALU.min).then_inc(route.sem, 1)
            dve.wait_ge(route.sem, route.at(c, 6))
            dve.tensor_tensor(oh[:, :, :], iota[:, :, :], wide(top), ALU.is_equal).then_inc(route.sem, 1)
            dve.tensor_scalar(ea[:, :, :], ea[:, :, :], 1.0, None, ALU.add).then_inc(route.sem, 1)
            dve.wait_ge(route.sem, route.at(c, 8))
            dve.reciprocal(ea[:, :, :], ea[:, :, :]).then_inc(route.sem, 1)
            dve.wait_ge(route.sem, route.at(c, 9))
            dve.tensor_tensor(sel[:, :, :], oh[:, :, :], ea[:, :, :], ALU.mult).then_inc(route.sem, 1)
            dve.wait_ge(rs_ready.sem, rs_ready.at(c, 3))
            dve.tensor_tensor(xh[:, :], xh[:, :], rs[:, :], ALU.mult).then_inc(normed.sem, 1)
            dve.wait_ge(route.sem, route.at(c, 10))

            def gather(e):
                b = bank_of[f"e{e}"]
                dve.wait_ge(b.full.sem, b.filled(c, f"e{e}"))
                if e:
                    dve.wait_ge(acc_step.sem, acc_step.at(c, e))
                for g in range(NG):
                    if e:
                        i = dve.scalar_tensor_tensor(out=acc[:, g, :], in0=b.t[:, D * g:D * g + D],
                                                     scalar=sel[:, g, e:e + 1], in1=acc[:, g, :],
                                                     op0=ALU.mult, op1=ALU.add)
                    else:
                        i = dve.tensor_scalar(acc[:, g, :], b.t[:, D * g:D * g + D], sel[:, g, e:e + 1], None,
                                              ALU.mult)
                i.then_inc(b.drained.sem, 1)
                dve.wait_ge(bank_of[f"e{e}"].drained.sem, bank_of[f"e{e}"].emptied(c, f"e{e}"))
                dve.sem_inc(acc_step.sem, 1)

            for e in range(E):
                for t in range(1, FT, 2):
                    fill = f"h{e}_{t}"
                    b = bank_of[fill]
                    dve.wait_ge(b.full.sem, b.filled(c, fill))
                    if e >= 2:
                        dve.wait_ge(bo[e % 2].full.sem, bo[e % 2].full.at(c, bo[e % 2].n(f"e{e - 2}") + 1))
                    else:
                        if later(c):
                            dve.wait_ge(bo[e % 2].full.sem, bo[e % 2].full.at(c, E // 2, 1))
                    dve.tensor_scalar(hm[:, e % 2, t, :], b.t[:, :], b1[:, e, t:t + 1], 0.0, ALU.add,
                                      ALU.max).then_inc(b.drained.sem, 1)
                if e:
                    gather(e - 1)
            gather(E - 1)
            b = bank_of["back"]
            dve.wait_ge(b.full.sem, b.filled(c, "back"))
            if later(c):
                dve.wait_ge(stored.sem, stored.at(c, 16, 1))
            dve.scalar_tensor_tensor(out=xf[:, :], in0=xl[:, :], scalar=2.0, in1=b.t[:, :], op0=ALU.mult,
                                     op1=ALU.add).then_inc(b.drained.sem, 1)
            dve.wait_ge(bank_of["back"].drained.sem, bank_of["back"].emptied(c, "back"))
            center(c, 3, "m3", xf, xf)
            dve.wait_ge(rs_ready.sem, rs_ready.at(c, 4))
            dve.tensor_tensor(xf[:, :], xf[:, :], rs[:, :], ALU.mult).then_inc(xf_ready.sem, 1)

        chunks(dve, body)


def _layouts(i):
    import numpy as np
    n = {k[3:]: np.asarray(v) for k, v in i.items()}
    g = {k.split("_", 1)[1]: v for k, v in n.items()}
    con = np.ascontiguousarray
    pairs = lambda x: con(x.reshape(HP, P).T)
    t = {
        "xT": con(g["x"].reshape(NB, NC, CH, D).transpose(1, 3, 0, 2).reshape(NC, D, TOK)),
        "alpha_spike": pairs(g["alpha_spike"]), "beta_spike": pairs(g["beta_spike"]),
        "w_hn": con(g["w_hn"].T), "w_out": con(g["w_out"].reshape(H, DV, D).transpose(1, 0, 2)),
        "w_ff2": con(g["w_ff2"].reshape(FT, P, D).transpose(1, 0, 2)),
        "w1": con(g["w1"].transpose(2, 0, 1)),
        "w2": con(g["w2"].reshape(E, D, FT, P).transpose(3, 0, 2, 1)),
        "b1": con(g["b1"].reshape(E, FT, P).transpose(2, 0, 1)), "b2": g["b2"],
        "ln_g": con(g["ln_g"].T), "ln_b": con(g["ln_b"].T), "centroids": con(g["centroids"].T),
    }
    for k in ("w_norm_in", "conv_w", "conv_b", "wq", "wk", "wv", "w_spike", "w_au", "b_au", "w_ad", "b_ad", "w_beta",
              "b_beta", "w_u1", "b_u1", "w_u2", "b_u2", "w_ffn", "w_ff1", "w_ff3"):
        t[k] = con(g[k])
    j, i_ = np.arange(P) % CH, np.arange(CH)
    leaf = (j[:, None] // LEAF) == (i_[None] // LEAF)
    t["leafmask"] = np.stack([leaf & (j[:, None] < i_), leaf & (j[:, None] <= i_)], 1).astype(np.float32)
    t["rowmask"] = np.stack([j // LEAF == 0, j // LEAF == 2, j < BLK], 1).astype(np.float32)
    t["eye"] = (j[:, None] == i_).astype(np.float32)
    t["ident"] = np.eye(P, dtype=np.float32)
    head = np.arange(P) // DK
    t["sumblk"] = (head[:, None] == head).astype(np.float32)
    ind = np.zeros((P, 2, HP, 16), np.float32)
    for m in range(2):
        for p in range(HP):
            ind[np.arange(P), m, p, 8 * m + 2 * p + head] = 1.0
    t["headind"] = ind
    t["iota"] = np.broadcast_to(np.arange(E, dtype=np.float32), (P, NG, E)).copy()
    return t


def kernel(**inputs):
    import numpy as np
    import concourse.bacc as bacc
    from concourse.bass_utils import run_bass_kernel_spmd as run

    nc = bacc.Bacc("TRN2", target_bir_lowering=False, num_devices=1)
    arrays = _layouts(inputs)
    args = {k: nc.dram_tensor(f"in_{k}", v.shape, mybir.dt.from_np(v.dtype), kind="ExternalInput").ap()
            for k, v in arrays.items()}
    out = nc.dram_tensor("out", (NC, P, TOK), F32, kind="ExternalOutput").ap()
    build(nc, args, out)
    r = run(nc, [{f"in_{k}": v for k, v in arrays.items()}], core_ids=[0])
    got = r.results[0]["out"]
    return np.ascontiguousarray(got.reshape(NC, D, NB, CH).transpose(2, 0, 3, 1).reshape(NB, NT, D))
```

```python
from contextlib import ExitStack

import concourse.bass as bass
from concourse import mybir

F32 = mybir.dt.float32
BF16 = mybir.dt.bfloat16
ALU = mybir.AluOpType
ACT = mybir.ActivationFunctionType
AX = mybir.AxisListType

P = 128
NB, NT, D = 16, 256, 128
H, DK, DV = 8, 64, 128
HP = H // 2
CH = 32
NC = NT // CH
TOK = NB * CH
NG = TOK // P
GB = P // CH
UN = HP * NG * 2
R = 64
FF = 512
FT = FF // P
E = 8
LEAF, BLK = 8, 16
THR2 = 1.0
DECAY = 0.9
EPS = 1e-6
LN_EPS = 1e-5
TINY = 1e-18
LMAX = 20.0
TILES = 2 * NG
EXP_LOG_SET = 6
STEPS = HP + 3
PACES = 2 + CH // 4
KEEP_WARM = 3
WARM = (2, 1, 0)


class Signal:

    def __init__(self, sem, per, start=0):
        self.sem, self.per, self.start = sem, per, start

    def at(self, c, n, back=0):
        return c.loop * self.per + (n + self.start + (c.plus - back) * self.per)


class Bank:

    def __init__(self, tensor, full, drained, fills):
        self.t, self.fills = tensor, list(fills)
        self.full = Signal(full, len(self.fills))
        self.drained = Signal(drained, len(self.fills), 1)

    def filled(self, c, fill, back=0):
        return self.full.at(c, self.fills.index(fill) + 1, back)

    def emptied(self, c, fill, back=0):
        return self.drained.at(c, self.fills.index(fill) + 1, back)

    def freed(self, c, fill):
        return self.drained.at(c, self.fills.index(fill))

    def n(self, fill):
        return self.fills.index(fill)


class Count:

    def __init__(self):
        self.n = 0

    def next(self):
        self.n += 1
        return 1


class Chunk:

    def __init__(self, loop, plus=0):
        self.loop, self.plus = loop, plus

    def next(self):
        return Chunk(self.loop, self.plus + 1)


def looped(c):
    return not isinstance(c.loop, int)


def later(c):
    return looped(c) or c.plus > 0


def load_exp_log_table(nc, act):
    act.add_instruction(mybir.InstLoadActFuncSet(name=nc.get_next_instruction_name(), act_func_set_id=EXP_LOG_SET,
                                                 engine=act.engine, ins=[], outs=[]))


def build(nc, a, out):
    top = ExitStack()
    with top:
        sem = lambda name: top.enter_context(nc.semaphore(name))
        ctx = ExitStack()
        sb = lambda name, shape, dt=F32: ctx.enter_context(nc.sbuf_tensor(name, shape, dt))
        attn_d = nc.dram_tensor("attn_d", (NC, P, TOK), F32, kind="Internal").ap()
        with ctx:
            attention(nc, a, attn_d, ctx, sb, sem)
        ctx = ExitStack()
        sb = lambda name, shape, dt=F32: ctx.enter_context(nc.sbuf_tensor(name, shape, dt))
        with ctx:
            feed_forward(nc, a, attn_d, out, ctx, sb, sem)


def attention(nc, a, attn_d, ctx, sb, sem):
    a_d = nc.dram_tensor("a_d", (GB, CH, UN, CH), F32, kind="Internal").ap()
    b_d = nc.dram_tensor("b_d", (GB, CH, NG, H, CH), F32, kind="Internal").ap()
    u_d = nc.dram_tensor("u_d", (GB, NG, H, CH, CH), F32, kind="Internal").ap()

    wq, wk, wsd = sb("wq", [P, H * DK]), sb("wk", [P, H * DK]), sb("wsd", [P, H * DK])
    wad = sb("wad", [R + 1, H * DK])
    wv = sb("wv", [P, H * DV])
    wout = sb("wout", [P, H, D])
    w_hn = sb("w_hn", [P, H])
    wau = sb("wau", [P, R])
    wbeta = sb("wbeta", [P, H])
    bbeta = sb("bbeta", [P, HP, NG, 2])
    wnorm, convw, convb = sb("wnorm", [P, 1]), sb("convw", [P, 4]), sb("convb", [P, 1])
    bau = sb("bau", [R, 1])
    aspike, bspike = sb("aspike", [P, HP]), sb("bspike", [P, HP])
    bsrest = sb("bsrest", [P, HP])
    bsel = sb("bsel", [P, HP, 8], BF16)
    ident = sb("ident", [P, P])
    eye = sb("eye", [P, CH])
    leafmask = sb("leafmask", [P, 2, CH])
    rowmask = sb("rowmask", [P, 3])
    headind = sb("headind", [P, 2, HP, 16])
    meanw = sb("meanw", [P, P])
    sumblk = sb("sumblk", [P, P], BF16)
    sumblk_f = sb("sumblk_f", [P, P])
    step0 = sb("step0", [P, NB, CH])
    eps_t, tiny_t = sb("eps_t", [P, 1]), sb("tiny_t", [P, 1])

    xt, xsq = sb("xt", [P, TOK]), sb("xsq", [P, TOK])
    rstd = xsq
    hn = sb("hn", [P, NB, CH + 3])
    cacc, tz = xt[:, :].rearrange("p (b t) -> p b t", t=CH), sb("tz", [P, TOK])
    h, hv = sb("h", [P, TOK]), sb("hv", [P, TOK])
    zau, au = sb("zau", [R, TOK]), sb("au", [R + 1, TOK])
    tau = tz[0:R, :]
    mem = sb("mem", [P, HP, NB, CH])
    carry, residue = sb("carry", [P, HP * NB]), sb("residue", [P, HP * NB])
    sp = sb("sp", [P, HP, NB * CH], BF16)
    yt = sb("yt", [P, 8, P])
    kq, kqsq = sb("kq", [P, 2, 2, TOK]), yt[:, :, :].rearrange("p (m u) t -> p m (u t)", m=2)
    ss_row = sb("ss_row", [16, TOK])
    dend, dleaf, dpair, dblk, eleaf = (sb(x, [P, 2, TOK]) for x in ("dend", "dleaf", "dpair", "dblk", "eleaf"))
    gam = sb("gam", [P, HP, NB])
    kq_leaf, kq_pair, kq_blk = (sb(x, [P, 2, TOK]) for x in ("kq_leaf", "kq_pair", "kq_blk"))
    km, kend = sb("km", [P, TOK]), sb("kend", [P, TOK])
    kq_start = sb("kq_start", [P, HP, 2, TOK])
    kend_t = sb("kend_t", [P, NG, HP, P])
    ab = sb("ab", [P, HP, 2, 8, CH])
    ca = kq_pair[:, :, :].rearrange("p m n -> p (m n)")
    na = kq_blk[:, :, :].rearrange("p m (i j) -> p (m i) j", j=CH)
    tu = kq[:, 0, :, :].rearrange("p m (i j) -> p (m i) j", j=CH)
    tmp = sb("tmp", [P, CH * CH // 4])
    stat = sb("stat", [P, UN * 4 + UN])
    logit, beta = sb("logit", [P, UN]), sb("beta", [P, UN])
    act_n, nrm, inv = sb("act_n", [P, UN]), sb("nrm", [P, 2, UN]), sb("inv", [P, 2, UN])
    sqn = sb("sqn", [P, 2, UN])
    cvec, q2 = sb("cvec", [P, UN]), sb("q2", [P, UN])
    state = sb("state", [P, HP, NB, DV])
    ub, bb = sb("ub", [P, 2, 8, P]), sb("bb", [P, 2, 8, P])
    nv, r, w = sb("nv", [P, 4, DV]), sb("r", [P, 4, DV]), sb("w", [P, 4, DV])
    ysb, ysq = sb("ysb", [P, 2, 8, DV]), sb("ysq", [P, 4, DV])
    yss, yr = sb("yss", [P, H]), sb("yr", [P, H])
    kx = sb("kx", [P, 2, GB, P])
    attn = sb("attn", [P, TOK])

    psum = [ctx.enter_context(nc.psum_tensor(f"ps{i}", [P, 512], F32)) for i in range(8)]

    def bank(i, name, fills):
        return Bank(psum[i], sem(f"{name}_full"), sem(f"{name}_drained"), fills)

    front = ["ms", "au", "sd0", "sd1", "sd2", "sd3"] + [f"{n}{p}" for p in range(HP) for n in ("ab", "cnt")] + ["beta"]
    front_banks = [bank(0, "front0", front[0::2]), bank(1, "front1", front[1::2])]
    of_pairs = lambda name: [f"{name}{p}" for p in range(HP)]
    of_tiles = lambda name: [f"{name}{i}" for i in range(TILES)]
    predictions, values_turned = ["p0"], ["ss", "sst", "v0"]
    for i in range(TILES + 1):
        if i + 1 < TILES:
            predictions.append(f"p{i + 1}")
            values_turned.append(f"v{i + 1}")
        if i % 2 == 0 and i:
            predictions.append(f"o{i // 2 - 1}")
            values_turned += [f"t{i - 2}", f"t{i - 1}"]
    bp = bank(2, "pred", of_pairs("kend") + predictions)
    bw = bank(3, "write", of_pairs("q") + of_tiles("w"))
    by = bank(4, "read", of_pairs("k") + of_tiles("y"))
    bv = bank(5, "value", values_turned)
    bd = [bank(6 + j, f"delta{j}", of_pairs(("leaf", "cross")[j]) + of_tiles("d")) for j in range(2)]
    main_banks = [bp, bw, by, bv] + bd
    bank_of = {f: b for b in front_banks + main_banks for f in b.fills if f[0] != "d"}

    sig = lambda name, per: Signal(sem(name), per)
    passed_pe, passed_pool, passed_sp = sem("passed_pe"), sem("passed_pool"), sem("passed_sp")
    s_const, s_zero = sem("const_loaded"), sem("constants_made")
    x_loaded = sig("x_loaded", 16)
    xsq_ready, rstd_ready = sig("xsq_ready", 1), sig("rstd_ready", 1)
    halo_ready, hn_ready, conv_step = sig("halo_ready", 1), sig("hn_ready", 1), sig("conv_step", 4)
    tz_ready, h_ready = sig("tz_ready", 1), sig("h_ready", 1)
    tau_ready, au_ready = sig("tau_ready", 1), sig("au_ready", 1)
    rec_step = sem("rec_step")
    sp_ready = sig("sp_ready", 1)
    xa_ready, e1_ready = sig("xa_ready", HP), sig("e1_ready", HP)
    l_ready, g_ready, hv_ready = sig("l_ready", 1), sig("g_ready", 1), sig("hv_ready", 1)
    d_ready, e_ready, dleaf_read = sig("d_ready", HP), sig("e_ready", HP), sig("dleaf_read", HP)
    kq_ready, kqsq_used = sig("kq_ready", 2 * HP), sig("kqsq_used", 2 * HP - 1)
    leaf_ready, cross_ready, kend_ready = sig("leaf_ready", HP), sig("cross_ready", HP), sig("kend_ready", HP)
    cross_step = sig("cross_step", 2 * HP)
    bsel_cleared, bsel_step = sem("bsel_cleared"), sem("bsel_step")
    row_step = sem("row_step")
    pace, kx_ready = sig("pace", PACES), sig("kx_ready", TILES)
    beta_step, norm_step = sig("beta_step", 8), sig("norm_step", 7)
    ab_ready, ca_step = sig("ab_ready", 1), sig("ca_step", 2)
    a_stored, b_stored, na_loaded = sig("a_stored", 16), sig("b_stored", 16 * NG), sig("na_loaded", 64)
    tu_cleared, tri_step, tri_done = sig("tu_cleared", 1), sem("tri_step"), sig("tri_done", 1)
    u_stored = sig("u_stored", 16)
    ub_loaded = [sig(f"ub_loaded{j}", 128) for j in range(2)]
    bb_loaded = [sig(f"bb_loaded{j}", 128) for j in range(2)]
    yss_ready, ylog, yrs_ready = sig("yss_ready", NG), sig("ylog", NG), sig("yrs_ready", NG)
    ysum_step, yn_ready = sig("ysum_step", TILES), sig("yn_ready", NG)
    yr_ready = sig("yr_ready", NG)
    attn_stored = sig("attn_stored", 16)

    loads = [
        (wq[:, :], a["wq"]), (wk[:, :], a["wk"]), (wsd[:, :], a["w_spike"]), (wad[0:R, :], a["w_ad"]),
        (wad[R:R + 1, :], a["b_ad"].unsqueeze(0)), (wv[:, :], a["wv"]), (wout[:, :, :], a["w_out"]),
        (w_hn[:, :], a["w_hn"]), (wau[:, :], a["w_au"]), (wbeta[:, :], a["w_beta"]),
        (wnorm[:, :], a["w_norm_in"].unsqueeze(1)), (convw[:, :], a["conv_w"]), (convb[:, :], a["conv_b"].unsqueeze(1)),
        (bau[:, :], a["b_au"].unsqueeze(1)), (aspike[:, :], a["alpha_spike"]), (bspike[:, :], a["beta_spike"]),
        (ident[:, :], a["ident"]), (eye[:, :], a["eye"]), (leafmask[:, :, :], a["leafmask"]),
        (rowmask[:, :], a["rowmask"]), (headind[:, :, :, :], a["headind"]), (sumblk_f[:, :], a["sumblk"]),
    ]
    for g in range(NG):
        loads.append((bbeta[:, :, g, :], a["b_beta"].rearrange("(p h) -> p h", h=2).unsqueeze(0).broadcast_to([P, HP, 2])))
    n_const = 16 * len(loads)
    n_made = 18

    def quad(t, g, q):
        return t.rearrange("p (a g h) -> p a g h", g=NG, h=2)[:, 2 * q:2 * q + 2, g, :]

    block = ctx.enter_context(nc.Block())

    def iterations(eng, first, body):
        first(Chunk(0))
        body(Chunk(0), Chunk(0, 1))
        with eng.Fori(1, NC - 1) as c:
            body(Chunk(c), Chunk(c, 1))
        body(Chunk(0, NC - 1), None)

    @block.sync
    def _(sp_e):
        for dst, src in loads:
            sp_e.dma_start(dst, src).then_inc(s_const, 16)

        def settle(c):
            if looped(c):
                sp_e.sem_inc(passed_sp, 1)

        def body(c, nxt):
            sp_e.wait_ge(ab_ready.sem, ab_ready.at(c, 1))
            settle(c)
            if later(c):
                for j in range(2):
                    sp_e.wait_ge(bb_loaded[j].sem, bb_loaded[j].at(c, 128, 1))
            for g in range(NG):
                sp_e.dma_start(b_d[:, :, g, :, :].rearrange("b j (a h) i -> (b j) a (h i)", h=2),
                               ab[:, :, 1, 2 * g:2 * g + 2, :].rearrange("p a h i -> p a (h i)")
                               ).then_inc(b_stored.sem, 16)
            sp_e.wait_ge(ca_step.sem, ca_step.at(c, 2))
            settle(c)
            if later(c):
                sp_e.wait_ge(na_loaded.sem, na_loaded.at(c, 64, 1))
            sp_e.dma_start(a_d.rearrange("b i u j -> (b i) (u j)"), ca).then_inc(a_stored.sem, 16)
            sp_e.wait_ge(a_stored.sem, a_stored.at(c, 16))
            settle(c)
            if later(c):
                sp_e.wait_ge(tri_done.sem, tri_done.at(c, 1, 1))
            for b4 in range(GB):
                sp_e.dma_start(na[CH * b4:CH * b4 + CH, :, :],
                               a_d[b4].rearrange("i u j -> u i j")).then_inc(na_loaded.sem, 16)
            sp_e.wait_ge(tri_done.sem, tri_done.at(c, 1))
            if later(c):
                for j in range(2):
                    sp_e.wait_ge(ub_loaded[j].sem, ub_loaded[j].at(c, 128, 1))
            sp_e.dma_start(u_d.rearrange("b g h c i -> (b g h) (c i)"),
                           tu.rearrange("p c i -> p (c i)")).then_inc(u_stored.sem, 16)
            sp_e.wait_ge(u_stored.sem, u_stored.at(c, 16))
            settle(c)
            sp_e.wait_ge(b_stored.sem, b_stored.at(c, 16 * NG))
            for g in range(NG):
                if g >= 2:
                    sp_e.wait_ge(by.full.sem, by.filled(c, f"y{2 * (g - 2) + 1}"))
                elif later(c):
                    sp_e.wait_ge(by.full.sem, by.filled(c, f"y{TILES - 3 + 2 * g}", 1))
                for buf, dram, loaded in ((ub, u_d, ub_loaded), (bb, b_d, bb_loaded)):
                    for b4 in range(GB):
                        rows, cols = slice(CH * b4, CH * b4 + CH), slice(CH * b4, CH * b4 + CH)
                        src = dram[b4, g].rearrange("h c i -> c h i") if dram is u_d else dram[b4, :, g]
                        sp_e.dma_start(buf[rows, g % 2, :, cols], src).then_inc(loaded[g % 2].sem, 16)
            sp_e.wait_ge(bp.drained.sem, bp.emptied(c, f"o{NG - 1}"))
            sp_e.dma_start(attn_d[c.plus:][c.loop], attn[:, :]).then_inc(attn_stored.sem, 16)

        iterations(sp_e, lambda c: None, body)
        sp_e.wait_ge(attn_stored.sem, 16 * NC)

    @block.gpsimd
    def _(pool):
        for b in front_banks + main_banks:
            pool.sem_inc(b.drained.sem, 1)
        pool.memset(hn[:, :, :], 0.0).then_inc(s_zero, 1)
        pool.memset(state[:, :, :, :], 0.0).then_inc(s_zero, 1)
        pool.memset(carry[:, :], 0.0).then_inc(s_zero, 1)
        pool.memset(kx[:, :, :, :], 0.0).then_inc(s_zero, 1)
        pool.memset(ub[:, :, :, :], 0.0).then_inc(s_zero, 1)
        pool.memset(bb[:, :, :, :], 0.0).then_inc(s_zero, 1)
        pool.memset(meanw[:, :], 1.0 / D).then_inc(s_zero, 1)
        pool.memset(eps_t[:, :], EPS).then_inc(s_zero, 1)
        pool.memset(tiny_t[:, :], TINY).then_inc(s_zero, 1)
        pool.memset(step0[:, :, 1:CH], 1.0).then_inc(s_zero, 1)
        pool.memset(step0[:, :, 0:1], 0.0).then_inc(s_zero, 1)

        def settle(c):
            if looped(c):
                pool.sem_inc(passed_pool, 1)

        def load_x(c):
            if later(c):
                pool.wait_ge(h_ready.sem, h_ready.at(c, 1, 1))
            settle(c)
            pool.dma_start(xt[:, :], a["xT"][c.plus:][c.loop]).then_inc(x_loaded.sem, 16)

        def body(c, nxt):
            if nxt:
                load_x(nxt)
            for p in range(HP):
                if p == 0:
                    pool.wait_ge(g_ready.sem, g_ready.at(c, 1))
                    if later(c):
                        pool.wait_ge(kx_ready.sem, kx_ready.at(c, TILES, 1))
                if p >= 2 or later(c):
                    pool.wait_ge(kend_ready.sem, kend_ready.at(c, p - 1))
                settle(c)
                g3 = mem[:, p, :, :].rearrange("p b t -> p (b t)")
                for dst, span, anchor in ((dleaf, LEAF, LEAF // 2 - 1), (dpair, BLK, LEAF - 1),
                                          (dblk, CH, BLK - 1), (dend, CH, CH - 1)):
                    v = g3.rearrange("p (n t) -> p n t", t=span)
                    i = pool.tensor_tensor(dst[:, p % 2, :].rearrange("p (n t) -> p n t", t=span), v,
                                           v[:, :, anchor:anchor + 1].broadcast_to([P, TOK // span, span]),
                                           ALU.subtract)
                i.then_inc(d_ready.sem, 1)
                if p == 1:
                    if later(c):
                        pool.wait_ge(bv.full.sem, bv.filled(c, f"v{TILES - 1}", 1))
                    pool.wait_ge(h_ready.sem, h_ready.at(c, 1))
                    settle(c)
                    pool.tensor_copy(hv[:, :], h[:, :]).then_inc(hv_ready.sem, 1)
            pool.wait_ge(kend_ready.sem, kend_ready.at(c, HP))
            settle(c)
            pool.memset(tu, 0.0).then_inc(tu_cleared.sem, 1)
            for i in range(TILES):
                g, q = i // 2, i % 2
                if i == 0:
                    pool.wait_ge(bp.drained.sem, bp.emptied(c, f"kend{HP - 1}"))
                    pool.wait_ge(tu_cleared.sem, tu_cleared.at(c, 1))
                for j in range(2):
                    if i:
                        pool.wait_ge(bd[j].full.sem, bd[j].filled(c, f"d{i - 1}"))
                    elif later(c):
                        pool.wait_ge(bd[j].full.sem, bd[j].filled(c, f"d{TILES - 1}", 1))
                settle(c)
                for b4 in range(GB):
                    part = slice(CH * b4, CH * b4 + CH)
                    m = pool.tensor_copy(kx[part, :, b4, :], kend_t[part, g, 2 * q:2 * q + 2, :])
                m.then_inc(kx_ready.sem, 1)

        pool.wait_ge(s_zero, n_made)
        iterations(pool, load_x, body)

    @block.scalar
    def _(act):
        act.wait_ge(s_const, n_const)
        act.activation(sumblk[:, :], sumblk_f[:, :], ACT.Copy).then_inc(s_zero, 1)
        act.wait_ge(s_zero, n_made)
        load_exp_log_table(nc, act)

        def square_x(f):
            if later(f):
                act.wait_ge(hn_ready.sem, hn_ready.at(f, 1, 1))
            act.wait_ge(x_loaded.sem, x_loaded.at(f, 16))
            act.activation(xsq[:, :], xt[:, :], ACT.Square).then_inc(xsq_ready.sem, 1)

        def rsqrt_x(f):
            b = bank_of["ms"]
            act.wait_ge(b.full.sem, b.filled(f, "ms"))
            act.activation(rstd[:, :], b.t[:, :], ACT.Ln, bias=eps_t[:, 0:1]).then_inc(b.drained.sem, 1)
            act.wait_ge(b.drained.sem, b.emptied(f, "ms"))
            act.activation(rstd[:, :], rstd[:, :], ACT.Exp, scale=-0.5).then_inc(rstd_ready.sem, 1)

        def tokens(f):
            act.wait_ge(conv_step.sem, conv_step.at(f, 4))
            if later(f):
                act.wait_ge(au_ready.sem, au_ready.at(f, 1, 1))
            act.activation(tz[:, :], cacc.rearrange("p b t -> p (b t)"), ACT.Tanh).then_inc(tz_ready.sem, 1)
            b = bank_of["au"]
            act.wait_ge(b.drained.sem, b.emptied(f, "au"))
            act.activation(tau, zau[:, :], ACT.Tanh).then_inc(tau_ready.sem, 1)
            if later(f):
                act.wait_ge(kend_ready.sem, kend_ready.at(f, HP, 1))
            for p in range(HP):
                b = bank_of[f"sd{p}"]
                act.wait_ge(b.full.sem, b.filled(f, f"sd{p}"))
                act.activation(mem[:, p, :, :].rearrange("p b t -> p (b t)"), b.t[:, :], ACT.Copy,
                               scale=2.0).then_inc(b.drained.sem, 1)

        def decays(f, step):
            if step < 3:
                for p in ((0,), (1, 2), (3,))[step]:
                    x = mem[:, p, :, :].rearrange("p b t -> p (b t)")
                    act.wait_ge(xa_ready.sem, xa_ready.at(f, p + 1))
                    act.activation(x, x, ACT.Exp, scale=-1.0).then_inc(e1_ready.sem, 1)
            if step == 5:
                b = bank_of[f"cnt{HP - 1}"]
                act.wait_ge(b.drained.sem, b.emptied(f, f"cnt{HP - 1}"))
                x = mem[:, :, :, :].rearrange("p a b t -> p (a b t)")
                act.activation(x, x, ACT.Ln, bias=1.0).then_inc(l_ready.sem, 1)
                act.wait_ge(beta_step.sem, beta_step.at(f, 3))
                act.activation(beta[:, :], logit[:, :], ACT.Exp, scale=-1.0).then_inc(beta_step.sem, 1)

        def keys(c, p):
            s = p % 2
            if p >= 2 or later(c):
                act.wait_ge(kend_ready.sem, kend_ready.at(c, p - 1))
            if p == 0 and later(c):
                act.wait_ge(u_stored.sem, u_stored.at(c, 16, 1))
            for j, name in ((0, "k"), (1, "q")):
                b = bank_of[f"{name}{p}"]
                act.wait_ge(b.full.sem, b.filled(c, f"{name}{p}"))
                act.activation(kq[:, s, j, :], b.t[:, :], ACT.Copy).then_inc(kq_ready.sem, 1)
                if p:
                    act.wait_ge(kqsq_used.sem, kqsq_used.at(c, 2 * p + j - 1))
                act.activation(kqsq[:, j, :], b.t[:, :], ACT.Square).then_inc(b.drained.sem, 1)

        def factors(c, p):
            s = p % 2
            act.wait_ge(d_ready.sem, d_ready.at(c, p + 1))
            g3 = mem[:, p, :, :].rearrange("p b t -> p (b t)")
            act.activation(g3, g3, ACT.Exp, scale=-1.0)
            act.activation(eleaf[:, s, :], dleaf[:, s, :], ACT.Exp, scale=-1.0).then_inc(dleaf_read.sem, 1)
            for t, span in ((dpair, BLK), (dblk, CH)):
                v = t[:, s, :].rearrange("p (n t) -> p n t", t=span)
                act.activation(v[:, :, 0:span // 2], v[:, :, 0:span // 2], ACT.Exp)
                act.activation(v[:, :, span // 2:span], v[:, :, span // 2:span], ACT.Exp, scale=-1.0)
            act.activation(dend[:, s, :], dend[:, s, :], ACT.Exp)
            act.wait_ge(dleaf_read.sem, dleaf_read.at(c, p + 1))
            act.activation(dleaf[:, s, :], dleaf[:, s, :], ACT.Exp).then_inc(e_ready.sem, 1)

        def body(c, nxt):
            keys(c, 0)
            factors(c, 0)
            for p in range(HP):
                if p + 1 < HP:
                    keys(c, p + 1)
                    factors(c, p + 1)
                b = bank_of[f"kend{p}"]
                act.wait_ge(b.full.sem, b.filled(c, f"kend{p}"))
                if p == 0 and later(c):
                    act.wait_ge(kx_ready.sem, kx_ready.at(c, TILES, 1))
                act.activation(kend_t[:, :, p, :], b.t[:, :].rearrange("p (g k) -> p g k", g=NG),
                               ACT.Copy).then_inc(b.drained.sem, 1)
                if nxt and p == 0:
                    square_x(nxt)
                if nxt and p == 1:
                    rsqrt_x(nxt)
            act.wait_ge(bv.full.sem, bv.filled(c, "ss"))
            act.activation(ss_row[:, :], bv.t[0:16, :], ACT.Copy).then_inc(bv.drained.sem, 1)
            b = bank_of["sst"]
            act.wait_ge(b.drained.sem, b.emptied(c, "sst"))
            act.activation(sqn[:, :, :], nrm[:, :, :], ACT.Ln, bias=tiny_t[:, 0:1]).then_inc(norm_step.sem, 1)
            act.wait_ge(norm_step.sem, norm_step.at(c, 1))
            act.activation(sqn[:, :, :], sqn[:, :, :], ACT.Exp, scale=0.5).then_inc(norm_step.sem, 1)
            if nxt:
                tokens(nxt)
                load_exp_log_table(nc, act)
                decays(nxt, 0)
            for i in range(TILES + 1):
                if i < TILES:
                    act.wait_ge(bw.full.sem, bw.filled(c, f"w{i}"))
                    if i:
                        act.wait_ge(bd[1].full.sem, bd[1].filled(c, f"d{i - 1}"))
                    act.activation(w[:, :, :].rearrange("p h v -> p (h v)"), bw.t[:, :],
                                   ACT.Copy).then_inc(bw.drained.sem, 1)
                if i % 2 == 0 and i:
                    g = i // 2 - 1
                    act.wait_ge(yss_ready.sem, yss_ready.at(c, g + 1))
                    act.activation(yr[:, :], yss[:, :], ACT.Ln, bias=eps_t[:, 0:1]).then_inc(ylog.sem, 1)
                    act.wait_ge(ylog.sem, ylog.at(c, g + 1))
                    act.activation(yr[:, :], yr[:, :], ACT.Exp, scale=-0.5).then_inc(yrs_ready.sem, 1)
                if i < TILES:
                    g, q = i // 2, i % 2
                    act.wait_ge(by.full.sem, by.filled(c, f"y{i}"))
                    if i:
                        act.wait_ge(ysum_step.sem, ysum_step.at(c, i))
                    ytile = by.t[:, :].rearrange("p (h v) -> p h v", v=DV)
                    act.activation(ysb[:, g % 2, 4 * q:4 * q + 4, :], ytile, ACT.Copy)
                    act.activation(ysq[:, :, :], ytile, ACT.Square).then_inc(by.drained.sem, 1)
                if nxt and i + 1 < STEPS:
                    decays(nxt, i + 1)
                if i % 2 == 0 and i:
                    g = i // 2 - 1
                    for q in range(2):
                        b = bank_of[f"t{2 * g + q}"]
                        act.wait_ge(b.full.sem, b.filled(c, f"t{2 * g + q}"))
                        act.activation(yt[:, 4 * q:4 * q + 4, :].rearrange("p h t -> p (h t)"), b.t[:, :],
                                       ACT.Copy).then_inc(b.drained.sem, 1)
                    act.wait_ge(bp.full.sem, bp.filled(c, f"o{g}"))
                    if g == 0 and later(c):
                        act.wait_ge(attn_stored.sem, attn_stored.at(c, 16, 1))
                    act.activation(attn[:, P * g:P * g + P], bp.t[:, 0:P], ACT.Copy).then_inc(bp.drained.sem, 1)

        def first(c):
            square_x(c)
            rsqrt_x(c)
            tokens(c)
            load_exp_log_table(nc, act)
            for step in range(STEPS):
                decays(c, step)

        iterations(act, first, body)

    @block.tensor
    def _(pe):
        pe.wait_ge(s_const, n_const)
        pe.wait_ge(s_zero, n_made)

        def settle(c):
            if looped(c):
                pe.sem_inc(passed_pe, 1)

        def mean_square(f):
            b = bank_of["ms"]
            pe.wait_ge(b.drained.sem, b.freed(f, "ms"))
            pe.wait_ge(xsq_ready.sem, xsq_ready.at(f, 1))
            settle(f)
            pe.matmul(b.t[:, :], meanw[:, :], xsq[:, :], start=True, stop=True).then_inc(b.full.sem, 1)

        def tokens(f):
            b = bank_of["au"]
            pe.wait_ge(h_ready.sem, h_ready.at(f, 1))
            pe.wait_ge(b.drained.sem, b.freed(f, "au"))
            settle(f)
            pe.matmul(b.t[0:R, :], wau[:, :], h[:, :], start=True, stop=True).then_inc(b.full.sem, 1)
            for p in range(HP):
                b = bank_of[f"sd{p}"]
                pe.wait_ge(b.drained.sem, b.freed(f, f"sd{p}"))
                settle(f)
                pe.matmul(b.t[:, :], wsd[:, P * p:P * p + P], h[:, :], start=True, stop=True).then_inc(b.full.sem, 1)

        def decays(f, step):
            for p in ((0, 1), (2,), (3,), (), (), ())[step] if step < HP + 2 else ():
                b = bank_of[f"ab{p}"]
                if p == 0:
                    pe.wait_ge(au_ready.sem, au_ready.at(f, 1))
                pe.wait_ge(b.drained.sem, b.freed(f, f"ab{p}"))
                settle(f)
                pe.matmul(b.t[:, :], wad[:, P * p:P * p + P], au[:, :], start=True, stop=True).then_inc(b.full.sem, 1)
            for p in ((0,), (), (1,), (2,), (3,), ())[step] if step < HP + 2 else ():
                b = bank_of[f"cnt{p}"]
                if p == 0:
                    pe.wait_ge(sp_ready.sem, sp_ready.at(f, 1))
                pe.wait_ge(b.drained.sem, b.freed(f, f"cnt{p}"))
                settle(f)
                pe.matmul(b.t[:, :], sumblk[:, :], sp[:, p, :], start=True, stop=True).then_inc(b.full.sem, 1)
            if step == HP + 1:
                b = bank_of["beta"]
                pe.wait_ge(b.drained.sem, b.freed(f, "beta"))
                settle(f)
                units = b.t[:, 0:4 * UN].rearrange("p (a g n) -> p a g n", a=HP, g=NG)
                lin = b.t[:, 4 * UN:5 * UN].rearrange("p (a g h) -> p a g h", a=HP, g=NG)
                for g in range(NG):
                    for p in range(HP):
                        pe.matmul(units[:, p, g, :], sp[:, p, P * g:P * g + P], bsel[:, p, :], start=True, stop=True)
                for g in range(NG):
                    m = pe.matmul(lin[:, :, g, :], h[:, P * g:P * g + P],
                                  wbeta[:, :].rearrange("p (a h) -> p a h", h=2), start=True, stop=True)
                m.then_inc(b.full.sem, 1)

        def keys(c, p):
            for name, wt in (("k", wk), ("q", wq)):
                b = bank_of[f"{name}{p}"]
                pe.wait_ge(b.drained.sem, b.freed(c, f"{name}{p}"))
                settle(c)
                pe.matmul(b.t[:, :], wt[:, P * p:P * p + P], h[:, :], start=True, stop=True).then_inc(b.full.sem, 1)

        def squares(c, p):
            for j, name in enumerate("kq"):
                first, last = p == 0 and j == 0, p == HP - 1 and j == 1
                b = bank_of[f"{name}{p}"]
                pe.wait_ge(b.drained.sem, b.emptied(c, f"{name}{p}"))
                if first:
                    pe.wait_ge(bv.drained.sem, bv.freed(c, "ss"))
                settle(c)
                pe.matmul(bv.t[0:16, :], headind[:, j, p, :], kqsq[:, j, :], start=first,
                          stop=last).then_inc(bv.full.sem if last else kqsq_used.sem, 1)

        def leaves(c, p, runs):
            leaf, cross = bank_of[f"leaf{p}"], bank_of[f"cross{p}"]
            o = leaf.t[:, :].rearrange("p (m u i) -> p m u i", m=2, u=8)
            o1 = cross.t[:, 0:256].rearrange("p (m u n i) -> p m u n i", m=2, u=8, n=2)
            o2 = cross.t[:, 256:512].rearrange("p (m u i) -> p m u i", m=2, u=8)
            pe.wait_ge(leaf_ready.sem, leaf_ready.at(c, p + 1))
            pe.wait_ge(leaf.drained.sem, leaf.freed(c, f"leaf{p}"))
            settle(c)
            for h2 in range(2):
                rows = slice(DK * h2, DK * h2 + DK)
                if h2:
                    pe.wait_ge(row_step, runs.n)
                for g in range(NG):
                    for b4 in range(GB):
                        t = CH * (GB * g + b4)
                        m = pe.matmul(o[CH * b4:CH * b4 + CH, :, 2 * g + h2, :], km[rows, t:t + CH],
                                      kq_leaf[rows, :, t:t + CH], start=True, stop=True)
                if h2:
                    m.then_inc(leaf.full.sem, 1)
                else:
                    m.then_inc(row_step, runs.next())
            pe.wait_ge(cross_ready.sem, cross_ready.at(c, p + 1))
            pe.wait_ge(cross.drained.sem, cross.freed(c, f"cross{p}"))
            settle(c)
            for h2 in range(2):
                rows = slice(DK * h2, DK * h2 + DK)
                if h2:
                    pe.wait_ge(row_step, runs.n)
                for g in range(NG):
                    for b4 in range(GB):
                        t, u = CH * (GB * g + b4), 2 * g + h2
                        part = slice(CH * b4, CH * b4 + CH)
                        second = kq_pair[rows, :, t:t + CH].rearrange("p m (n i) -> p m n i", i=BLK)[:, :, :, LEAF:BLK]
                        pe.matmul(o1[part, :, u, :, :], kq_pair[rows, 0, t:t + CH], second, start=True, stop=True)
                        m = pe.matmul(o2[part, :, u, :], kq_blk[rows, 0, t:t + CH], kq_blk[rows, :, t + BLK:t + CH],
                                      start=True, stop=True)
                if h2:
                    m.then_inc(cross.full.sem, 1)
                else:
                    m.then_inc(row_step, runs.next())

        def predict(c, i, runs):
            g, q = i // 2, i % 2
            pe.wait_ge(bp.drained.sem, bp.freed(c, f"p{i}"))
            if i == 0:
                pe.wait_ge(kend_ready.sem, kend_ready.at(c, HP))
            if later(c):
                for j in range(2):
                    pe.wait_ge(bd[j].drained.sem, bd[j].emptied(c, f"d{i}", 1))
            settle(c)
            for hq in (0, 2, 1, 3):
                hp, h2 = 2 * q + hq // 2, hq % 2
                rows = slice(DK * h2, DK * h2 + DK)
                if hq == 1:
                    m.then_inc(row_step, runs.next())
                    pe.wait_ge(row_step, runs.n)
                for b4 in range(GB):
                    b = GB * g + b4
                    m = pe.matmul(bp.t[CH * b4:CH * b4 + CH, DV * hq:DV * hq + DV],
                                  kq_start[rows, hp, 0, CH * b:CH * b + CH], state[rows, hp, b, :],
                                  start=True, stop=True)
            m.then_inc(bp.full.sem, 1)

        def values(c, i):
            g, q = i // 2, i % 2
            if i == 0:
                pe.wait_ge(hv_ready.sem, hv_ready.at(c, 1))
            pe.wait_ge(bv.drained.sem, bv.freed(c, f"v{i}"))
            settle(c)
            pe.matmul(bv.t[:, :], hv[:, P * g:P * g + P], wv[:, 512 * q:512 * q + 512],
                      start=True, stop=True).then_inc(bv.full.sem, 1)

        def body(c, nxt):
            runs = Count()
            keys(c, 0)
            squares(c, 0)
            for p in range(HP):
                if p + 1 < HP:
                    keys(c, p + 1)
                leaves(c, p, runs)
                if p + 1 < HP:
                    squares(c, p + 1)
                b = bank_of[f"kend{p}"]
                pe.wait_ge(kend_ready.sem, kend_ready.at(c, p + 1))
                pe.wait_ge(b.drained.sem, b.freed(c, f"kend{p}"))
                settle(c)
                for g in range(NG):
                    m = pe.transpose(b.t[:, P * g:P * g + P], kend[:, P * g:P * g + P], ident[:, :])
                m.then_inc(b.full.sem, 1)
                if nxt and p == 0:
                    mean_square(nxt)
            pe.wait_ge(bv.drained.sem, bv.emptied(c, "ss"))
            settle(c)
            for g in range(NG):
                m = pe.transpose(bv.t[:, 16 * g:16 * g + 16], ss_row[:, P * g:P * g + P], ident[0:16, 0:16])
            m.then_inc(bv.full.sem, 1)
            values(c, 0)
            predict(c, 0, runs)
            if nxt:
                tokens(nxt)
            for j in range(2):
                pe.wait_ge(bd[j].drained.sem, bd[j].freed(c, "d0"))
            for n in range(PACES):
                pe.wait_ge(pace.sem, pace.at(c, n + 1))
                settle(c)
                for k in range(KEEP_WARM):
                    pe.matmul(bd[k % 2].t[:, :], ident[:, :], wv[:, 0:512], start=True, stop=True)
            if nxt:
                decays(nxt, 0)
            for i in range(TILES + 1):
                g, q = i // 2, i % 2
                if i < TILES:
                    if i + 1 < TILES:
                        values(c, i + 1)
                    if nxt and i + 1 < STEPS:
                        decays(nxt, i + 1)
                    if i == 0:
                        for k in range(WARM[0]):
                            pe.matmul(bd[k % 2].t[:, :], ident[:, :], wv[:, 0:512], start=True, stop=True)
                    pe.wait_ge(bp.drained.sem, bp.emptied(c, f"p{i}"))
                    if q == 0:
                        pe.wait_ge(ub_loaded[g % 2].sem, ub_loaded[g % 2].at(c, 64 * (g // 2) + 64))
                    pe.wait_ge(bw.drained.sem, bw.freed(c, f"w{i}"))
                    settle(c)
                    for hq in range(4):
                        m = pe.matmul(bw.t[:, DV * hq:DV * hq + DV], ub[:, g % 2, 4 * q + hq, :], r[:, hq, :],
                                      start=True, stop=True)
                    m.then_inc(bw.full.sem, 1)
                    if i == 0:
                        for k in range(WARM[1]):
                            pe.matmul(bd[k % 2].t[:, :], ident[:, :], wv[:, 0:512], start=True, stop=True)
                    if i + 1 < TILES:
                        predict(c, i + 1, runs)
                    if i == 0:
                        for k in range(WARM[2]):
                            pe.matmul(bd[k % 2].t[:, :], ident[:, :], wv[:, 0:512], start=True, stop=True)
                    pe.wait_ge(bw.drained.sem, bw.emptied(c, f"w{i}"))
                    if q == 0:
                        pe.wait_ge(bb_loaded[g % 2].sem, bb_loaded[g % 2].at(c, 64 * (g // 2) + 64))
                    pe.wait_ge(by.drained.sem, by.freed(c, f"y{i}"))
                    settle(c)
                    for hq in range(4):
                        cols = slice(DV * hq, DV * hq + DV)
                        m = pe.matmul(by.t[:, cols], bb[:, g % 2, 4 * q + hq, :], w[:, hq, :], start=(hq == 0),
                                      stop=False)
                    m.then_inc(row_step, runs.next())
                    pe.wait_ge(row_step, runs.n)
                    for hq in (0, 2, 1, 3):
                        hp, rows = 2 * q + hq // 2, slice(DK * (hq % 2), DK * (hq % 2) + DK)
                        cols = slice(DV * hq, DV * hq + DV)
                        if hq == 1:
                            m.then_inc(row_step, runs.next())
                            pe.wait_ge(row_step, runs.n)
                        for b4 in range(GB):
                            b = GB * g + b4
                            m = pe.matmul(by.t[CH * b4:CH * b4 + CH, cols], kq_start[rows, hp, 1, CH * b:CH * b + CH],
                                          state[rows, hp, b, :], start=False, stop=(hq == 3))
                    m.then_inc(by.full.sem, 1)
                    for j in range(2):
                        pe.wait_ge(bd[j].drained.sem, bd[j].freed(c, f"d{i}"))
                    pe.wait_ge(kx_ready.sem, kx_ready.at(c, i + 1))
                    settle(c)
                    for b4 in range(GB):
                        for j in range(2):
                            for h2 in range(2):
                                o = DV * (2 * (b4 // 2) + j)
                                m = pe.matmul(bd[b4 % 2].t[DK * h2:DK * h2 + DK, o:o + DV],
                                              kx[:, j, b4, DK * h2:DK * h2 + DK], w[:, 2 * j + h2, :],
                                              start=True, stop=True)
                        if b4 >= 2:
                            m.then_inc(bd[b4 % 2].full.sem, 1)
                if i % 2 == 0 and i:
                    g = i // 2 - 1
                    pe.wait_ge(yn_ready.sem, yn_ready.at(c, g + 1))
                    for q in range(2):
                        pe.wait_ge(bv.drained.sem, bv.freed(c, f"t{2 * g + q}"))
                        settle(c)
                        for hq in range(4):
                            m = pe.transpose(bv.t[:, P * hq:P * hq + P], ysb[:, g % 2, 4 * q + hq, :], ident[:, :])
                        m.then_inc(bv.full.sem, 1)
                    pe.wait_ge(bv.drained.sem, bv.emptied(c, f"t{2 * g + 1}"))
                    pe.wait_ge(bp.drained.sem, bp.freed(c, f"o{g}"))
                    settle(c)
                    for hh in range(H):
                        m = pe.matmul(bp.t[:, 0:P], wout[:, hh, :], yt[:, hh, :], start=(hh == 0), stop=(hh == H - 1))
                    m.then_inc(bp.full.sem, 1)
            pe.wait_ge(row_step, runs.n)
            pe.sem_clear(row_step)

        def first(c):
            mean_square(c)
            tokens(c)
            for step in range(STEPS):
                decays(c, step)

        iterations(pe, first, body)

    @block.vector
    def _(dve):
        dve.wait_ge(s_const, n_const)
        dve.memset(au[R:R + 1, :], 1.0).then_inc(s_zero, 1)
        dve.memset(bsel[:, :, :], 0.0).then_inc(bsel_cleared, 1)
        dve.tensor_scalar(convw[:, :], convw[:, :], 0.5, None, ALU.mult).then_inc(s_zero, 1)
        dve.tensor_scalar(convb[:, :], convb[:, :], 0.5, None, ALU.mult).then_inc(s_zero, 1)
        dve.tensor_scalar(bau[:, :], bau[:, :], 0.5, None, ALU.mult).then_inc(s_zero, 1)
        for hh in range(H):
            i = dve.tensor_scalar(wout[:, hh, :], wout[:, hh, :], w_hn[:, hh:hh + 1], None, ALU.mult)
        i.then_inc(s_zero, 1)
        dve.wait_ge(bsel_cleared, 1)
        halves = ((slice(0, DK), 0), (slice(DK, P), 4))
        for n in range(3):
            if n:
                dve.wait_ge(bsel_step, 4 * n)
            for rows, col in halves:
                dve.tensor_copy(bsel[rows, :, col + n], bspike[rows, :]).then_inc(bsel_step, 1)
            dve.wait_ge(bsel_step, 4 * n + 2)
            for rows, col in halves:
                dve.tensor_tensor(bspike[rows, :], bspike[rows, :], bsel[rows, :, col + n],
                                  ALU.subtract).then_inc(bsel_step, 1)
        dve.wait_ge(bsel_step, 12)
        dve.memset(bsel[0:DK, :, 3], 1.0)
        dve.memset(bsel[DK:P, :, 7], 1.0).then_inc(s_zero, 1)
        dve.wait_ge(s_zero, n_made)

        def convolve(f):
            if later(f):
                dve.wait_ge(conv_step.sem, conv_step.at(f, 4, 1))
                dve.tensor_copy(hn[:, :, 0:3], hn[:, :, CH:CH + 3]).then_inc(halo_ready.sem, 1)
                dve.wait_ge(halo_ready.sem, halo_ready.at(f, 0))
                dve.wait_ge(h_ready.sem, h_ready.at(f, 1, 1))
            dve.wait_ge(rstd_ready.sem, rstd_ready.at(f, 1))
            tok3 = lambda t: t[:, :].rearrange("p (b t) -> p b t", t=CH)
            dve.scalar_tensor_tensor(out=hn[:, :, 3:CH + 3], in0=tok3(xt), scalar=wnorm[:, 0:1], in1=tok3(rstd),
                                     op0=ALU.mult, op1=ALU.mult).then_inc(hn_ready.sem, 1)
            dve.wait_ge(hn_ready.sem, hn_ready.at(f, 1))
            dve.tensor_scalar(cacc, hn[:, :, 0:CH], convw[:, 0:1], convb[:, 0:1], ALU.mult,
                              ALU.add).then_inc(conv_step.sem, 1)
            for k in range(1, 4):
                dve.wait_ge(conv_step.sem, conv_step.at(f, k))
                dve.scalar_tensor_tensor(out=cacc, in0=hn[:, :, k:k + CH], scalar=convw[:, k:k + 1],
                                         in1=cacc, op0=ALU.mult, op1=ALU.add).then_inc(conv_step.sem, 1)

        def silus(f):
            dve.wait_ge(tz_ready.sem, tz_ready.at(f, 1))
            if later(f):
                dve.wait_ge(hv_ready.sem, hv_ready.at(f, 1, 1))
                b = bank_of[f"q{HP - 1}"]
                dve.wait_ge(b.full.sem, b.filled(f, f"q{HP - 1}", 1))
            dve.scalar_tensor_tensor(out=h[:, :], in0=tz[:, :], scalar=1.0,
                                     in1=cacc.rearrange("p b t -> p (b t)"),
                                     op0=ALU.add, op1=ALU.mult).then_inc(h_ready.sem, 1)
            b = bank_of["au"]
            dve.wait_ge(b.full.sem, b.filled(f, "au"))
            dve.tensor_scalar(zau[:, :], b.t[0:R, :], 0.5, bau[:, 0:1], ALU.mult, ALU.add).then_inc(b.drained.sem, 1)
            dve.wait_ge(tau_ready.sem, tau_ready.at(f, 1))
            dve.scalar_tensor_tensor(out=au[0:R, :], in0=tau, scalar=1.0, in1=zau[:, :],
                                     op0=ALU.add, op1=ALU.mult).then_inc(au_ready.sem, 1)
            for p in range(HP):
                b = bank_of[f"sd{p}"]
                dve.wait_ge(b.drained.sem, b.emptied(f, f"sd{p}"))

        def membrane(n):
            t = n // 2
            now = mem[:, :, :, t].rearrange("p a b -> p (a b)")
            last = carry[:, :] if t == 0 else mem[:, :, :, t - 1].rearrange("p a b -> p (a b)")
            if n:
                dve.wait_ge(rec_step, n)
            if n % 2 == 0:
                dve.scalar_tensor_tensor(out=residue[:, :], in0=last, scalar=THR2, in1=last,
                                         op0=ALU.is_gt, op1=ALU.subtract).then_inc(rec_step, 1)
            else:
                dve.scalar_tensor_tensor(out=now, in0=residue[:, :], scalar=-DECAY, in1=now,
                                         op0=ALU.mult, op1=ALU.add).then_inc(rec_step, 1)

        def alpha_input(f, p):
            x = mem[:, p, :, :].rearrange("p b t -> p (b t)")
            b = bank_of[f"ab{p}"]
            dve.wait_ge(b.full.sem, b.filled(f, f"ab{p}"))
            dve.scalar_tensor_tensor(out=x, in0=sp[:, p, :], scalar=aspike[:, p:p + 1], in1=b.t[:, :],
                                     op0=ALU.mult, op1=ALU.add).then_inc(b.drained.sem, 1)
            dve.wait_ge(b.drained.sem, b.emptied(f, f"ab{p}"))
            dve.tensor_scalar(x, x, -LMAX, None, ALU.max).then_inc(xa_ready.sem, 1)

        def decays(f, step):
            if step == 0:
                dve.wait_ge(rec_step, 2 * CH)
                dve.sem_clear(rec_step)
                dve.tensor_copy(carry[:, :], mem[:, :, :, CH - 1].rearrange("p a b -> p (a b)"))
                dve.tensor_scalar(sp[:, :, :].rearrange("p a n -> p (a n)"),
                                  mem[:, :, :, :].rearrange("p a b t -> p (a b t)"), THR2, None,
                                  ALU.is_gt).then_inc(sp_ready.sem, 1)
                dve.wait_ge(sp_ready.sem, sp_ready.at(f, 1))
                alpha_input(f, 0)
                alpha_input(f, 1)
            if 1 <= step <= HP:
                p = step - 1
                if p + 2 < HP:
                    alpha_input(f, p + 2)
                x = mem[:, p, :, :].rearrange("p b t -> p (b t)")
                b = bank_of[f"cnt{p}"]
                dve.wait_ge(b.full.sem, b.filled(f, f"cnt{p}"))
                dve.wait_ge(e1_ready.sem, e1_ready.at(f, p + 1))
                dve.scalar_tensor_tensor(out=x, in0=b.t[:, :], scalar=0.0, in1=x, op0=ALU.is_gt,
                                         op1=ALU.mult).then_inc(b.drained.sem, 1)
            s4 = stat[:, 0:4 * UN].rearrange("p (u n) -> p u n", n=4)
            if step == HP + 1:
                b = bank_of["beta"]
                dve.wait_ge(b.full.sem, b.filled(f, "beta"))
                dve.tensor_copy(stat[:, :], b.t[:, 0:5 * UN]).then_inc(b.drained.sem, 1)
                dve.wait_ge(b.drained.sem, b.emptied(f, "beta"))
                dve.tensor_reduce(logit[:, :], s4[:, :, 0:3], AX.X, ALU.add).then_inc(beta_step.sem, 1)
                dve.wait_ge(beta_step.sem, beta_step.at(f, 1))
                dve.tensor_tensor(logit[:, :], logit[:, :], stat[:, 4 * UN:5 * UN], ALU.add).then_inc(beta_step.sem, 1)
                dve.wait_ge(beta_step.sem, beta_step.at(f, 2))
                dve.tensor_tensor(logit[:, :], logit[:, :], bbeta[:, :, :, :].rearrange("p a g h -> p (a g h)"),
                                  ALU.add).then_inc(beta_step.sem, 1)
            if step == HP + 2:
                dve.wait_ge(beta_step.sem, beta_step.at(f, 4))
                dve.tensor_scalar(beta[:, :], beta[:, :], 1.0, None, ALU.add).then_inc(beta_step.sem, 1)
                dve.wait_ge(beta_step.sem, beta_step.at(f, 5))
                dve.reciprocal(beta[:, :], beta[:, :]).then_inc(beta_step.sem, 1)
                dve.tensor_scalar(act_n[:, :], s4[:, :, 3], 1.0, None, ALU.min).then_inc(beta_step.sem, 1)
                dve.wait_ge(beta_step.sem, beta_step.at(f, 7))
                dve.tensor_tensor(beta[:, :], beta[:, :], act_n[:, :], ALU.mult).then_inc(beta_step.sem, 1)
                dve.wait_ge(l_ready.sem, l_ready.at(f, 1))
                for p in range(HP):
                    x = mem[:, p, :, :].rearrange("p b t -> p (b t)")
                    i = dve.tensor_tensor_scan(x, step0[:, :, :].rearrange("p b t -> p (b t)"), x, 0.0, ALU.mult,
                                               ALU.add)
                i.then_inc(g_ready.sem, 1)

        def leaf_products(c, p):
            s = p % 2
            both = lambda t: t.unsqueeze(1).broadcast_to([P, 2, TOK])
            dve.wait_ge(kq_ready.sem, kq_ready.at(c, 2 * p + 2))
            dve.wait_ge(e_ready.sem, e_ready.at(c, p + 1))
            if p:
                b = bank_of[f"leaf{p - 1}"]
                dve.wait_ge(b.full.sem, b.filled(c, f"leaf{p - 1}"))
            elif later(c):
                dve.wait_ge(tri_done.sem, tri_done.at(c, 1, 1))
            dve.tensor_tensor(kq_leaf[:, :, :], kq[:, s, :, :], both(eleaf[:, s, :]), ALU.mult)
            dve.tensor_tensor(km[:, :], kq[:, s, 0, :], dleaf[:, s, :], ALU.mult).then_inc(leaf_ready.sem, 1)

        def cross_products(c, p):
            s = p % 2
            both = lambda t: t.unsqueeze(1).broadcast_to([P, 2, TOK])
            if p:
                b = bank_of[f"cross{p - 1}"]
                dve.wait_ge(b.full.sem, b.filled(c, f"cross{p - 1}"))
            elif later(c):
                dve.wait_ge(a_stored.sem, a_stored.at(c, 16, 1))
            dve.tensor_tensor(kq_pair[:, :, :], kq[:, s, :, :], both(dpair[:, s, :]), ALU.mult)
            dve.tensor_tensor(kq_blk[:, :, :], kq[:, s, :, :], both(dblk[:, s, :]), ALU.mult).then_inc(
                cross_ready.sem, 1)
            if p == 0 and later(c):
                dve.wait_ge(by.full.sem, by.filled(c, f"y{TILES - 1}", 1))
            g3 = mem[:, p, :, :].rearrange("p b t -> p (b t)")
            dve.tensor_tensor(kq_start[:, p, :, :], kq[:, s, :, :], both(g3), ALU.mult)
            if p == 0 and later(c):
                for j in range(2):
                    dve.wait_ge(bd[j].drained.sem, bd[j].emptied(c, f"d{TILES - 1}", 1))
            dve.tensor_copy(gam[:, p, :], mem[:, p, :, CH - 1])
            if p:
                b = bank_of[f"kend{p - 1}"]
                dve.wait_ge(b.full.sem, b.filled(c, f"kend{p - 1}"))
            dve.tensor_tensor(kend[:, :], kq[:, s, 0, :], dend[:, s, :], ALU.mult).then_inc(kend_ready.sem, 1)

        def mask_leaves(c, p):
            b = bank_of[f"leaf{p}"]
            dve.wait_ge(b.full.sem, b.filled(c, f"leaf{p}"))
            if p == 0 and later(c):
                dve.wait_ge(b_stored.sem, b_stored.at(c, 16 * NG, 1))
            dve.tensor_tensor(ab[:, p, :, :, :], b.t[:, :].rearrange("p (m u i) -> p m u i", m=2, u=8),
                              leafmask[:, :, :].unsqueeze(2).broadcast_to([P, 2, 8, CH]),
                              ALU.mult).then_inc(b.drained.sem, 1)

        def mask_cross(c, p):
            b = bank_of[f"leaf{p}"]
            dve.wait_ge(b.drained.sem, b.emptied(c, f"leaf{p}"))
            b = bank_of[f"cross{p}"]
            dve.wait_ge(b.full.sem, b.filled(c, f"cross{p}"))
            abp = ab[:, p, :, :, :].rearrange("p m u i -> p (m u) i")
            for n in range(2):
                o = abp[:, :, BLK * n + LEAF:BLK * n + BLK]
                dve.scalar_tensor_tensor(
                    out=o, in0=b.t[:, 0:256].rearrange("p (x n i) -> p x n i", n=2, i=LEAF)[:, :, n, :],
                    scalar=rowmask[:, n:n + 1], in1=o, op0=ALU.mult, op1=ALU.add).then_inc(cross_step.sem, 1)
            dve.wait_ge(cross_step.sem, cross_step.at(c, 2 * p + 2))
            dve.scalar_tensor_tensor(
                out=abp[:, :, BLK:CH], in0=b.t[:, 256:512].rearrange("p (x i) -> p x i", i=BLK),
                scalar=rowmask[:, 2:3], in1=abp[:, :, BLK:CH], op0=ALU.mult, op1=ALU.add).then_inc(b.drained.sem, 1)

        def prepare_solve(c):
            b = bank_of[f"cross{HP - 1}"]
            dve.wait_ge(b.drained.sem, b.emptied(c, f"cross{HP - 1}"))
            a4 = ab[:, :, 0, :, :]
            dve.tensor_tensor(a4, a4, eye[:, :].unsqueeze(1).unsqueeze(1).broadcast_to([P, HP, 8, CH]),
                              ALU.add).then_inc(ab_ready.sem, 1)
            dve.wait_ge(bv.full.sem, bv.filled(c, "sst"))
            for j in range(2):
                i = dve.tensor_copy(
                    nrm[:, j, :].rearrange("p (a g h) -> p a g h", a=HP, g=NG),
                    bv.t[:, 0:64].rearrange("p (g m a h) -> p m a g h", g=NG, m=2, a=HP)[:, j, :, :, :])
            i.then_inc(bv.drained.sem, 1)
            dve.wait_ge(ab_ready.sem, ab_ready.at(c, 1))
            turned = kq_leaf[:, :, :].rearrange("p m n -> p (m n)")
            for p in range(HP):
                i = dve.transpose(turned[:, 256 * p:256 * p + 256], ab[:, p, 0, :, :].rearrange("p u i -> p (u i)"))
            i.then_inc(ca_step.sem, 1)
            dve.wait_ge(norm_step.sem, norm_step.at(c, 2))
            dve.tensor_scalar(nrm[:, :, :], sqn[:, :, :], EPS, None, ALU.add).then_inc(norm_step.sem, 1)
            dve.wait_ge(norm_step.sem, norm_step.at(c, 3))
            dve.reciprocal(inv[:, :, :], nrm[:, :, :]).then_inc(norm_step.sem, 1)
            dve.wait_ge(norm_step.sem, norm_step.at(c, 4))
            dve.tensor_tensor(sqn[:, :, :], inv[:, :, :], inv[:, :, :], ALU.mult).then_inc(norm_step.sem, 1)
            dve.wait_ge(norm_step.sem, norm_step.at(c, 5))
            dve.tensor_tensor(cvec[:, :], beta[:, :], sqn[:, 0, :], ALU.mult).then_inc(norm_step.sem, 1)
            dve.tensor_scalar(q2[:, :], sqn[:, 1, :], 1.0 / DV, None, ALU.mult).then_inc(norm_step.sem, 1)
            dve.wait_ge(ca_step.sem, ca_step.at(c, 1))
            dve.wait_ge(norm_step.sem, norm_step.at(c, 7))
            ca4 = ca.rearrange("p (g u j) -> p g u j", g=NG, u=H)
            for p in range(HP):
                i = dve.tensor_tensor(ca4[:, :, 2 * p:2 * p + 2, :],
                                      turned[:, 256 * p:256 * p + 256].rearrange("p (g h j) -> p g h j", g=NG, h=2),
                                      cvec[:, 8 * p:8 * p + 8].rearrange("p (g h) -> p g h", h=2).unsqueeze(3)
                                      .broadcast_to([P, NG, 2, CH]), ALU.mult)
            i.then_inc(ca_step.sem, 1)

        def solve(c, other):
            lead = min(len(other), 16)
            for n in range(lead):
                membrane(other[n])
                if n in (4, 10):
                    dve.sem_inc(pace.sem, 1)
            if not lead:
                dve.sem_inc(pace.sem, 2)
            rest = list(other[lead:])
            dve.wait_ge(na_loaded.sem, na_loaded.at(c, 64))
            dve.wait_ge(tu_cleared.sem, tu_cleared.at(c, 1))
            diag = lambda t: t.rearrange("p i j -> p (i j)")[:, 0:CH * CH:CH + 1]
            dve.tensor_copy(diag(tu), diag(na)).then_inc(tri_step, 1)
            for j in range(CH - 1):
                n, m = j + 1, CH - 1 - j
                prod = tmp[:, 0:n * m].rearrange("p (c i) -> p c i", i=m)
                dve.wait_ge(tri_step, 2 * j + 1)
                dve.tensor_tensor(prod, tu[:, 0:n, j:j + 1].broadcast_to([P, n, m]),
                                  na[:, j + 1:CH, j].unsqueeze(1).broadcast_to([P, n, m]),
                                  ALU.mult).then_inc(tri_step, 1)
                if rest:
                    membrane(rest.pop(0))
                dve.wait_ge(tri_step, 2 * j + 2)
                i = dve.tensor_tensor(tu[:, 0:n, j + 1:CH], tu[:, 0:n, j + 1:CH], prod, ALU.subtract)
                i.then_inc(tri_step if j < CH - 2 else tri_done.sem, 1)
                if rest:
                    membrane(rest.pop(0))
                if j % 4 == 0:
                    dve.sem_inc(pace.sem, 1)
            dve.wait_ge(tri_step, 2 * CH - 2)
            dve.sem_clear(tri_step)

        def values(c, i):
            g, q = i // 2, i % 2
            dve.wait_ge(bv.full.sem, bv.filled(c, f"v{i}"))
            if i:
                dve.wait_ge(bp.drained.sem, bp.emptied(c, f"p{i - 1}"))
            elif later(c):
                dve.wait_ge(bp.drained.sem, bp.emptied(c, f"p{TILES - 1}", 1))
            dve.tensor_tensor(nv[:, :, :].rearrange("p (a h) v -> p a h v", h=2),
                              bv.t[:, :].rearrange("p (a h v) -> p a h v", h=2, v=DV),
                              quad(nrm[:, 0, :], g, q).unsqueeze(3).broadcast_to([P, 2, 2, DV]),
                              ALU.mult).then_inc(bv.drained.sem, 1)

        def body(c, nxt):
            leaf_products(c, 0)
            cross_products(c, 0)
            for p in range(HP):
                if p + 1 < HP:
                    leaf_products(c, p + 1)
                mask_leaves(c, p)
                if p + 1 < HP:
                    cross_products(c, p + 1)
                mask_cross(c, p)
                if nxt and p == 1:
                    convolve(nxt)
            prepare_solve(c)
            if nxt:
                silus(nxt)
            solve(c, range(2 * CH) if nxt else [])
            values(c, 0)
            if nxt:
                decays(nxt, 0)
            for i in range(TILES + 1):
                g, q = i // 2, i % 2
                if i < TILES:
                    if i:
                        dve.wait_ge(bw.full.sem, bw.filled(c, f"w{i - 1}"))
                    elif later(c):
                        dve.wait_ge(bw.full.sem, bw.filled(c, f"w{TILES - 1}", 1))
                    dve.wait_ge(bv.drained.sem, bv.emptied(c, f"v{i}"))
                    dve.wait_ge(bp.full.sem, bp.filled(c, f"p{i}"))
                    dve.tensor_tensor(r[:, :, :], nv[:, :, :], bp.t[:, :].rearrange("p (h v) -> p h v", v=DV),
                                      ALU.subtract).then_inc(bp.drained.sem, 1)
                    if i + 1 < TILES:
                        values(c, i + 1)
                if i:
                    n = i - 1
                    for j in range(2):
                        dve.wait_ge(bd[j].full.sem, bd[j].filled(c, f"d{n}"))
                        for x in range(4):
                            hp, b = 2 * (n % 2) + x % 2, GB * (n // 2) + j + 2 * (x // 2)
                            k = dve.scalar_tensor_tensor(
                                out=state[:, hp, b, :], in0=state[:, hp, b, :], scalar=gam[:, hp, b:b + 1],
                                in1=bd[j].t[:, DV * x:DV * x + DV], op0=ALU.mult, op1=ALU.add)
                        k.then_inc(bd[j].drained.sem, 1)
                    dve.wait_ge(by.drained.sem, by.emptied(c, f"y{n}"))
                    dve.tensor_reduce(yss[:, 4 * (n % 2):4 * (n % 2) + 4], ysq[:, :, :], AX.X,
                                      ALU.add).then_inc(ysum_step.sem, 1)
                if i and q == 0:
                    g -= 1
                    unit = lambda t: t.rearrange("p (a g h) -> p a g h", g=NG, h=2)[:, :, g, :]
                    by2 = lambda t: t[:, :].rearrange("p (a h) -> p a h", h=2)
                    dve.wait_ge(ysum_step.sem, ysum_step.at(c, 2 * g + 2))
                    dve.tensor_tensor(by2(yss), by2(yss), unit(q2[:, :]), ALU.mult).then_inc(yss_ready.sem, 1)
                    dve.wait_ge(yrs_ready.sem, yrs_ready.at(c, g + 1))
                    dve.tensor_tensor(by2(yr), by2(yr), unit(inv[:, 1, :]), ALU.mult).then_inc(yr_ready.sem, 1)
                    dve.wait_ge(yr_ready.sem, yr_ready.at(c, g + 1))
                    dve.tensor_tensor(ysb[:, g % 2, :, :], ysb[:, g % 2, :, :],
                                      yr[:, :].unsqueeze(2).broadcast_to([P, H, DV]), ALU.mult).then_inc(yn_ready.sem, 1)
                if nxt and i + 1 < STEPS:
                    decays(nxt, i + 1)

        def first(c):
            convolve(c)
            silus(c)
            for n in range(2 * CH):
                membrane(n)
            for step in range(STEPS):
                decays(c, step)

        iterations(dve, first, body)


def feed_forward(nc, a, attn_d, out, ctx, sb, sem):
    wu1, bu1, wu2, bu2 = sb("wu1", [P, R]), sb("bu1", [R, 1]), sb("wu2", [R, D]), sb("bu2", [P, 1])
    wffn = sb("wffn", [P, 1])
    wf1, wf3, wf2 = sb("wf1", [P, FF]), sb("wf3", [P, FF]), sb("wf2", [P, FT, D])
    w1, w2 = sb("w1", [P, E, FF]), sb("w2", [P, E, FT, D])
    b1, b2 = sb("b1", [P, E, FT]), sb("b2", [E, D])
    lng, lnb = sb("lng", [P, E]), sb("lnb", [P, E])
    cent = sb("cent", [P, E])
    iota = sb("iota", [P, NG, E])
    ident = sb("ident2", [P, P])
    meanw = sb("meanw2", [P, P])
    eps_t, ln_eps_t = sb("eps2", [P, 1]), sb("ln_eps", [P, 1])

    x0, at = sb("x0", [P, TOK]), sb("at", [P, TOK])
    zu, tu, u1 = sb("zu", [R, TOK]), sb("tu1", [R, TOK]), sb("u1", [R, TOK])
    gate, sq, y1, h2, rs = (sb(n, [P, TOK]) for n in ("gate", "sq", "y1", "h2", "rs"))
    th, hid = sb("th", [P, 2, TOK]), sb("hid", [P, FT, TOK])
    x1, xl, xc, xh, xk, xf, sqf, rsf = (sb(n, [P, TOK]) for n in ("x1", "xl", "xc", "xh", "xk", "xf", "sqf", "rsf"))
    hm = sb("hm", [P, 2, FT, TOK])
    acc = sb("acc", [P, NG, D])
    aff, ea, oh, sel = (sb(n, [P, NG, E]) for n in ("aff", "ea", "oh", "sel"))
    top = sb("top", [P, NG])
    sel_t = sb("sel_t", [E, TOK])

    head_fills = ["u1", "u2", "ms"] + [f"{n}{t}" for t in range(FT) for n in ("f", "g")] + [
        "ff", "m1", "v1", "aff", "m2", "v2"]
    psum = [ctx.enter_context(nc.psum_tensor(f"pf{i}", [P, 512], F32)) for i in range(8)]

    def bank(i, name, fills):
        return Bank(psum[i], sem(f"{name}_full"), sem(f"{name}_drained"), fills)

    head_banks = [bank(i, f"head{i}", head_fills[i::2]) for i in range(2)]
    bt = bank(2, "tail", ["selt", "back", "m3", "v3"])
    bh = [bank(3 + i, f"hidden{i}", [f"h{e}_{t}" for e in range(E) for t in range(FT) if (FT * e + t) % 3 == i])
          for i in range(3)]
    bo = [bank(6 + i, f"expert{i}", [f"e{e}" for e in range(E) if e % 2 == i]) for i in range(2)]
    bank_of = {f: b for b in head_banks + [bt] + bh + bo for f in b.fills}

    sig = lambda name, per: Signal(sem(name), per)
    s_const, s_made, s_b1 = sem("ffn_const_loaded"), sem("ffn_made"), sem("b1_folded")
    in_loaded = sig("in_loaded", 32)
    tu_ready, u1_ready = sig("tanh_u_ready", 1), sig("u1_ready", 1)
    gate_ready, gated, y1_ready = sig("gate_ready", 1), sig("gated", 1), sig("y1_ready", 1)
    sq_ready, rs_ready = sig("sq_ready", 3), sig("rs_ready", 3)
    sqf_ready, rsf_ready, xf_step, xfc_ready = (sig(n, 1) for n in ("sqf_ready", "rsf_ready", "xf_step", "xfc_ready"))
    h2_ready, th_ready, hid_ready = sig("h2_ready", 1), sig("th_ready", FT), sig("hid_ready", 2 * FT)
    x1_ready, xc_ready, xk_ready = sig("x1_ready", 2), sig("xc_ready", 2), sig("xk_ready", 1)
    normed = sig("normed", 2)
    route, sel_ready = sig("route_step", 9), sig("sel_ready", 1)
    acc_step = sig("acc_step", E)
    xf_ready, stored = sig("xf_ready", 1), Signal(sem("out_stored"), 16, 16)
    passed_pe, passed_pool = sem("ffn_passed_pe"), sem("ffn_passed_pool")

    col = lambda x: x.unsqueeze(1)
    loads = [(wu1[:, :], a["w_u1"]), (bu1[:, :], col(a["b_u1"])), (wu2[:, :], a["w_u2"]), (bu2[:, :], col(a["b_u2"])),
             (wffn[:, :], col(a["w_ffn"])), (wf1[:, :], a["w_ff1"]), (wf3[:, :], a["w_ff3"]),
             (wf2[:, :, :], a["w_ff2"]), (w1[:, :, :], a["w1"]), (w2[:, :, :, :], a["w2"]), (b1[:, :, :], a["b1"]),
             (b2[:, :], a["b2"]), (lng[:, :], a["ln_g"]), (lnb[:, :], a["ln_b"]), (cent[:, :], a["centroids"]),
             (iota[:, :, :], a["iota"]), (ident[:, :], a["ident"])]
    n_const = 16 * len(loads)
    n_made = 6

    block = ctx.enter_context(nc.Block())

    def iterations(eng, head, body, tail):
        head(Chunk(0))
        body(Chunk(0), Chunk(0, 1), None)
        with eng.Fori(1, NC - 1) as c:
            body(Chunk(c), Chunk(c, 1), Chunk(c, -1))
        body(Chunk(0, NC - 1), None, Chunk(0, NC - 2))
        tail(Chunk(0, NC - 1))

    @block.sync
    def _(sp):
        for dst, src in loads:
            sp.dma_start(dst, src).then_inc(s_const, 16)

        def fetch(c):
            if later(c):
                sp.wait_ge(x1_ready.sem, x1_ready.at(c, 2, 1))
            sp.dma_start(x0[:, :], a["xT"][c.plus:][c.loop]).then_inc(in_loaded.sem, 16)
            sp.dma_start(at[:, :], attn_d[c.plus:][c.loop]).then_inc(in_loaded.sem, 16)

        def store(c):
            sp.wait_ge(xf_ready.sem, xf_ready.at(c, 1))
            if looped(c):
                sp.dma_start(out[c.loop + c.plus], xf[:, :]).then_inc(stored.sem, 16)
            else:
                sp.dma_start(out[c.plus], xf[:, :]).then_inc(stored.sem, 16)

        def body(c, nxt, last):
            if nxt:
                fetch(nxt)
            if last:
                store(last)

        iterations(sp, fetch, body, store)
        sp.wait_ge(stored.sem, stored.at(Chunk(0, NC - 1), 16))

    @block.gpsimd
    def _(pool):
        for b in head_banks + [bt] + bh + bo:
            pool.sem_inc(b.drained.sem, 1)
        pool.sem_inc(stored.sem, 16)
        pool.memset(meanw[:, :], 1.0 / D).then_inc(s_made, 1)
        pool.memset(eps_t[:, :], EPS).then_inc(s_made, 1)
        pool.memset(ln_eps_t[:, :], LN_EPS).then_inc(s_made, 1)

        def settle(c):
            if looped(c):
                pool.sem_inc(passed_pool, 1)

        def keep(c, last):
            pool.wait_ge(normed.sem, normed.at(c, 1))
            if last:
                pool.wait_ge(bt.drained.sem, bt.emptied(last, "back"))
            settle(c)
            pool.tensor_copy(xk[:, :], xl[:, :]).then_inc(xk_ready.sem, 1)

        iterations(pool, lambda c: None, lambda c, nxt, last: keep(c, last), lambda c: None)

    @block.scalar
    def _(act):
        act.wait_ge(s_const, n_const)
        act.wait_ge(s_made, n_made)

        def rsqrt(c, fill, eps, rs, rs_ready):
            b = bank_of[fill]
            act.wait_ge(b.full.sem, b.filled(c, fill))
            act.activation(rs[:, :], b.t[:, :], ACT.Ln, bias=eps[:, 0:1]).then_inc(b.drained.sem, 1)
            act.wait_ge(b.drained.sem, b.emptied(c, fill))
            act.activation(rs[:, :], rs[:, :], ACT.Exp, scale=-0.5).then_inc(rs_ready.sem, 1)

        def head(c, s):
            if s == 1:
                b = bank_of["u1"]
                act.wait_ge(b.drained.sem, b.emptied(c, "u1"))
                act.activation(tu[:, :], zu[:, :], ACT.Tanh).then_inc(tu_ready.sem, 1)
            if s == 2:
                b = bank_of["u2"]
                act.wait_ge(b.full.sem, b.filled(c, "u2"))
                act.activation(gate[:, :], b.t[:, :], ACT.Tanh, bias=bu2[:, 0:1], scale=0.5).then_inc(b.drained.sem, 1)
                load_exp_log_table(nc, act)
            if s == 3:
                act.wait_ge(y1_ready.sem, y1_ready.at(c, 1))
                act.activation(sq[:, :], y1[:, :], ACT.Square).then_inc(sq_ready.sem, 1)
            if s == 4:
                rsqrt(c, "ms", eps_t, rs, rs_ready)
            if 5 <= s < 5 + FT:
                t = s - 5
                if t >= 2:
                    act.wait_ge(hid_ready.sem, hid_ready.at(c, 2 * (t - 2) + 1))
                b = bank_of[f"f{t}"]
                act.wait_ge(b.full.sem, b.filled(c, f"f{t}"))
                act.activation(th[:, t % 2, :], b.t[:, :], ACT.Tanh, scale=0.5).then_inc(th_ready.sem, 1)
                if t == FT - 1:
                    load_exp_log_table(nc, act)
            if s == 10:
                act.wait_ge(xc_ready.sem, xc_ready.at(c, 1))
                act.activation(sq[:, :], x1[:, :], ACT.Square).then_inc(sq_ready.sem, 1)
            if s == 11:
                rsqrt(c, "v1", ln_eps_t, rs, rs_ready)
            if s == 12:
                act.wait_ge(xc_ready.sem, xc_ready.at(c, 2))
                act.activation(sq[:, :], xc[:, :], ACT.Square).then_inc(sq_ready.sem, 1)
                act.wait_ge(route.sem, route.at(c, 1))
                act.activation(ea[:, :, :], aff[:, :, :], ACT.Exp, scale=-1.0).then_inc(route.sem, 1)
            if s == 13:
                rsqrt(c, "v2", ln_eps_t, rs, rs_ready)

        def tail(c, s):
            if s == 1:
                act.wait_ge(xfc_ready.sem, xfc_ready.at(c, 1))
                act.activation(sqf[:, :], xf[:, :], ACT.Square).then_inc(sqf_ready.sem, 1)
            if s == 3:
                rsqrt(c, "v3", ln_eps_t, rsf, rsf_ready)

        def turned(c):
            b = bank_of["selt"]
            act.wait_ge(b.full.sem, b.filled(c, "selt"))
            act.activation(sel_t[:, :], b.t[0:E, :], ACT.Copy).then_inc(b.drained.sem, 1)

        def hidden(c, e):
            for t in range(0, FT, 2):
                fill = f"h{e}_{t}"
                b = bank_of[fill]
                act.wait_ge(b.full.sem, b.filled(c, fill))
                if e >= 2:
                    act.wait_ge(bo[e % 2].full.sem, bo[e % 2].filled(c, f"e{e - 2}"))
                elif later(c):
                    act.wait_ge(bo[e % 2].full.sem, bo[e % 2].filled(c, f"e{E - 2 + e}", 1))
                act.activation(hm[:, e % 2, t, :], b.t[:, :], ACT.Relu, bias=b1[:, e, t:t + 1]).then_inc(b.drained.sem, 1)

        def body(c, nxt, last):
            hidden(c, 0)
            for e in range(E):
                if e + 1 < E:
                    hidden(c, e + 1)
                for s in (2 * e, 2 * e + 1):
                    if last:
                        tail(last, s)
                    if nxt:
                        head(nxt, s)
                if e == 1:
                    turned(c)

        def alone(part):
            def run(c):
                for s in range(2 * E):
                    part(c, s)
            return run

        iterations(act, alone(head), body, alone(tail))

    @block.tensor
    def _(pe):
        pe.wait_ge(s_const, n_const)
        pe.wait_ge(s_made, 3)
        m = None
        for e in range(E):
            for t in range(FT):
                m = pe.matmul(bh[0].t[:, FT * e + t:FT * e + t + 1], w1[:, e, P * t:P * t + P], lnb[:, e:e + 1],
                              start=True, stop=True)
        m.then_inc(s_b1, 1)
        pe.wait_ge(s_made, n_made)

        def settle(c):
            if looped(c):
                pe.sem_inc(passed_pe, 1)

        def mean(c, fill, src, ready, n):
            b = bank_of[fill]
            pe.wait_ge(ready.sem, ready.at(c, n))
            pe.wait_ge(b.drained.sem, b.freed(c, fill))
            settle(c)
            pe.matmul(b.t[:, :], meanw[:, :], src[:, :], start=True, stop=True).then_inc(b.full.sem, 1)

        def head(c, s):
            if s == 1:
                b = bank_of["u1"]
                pe.wait_ge(in_loaded.sem, in_loaded.at(c, 32))
                pe.wait_ge(b.drained.sem, b.freed(c, "u1"))
                settle(c)
                pe.matmul(b.t[0:R, :], wu1[:, :], x0[:, :], start=True, stop=True).then_inc(b.full.sem, 1)
            if s == 2:
                b = bank_of["u2"]
                pe.wait_ge(u1_ready.sem, u1_ready.at(c, 1))
                pe.wait_ge(b.drained.sem, b.freed(c, "u2"))
                settle(c)
                pe.matmul(b.t[:, :], wu2[:, :], u1[:, :], start=True, stop=True).then_inc(b.full.sem, 1)
            if s == 4:
                mean(c, "ms", sq, sq_ready, 1)
            if s == 5:
                pe.wait_ge(h2_ready.sem, h2_ready.at(c, 1))
            if 5 <= s < 5 + FT:
                t = s - 5
                for name, wt in (("f", wf1), ("g", wf3)):
                    b = bank_of[f"{name}{t}"]
                    pe.wait_ge(b.drained.sem, b.freed(c, f"{name}{t}"))
                    settle(c)
                    pe.matmul(b.t[:, :], wt[:, P * t:P * t + P], h2[:, :], start=True, stop=True).then_inc(b.full.sem, 1)
            if s == 9:
                b = bank_of["ff"]
                pe.wait_ge(b.drained.sem, b.freed(c, "ff"))
                for t in range(FT):
                    pe.wait_ge(hid_ready.sem, hid_ready.at(c, 2 * t + 2))
                    settle(c)
                    m = pe.matmul(b.t[:, :], wf2[:, t, :], hid[:, t, :], start=(t == 0), stop=(t == FT - 1))
                m.then_inc(b.full.sem, 1)
            if s == 10:
                mean(c, "m1", x1, x1_ready, 2)
            if s == 11:
                mean(c, "v1", sq, sq_ready, 2)
            if s == 12:
                b = bank_of["aff"]
                pe.wait_ge(normed.sem, normed.at(c, 1))
                pe.wait_ge(b.drained.sem, b.freed(c, "aff"))
                settle(c)
                for g in range(NG):
                    m = pe.matmul(b.t[:, E * g:E * g + E], xl[:, P * g:P * g + P], cent[:, :], start=True, stop=True)
                m.then_inc(b.full.sem, 1)
                mean(c, "m2", xl, normed, 1)
            if s == 13:
                mean(c, "v2", sq, sq_ready, 3)

        def tail(c, s):
            if s == 0:
                b = bank_of["back"]
                pe.wait_ge(b.drained.sem, b.emptied(c, "selt"))
                pe.wait_ge(acc_step.sem, acc_step.at(c, E))
                settle(c)
                pe.matmul(b.t[:, :], b2[:, :], sel_t[:, :], start=True, stop=False)
                for g in range(NG):
                    m = pe.matmul(b.t[:, P * g:P * g + P], acc[:, g, :], ident[:, :], start=False, stop=(g == NG - 1))
                m.then_inc(b.full.sem, 1)
            if s == 1:
                mean(c, "m3", xf, xf_step, 1)
            if s == 3:
                mean(c, "v3", sqf, sqf_ready, 1)

        def turn(c):
            b = bank_of["selt"]
            pe.wait_ge(b.drained.sem, b.freed(c, "selt"))
            pe.wait_ge(sel_ready.sem, sel_ready.at(c, 1))
            settle(c)
            for g in range(NG):
                m = pe.transpose(b.t[0:E, P * g:P * g + P], sel[:, g, :], ident[:, :])
            m.then_inc(b.full.sem, 1)

        def up(c, e, t):
            b = bank_of[f"h{e}_{t}"]
            pe.wait_ge(b.drained.sem, b.freed(c, f"h{e}_{t}"))
            settle(c)
            pe.matmul(b.t[:, :], w1[:, e, P * t:P * t + P], xh[:, :], start=True, stop=True).then_inc(b.full.sem, 1)

        def body(c, nxt, last):
            pe.wait_ge(normed.sem, normed.at(c, 2))
            for t in range(FT):
                up(c, 0, t)
            for e in range(E):
                if e + 1 < E:
                    for t in range(FT):
                        up(c, e + 1, t)
                if last:
                    tail(last, 2 * e)
                if nxt:
                    head(nxt, 2 * e)
                b = bank_of[f"e{e}"]
                for t in range(FT):
                    hb = bank_of[f"h{e}_{t}"]
                    pe.wait_ge(hb.drained.sem, hb.emptied(c, f"h{e}_{t}"))
                pe.wait_ge(b.drained.sem, b.freed(c, f"e{e}"))
                settle(c)
                for g in range(NG):
                    for t in range(FT):
                        m = pe.matmul(b.t[:, D * g:D * g + D], hm[:, e % 2, t, P * g:P * g + P], w2[:, e, t, :],
                                      start=(t == 0), stop=(t == FT - 1))
                m.then_inc(b.full.sem, 1)
                if last:
                    tail(last, 2 * e + 1)
                if nxt:
                    head(nxt, 2 * e + 1)
                if e == 1:
                    turn(c)

        def alone(part):
            def run(c):
                for s in range(2 * E):
                    part(c, s)
            return run

        iterations(pe, alone(head), body, alone(tail))

    @block.vector
    def _(dve):
        dve.wait_ge(s_const, n_const)
        dve.wait_ge(s_made, 3)
        dve.tensor_scalar(bu1[:, :], bu1[:, :], 0.5, None, ALU.mult)
        dve.tensor_scalar(bu2[:, :], bu2[:, :], 0.5, None, ALU.mult).then_inc(s_made, 1)
        dve.wait_ge(s_b1, 1)
        dve.tensor_tensor(b1[:, :, :].rearrange("p e t -> p (e t)"), b1[:, :, :].rearrange("p e t -> p (e t)"),
                          bh[0].t[:, 0:E * FT], ALU.add).then_inc(s_made, 1)
        for e in range(E):
            i = dve.tensor_scalar(w1[:, e, :], w1[:, e, :], lng[:, e:e + 1], None, ALU.mult)
        i.then_inc(s_made, 1)
        dve.wait_ge(s_made, n_made)

        def center(c, fill, src, dst, ready):
            b = bank_of[fill]
            dve.wait_ge(b.full.sem, b.filled(c, fill))
            dve.tensor_tensor(dst[:, :], src[:, :], b.t[:, :], ALU.subtract).then_inc(b.drained.sem, 1)
            dve.wait_ge(b.drained.sem, b.emptied(c, fill))
            dve.sem_inc(ready.sem, 1)

        wide = lambda t: t[:, :].unsqueeze(2).broadcast_to([P, NG, E])

        def head(c, s):
            if s == 1:
                b = bank_of["u1"]
                dve.wait_ge(b.full.sem, b.filled(c, "u1"))
                dve.tensor_scalar(zu[:, :], b.t[0:R, :], 0.5, bu1[:, 0:1], ALU.mult, ALU.add).then_inc(b.drained.sem, 1)
                dve.wait_ge(tu_ready.sem, tu_ready.at(c, 1))
                dve.scalar_tensor_tensor(out=u1[:, :], in0=tu[:, :], scalar=1.0, in1=zu[:, :], op0=ALU.add,
                                         op1=ALU.mult).then_inc(u1_ready.sem, 1)
            if s == 2:
                dve.wait_ge(in_loaded.sem, in_loaded.at(c, 32))
                b = bank_of["u2"]
                dve.wait_ge(b.drained.sem, b.emptied(c, "u2"))
                dve.scalar_tensor_tensor(out=gate[:, :], in0=gate[:, :], scalar=1.0, in1=at[:, :], op0=ALU.add,
                                         op1=ALU.mult).then_inc(gated.sem, 1)
                dve.wait_ge(gated.sem, gated.at(c, 1))
                dve.scalar_tensor_tensor(out=y1[:, :], in0=gate[:, :], scalar=0.5, in1=x0[:, :], op0=ALU.mult,
                                         op1=ALU.add).then_inc(y1_ready.sem, 1)
            if s == 4:
                dve.wait_ge(rs_ready.sem, rs_ready.at(c, 1))
                dve.scalar_tensor_tensor(out=h2[:, :], in0=y1[:, :], scalar=wffn[:, 0:1], in1=rs[:, :], op0=ALU.mult,
                                         op1=ALU.mult).then_inc(h2_ready.sem, 1)
            if 5 <= s < 5 + FT:
                t = s - 5
                b = bank_of[f"f{t}"]
                dve.wait_ge(th_ready.sem, th_ready.at(c, t + 1))
                dve.scalar_tensor_tensor(out=hid[:, t, :], in0=th[:, t % 2, :], scalar=1.0, in1=b.t[:, :],
                                         op0=ALU.add, op1=ALU.mult).then_inc(b.drained.sem, 1)
                dve.wait_ge(b.drained.sem, b.emptied(c, f"f{t}"))
                dve.sem_inc(hid_ready.sem, 1)
                b = bank_of[f"g{t}"]
                dve.wait_ge(b.full.sem, b.filled(c, f"g{t}"))
                dve.tensor_tensor(hid[:, t, :], hid[:, t, :], b.t[:, :], ALU.mult).then_inc(b.drained.sem, 1)
                dve.wait_ge(b.drained.sem, b.emptied(c, f"g{t}"))
                dve.sem_inc(hid_ready.sem, 1)
            if s == 9:
                b = bank_of["ff"]
                dve.wait_ge(b.full.sem, b.filled(c, "ff"))
                dve.scalar_tensor_tensor(out=x1[:, :], in0=b.t[:, :], scalar=0.5, in1=y1[:, :], op0=ALU.mult,
                                         op1=ALU.add).then_inc(b.drained.sem, 1)
                dve.wait_ge(b.drained.sem, b.emptied(c, "ff"))
                dve.sem_inc(x1_ready.sem, 1)
                dve.tensor_tensor(x1[:, :], x1[:, :], x0[:, :], ALU.add).then_inc(x1_ready.sem, 1)
                dve.wait_ge(x1_ready.sem, x1_ready.at(c, 2))
            if s == 10:
                center(c, "m1", x1, x1, xc_ready)
            if s == 11:
                dve.wait_ge(rs_ready.sem, rs_ready.at(c, 2))
                if later(c):
                    dve.wait_ge(xk_ready.sem, xk_ready.at(c, 1, 1))
                dve.tensor_tensor(xl[:, :], x1[:, :], rs[:, :], ALU.mult).then_inc(normed.sem, 1)
            if s == 12:
                b = bank_of["aff"]
                dve.wait_ge(b.full.sem, b.filled(c, "aff"))
                dve.tensor_copy(aff[:, :, :].rearrange("p g e -> p (g e)"), b.t[:, 0:NG * E]).then_inc(b.drained.sem, 1)
                dve.wait_ge(b.drained.sem, b.emptied(c, "aff"))
                dve.sem_inc(route.sem, 1)
                dve.wait_ge(normed.sem, normed.at(c, 1))
                center(c, "m2", xl, xc, xc_ready)
                dve.wait_ge(route.sem, route.at(c, 2))
                dve.tensor_reduce(top[:, :], aff[:, :, :], AX.X, ALU.max).then_inc(route.sem, 1)
                dve.wait_ge(route.sem, route.at(c, 3))
                dve.tensor_tensor(oh[:, :, :], aff[:, :, :], wide(top), ALU.is_lt).then_inc(route.sem, 1)
                dve.wait_ge(route.sem, route.at(c, 4))
                dve.scalar_tensor_tensor(out=oh[:, :, :], in0=oh[:, :, :], scalar=float(2 * E), in1=iota[:, :, :],
                                         op0=ALU.mult, op1=ALU.add).then_inc(route.sem, 1)
                dve.wait_ge(route.sem, route.at(c, 5))
                dve.tensor_reduce(top[:, :], oh[:, :, :], AX.X, ALU.min).then_inc(route.sem, 1)
                dve.wait_ge(route.sem, route.at(c, 6))
                dve.tensor_tensor(oh[:, :, :], iota[:, :, :], wide(top), ALU.is_equal).then_inc(route.sem, 1)
                dve.tensor_scalar(ea[:, :, :], ea[:, :, :], 1.0, None, ALU.add).then_inc(route.sem, 1)
                dve.wait_ge(route.sem, route.at(c, 8))
                dve.reciprocal(ea[:, :, :], ea[:, :, :]).then_inc(route.sem, 1)
                dve.wait_ge(route.sem, route.at(c, 9))
            if s == 13:
                dve.wait_ge(rs_ready.sem, rs_ready.at(c, 3))
                if later(c):
                    b = bank_of[f"h{E - 1}_{FT - 1}"]
                    dve.wait_ge(b.full.sem, b.filled(c, f"h{E - 1}_{FT - 1}", 1))
                dve.tensor_tensor(xh[:, :], xc[:, :], rs[:, :], ALU.mult).then_inc(normed.sem, 1)

        def choose(c):
            if later(c):
                dve.wait_ge(acc_step.sem, acc_step.at(c, E, 1))
                b = bank_of["selt"]
                dve.wait_ge(b.full.sem, b.filled(c, "selt", 1))
            dve.tensor_tensor(sel[:, :, :], oh[:, :, :], ea[:, :, :], ALU.mult).then_inc(sel_ready.sem, 1)

        def tail(c, s):
            if s == 0:
                b = bank_of["back"]
                dve.wait_ge(b.full.sem, b.filled(c, "back"))
                dve.wait_ge(stored.sem, stored.at(c, 0))
                dve.wait_ge(xk_ready.sem, xk_ready.at(c, 1))
                dve.scalar_tensor_tensor(out=xf[:, :], in0=xk[:, :], scalar=2.0, in1=b.t[:, :], op0=ALU.mult,
                                         op1=ALU.add).then_inc(b.drained.sem, 1)
                dve.wait_ge(b.drained.sem, b.emptied(c, "back"))
                dve.sem_inc(xf_step.sem, 1)
            if s == 1:
                center(c, "m3", xf, xf, xfc_ready)
            if s == 3:
                dve.wait_ge(rsf_ready.sem, rsf_ready.at(c, 1))
                dve.tensor_tensor(xf[:, :], xf[:, :], rsf[:, :], ALU.mult).then_inc(xf_ready.sem, 1)

        def gather(c, e, last):
            b = bank_of[f"e{e}"]
            dve.wait_ge(b.full.sem, b.filled(c, f"e{e}"))
            if e:
                dve.wait_ge(acc_step.sem, acc_step.at(c, e))
            elif last:
                dve.wait_ge(bt.full.sem, bt.filled(last, "back"))
            for g in range(NG):
                if e:
                    i = dve.scalar_tensor_tensor(out=acc[:, g, :], in0=b.t[:, D * g:D * g + D],
                                                 scalar=sel[:, g, e:e + 1], in1=acc[:, g, :],
                                                 op0=ALU.mult, op1=ALU.add)
                else:
                    i = dve.tensor_scalar(acc[:, g, :], b.t[:, D * g:D * g + D], sel[:, g, e:e + 1], None,
                                          ALU.mult)
            i.then_inc(b.drained.sem, 1)
            dve.wait_ge(b.drained.sem, b.emptied(c, f"e{e}"))
            dve.sem_inc(acc_step.sem, 1)

        def hidden(c, e):
            for t in range(1, FT, 2):
                fill = f"h{e}_{t}"
                b = bank_of[fill]
                dve.wait_ge(b.full.sem, b.filled(c, fill))
                if e >= 2:
                    dve.wait_ge(bo[e % 2].full.sem, bo[e % 2].filled(c, f"e{e - 2}"))
                elif later(c):
                    dve.wait_ge(bo[e % 2].full.sem, bo[e % 2].filled(c, f"e{E - 2 + e}", 1))
                dve.tensor_scalar(hm[:, e % 2, t, :], b.t[:, :], b1[:, e, t:t + 1], 0.0, ALU.add,
                                  ALU.max).then_inc(b.drained.sem, 1)

        def body(c, nxt, last):
            choose(c)
            dve.wait_ge(sel_ready.sem, sel_ready.at(c, 1))
            hidden(c, 0)
            for e in range(E):
                if e + 1 < E:
                    hidden(c, e + 1)
                if last:
                    tail(last, 2 * e)
                if e:
                    gather(c, e - 1, last)
                if nxt:
                    head(nxt, 2 * e)
                if last:
                    tail(last, 2 * e + 1)
                if nxt:
                    head(nxt, 2 * e + 1)
            gather(c, E - 1, last)

        def alone(part):
            def run(c):
                for s in range(2 * E):
                    part(c, s)
            return run

        iterations(dve, alone(head), body, alone(tail))


def _layouts(i):
    import numpy as np
    n = {k[3:]: np.asarray(v) for k, v in i.items()}
    g = {k.split("_", 1)[1]: v for k, v in n.items()}
    con = np.ascontiguousarray
    pairs = lambda x: con(x.reshape(HP, P).T)
    t = {
        "xT": con(g["x"].reshape(NB, NC, CH, D).transpose(1, 3, 0, 2).reshape(NC, D, TOK)),
        "alpha_spike": pairs(g["alpha_spike"]), "beta_spike": pairs(g["beta_spike"]),
        "w_hn": con(g["w_hn"].T), "w_out": con(g["w_out"].reshape(H, DV, D).transpose(1, 0, 2)),
        "w_ff2": con(g["w_ff2"].reshape(FT, P, D).transpose(1, 0, 2)),
        "w1": con(g["w1"].transpose(2, 0, 1)),
        "w2": con(g["w2"].reshape(E, D, FT, P).transpose(3, 0, 2, 1)),
        "b1": con(g["b1"].reshape(E, FT, P).transpose(2, 0, 1)), "b2": g["b2"],
        "ln_g": con(g["ln_g"].T), "ln_b": con(g["ln_b"].T), "centroids": con(g["centroids"].T),
    }
    for k in ("w_norm_in", "conv_w", "conv_b", "wq", "wk", "wv", "w_spike", "w_au", "b_au", "w_ad", "b_ad", "w_beta",
              "b_beta", "w_u1", "b_u1", "w_u2", "b_u2", "w_ffn", "w_ff1", "w_ff3"):
        t[k] = con(g[k])
    j, i_ = np.arange(P) % CH, np.arange(CH)
    leaf = (j[:, None] // LEAF) == (i_[None] // LEAF)
    t["leafmask"] = np.stack([leaf & (j[:, None] < i_), leaf & (j[:, None] <= i_)], 1).astype(np.float32)
    t["rowmask"] = np.stack([j // LEAF == 0, j // LEAF == 2, j < BLK], 1).astype(np.float32)
    t["eye"] = (j[:, None] == i_).astype(np.float32)
    t["ident"] = np.eye(P, dtype=np.float32)
    head = np.arange(P) // DK
    t["sumblk"] = (head[:, None] == head).astype(np.float32)
    ind = np.zeros((P, 2, HP, 16), np.float32)
    for m in range(2):
        for p in range(HP):
            ind[np.arange(P), m, p, 8 * m + 2 * p + head] = 1.0
    t["headind"] = ind
    t["iota"] = np.broadcast_to(np.arange(E, dtype=np.float32), (P, NG, E)).copy()
    return t


def kernel(**inputs):
    import numpy as np
    import concourse.bacc as bacc
    from concourse.bass_utils import run_bass_kernel_spmd as run

    nc = bacc.Bacc("TRN2", target_bir_lowering=False, num_devices=1)
    arrays = _layouts(inputs)
    args = {k: nc.dram_tensor(f"in_{k}", v.shape, mybir.dt.from_np(v.dtype), kind="ExternalInput").ap()
            for k, v in arrays.items()}
    out = nc.dram_tensor("out", (NC, P, TOK), F32, kind="ExternalOutput").ap()
    build(nc, args, out)
    r = run(nc, [{f"in_{k}": v for k, v in arrays.items()}], core_ids=[0])
    got = r.results[0]["out"]
    return np.ascontiguousarray(got.reshape(NC, D, NB, CH).transpose(2, 0, 3, 1).reshape(NB, NT, D))
```
